# Optimizing a Trainium2 kernel written in Bass

```python
import numpy as np
import jax
import jax.numpy as jnp

def _softmax(x, axis=-1):
    return jax.nn.softmax(x, axis=axis)

def _gelu(x):
    return jax.nn.gelu(x, approximate=True)

def _silu(x):
    return jax.nn.silu(x)

def _sigmoid(x):
    return jax.nn.sigmoid(x)

def _layernorm(x, axis=-1, eps=1e-05):
    m = jnp.mean(x, axis=axis, keepdims=True)
    v = jnp.var(x, axis=axis, keepdims=True)
    return (x - m) / jnp.sqrt(v + eps)

def _scatter_add(tgt, idx, src, axis=0):
    return tgt.at[idx].add(src)

def _segment_sum(src, seg, n):
    return jax.ops.segment_sum(src, seg, n)
kernel_name = 'mk_lm_tower_d2_tok_ids1024_r4_1f61da'

def setup_inputs(seed: int=0):
    np.random.seed(seed)
    _w = jnp.asarray

    def _rec_inputs():
        import jax
        import jax.numpy as jnp
        _rk = jax.random.key(seed)
        x = jax.random.randint(jax.random.fold_in(_rk, 1), (8, 256), 0, 49991, jnp.int32)
        return x
    x = _rec_inputs()

    def _L0_tok_setup():
        import jax, jax.numpy as jnp
        import numpy as np
        HIDDEN = 256
        CUTOFFS = [5000, 20000, 50000]
        PROJECT_FACTOR = 4
        NUM_TAILS = len(CUTOFFS) - 1
        CUTOFF_ENDS = [0] + CUTOFFS
        BATCH, SEQ = (8, 256)

        def _glorot(key, shape):
            fan_in, fan_out = shape
            limit = np.sqrt(6.0 / (fan_in + fan_out)).astype(np.float32)
            return jax.random.uniform(key, shape, jnp.float32, -limit, limit)
        key = jax.random.key(seed)
        ks = jax.random.split(key, 7)
        return {'x': jax.random.randint(ks[0], (BATCH, SEQ), 0, CUTOFFS[-1], dtype=jnp.int64.dtype if jax.config.jax_enable_x64 else jnp.int32), 'head_weight_proj': _glorot(ks[1], (HIDDEN, HIDDEN)), 'head_weight': _glorot(ks[2], (HIDDEN, CUTOFFS[0] + NUM_TAILS)), 'tail_weight_proj_0': _glorot(ks[3], (HIDDEN, HIDDEN // PROJECT_FACTOR)), 'tail_weight_0': _glorot(ks[4], (HIDDEN // PROJECT_FACTOR, CUTOFFS[1] - CUTOFFS[0])), 'tail_weight_proj_1': _glorot(ks[5], (HIDDEN, HIDDEN // PROJECT_FACTOR ** 2)), 'tail_weight_1': _glorot(ks[6], (HIDDEN // PROJECT_FACTOR ** 2, CUTOFFS[2] - CUTOFFS[1]))}
    _L0_tok_all = _L0_tok_setup()
    _L0_tok_in = {k: v for k, v in _L0_tok_all.items() if k in ('head_weight_proj', 'head_weight', 'tail_weight_proj_0', 'tail_weight_0', 'tail_weight_proj_1', 'tail_weight_1')}
    del _L0_tok_all

    def _L0_attn_setup():
        import jax, jax.numpy as jnp
        import numpy as np
        NUM_BLOCKS = 4
        B, S, D = (4, 1024, 256)
        A, FF = (256, 1024)
        LN_EPS = 1e-06

        def _ln(x, s, b):
            m = jnp.mean(x, axis=-1, keepdims=True)
            v = jnp.mean(jnp.square(x - m), axis=-1, keepdims=True)
            return (x - m) * jax.lax.rsqrt(v + LN_EPS) * s + b
        key = jax.random.key(seed)
        ks = jax.random.split(key, 8)
        w = lambda k, shape: jax.random.normal(k, shape, dtype=jnp.float32) * 0.02
        return {'x': jax.random.normal(ks[0], (B, S, D), dtype=jnp.float32), 'Wq': w(ks[1], (NUM_BLOCKS, D, A)), 'bq': jnp.zeros((NUM_BLOCKS, A), jnp.float32), 'Wk': w(ks[2], (NUM_BLOCKS, D, A)), 'bk': jnp.zeros((NUM_BLOCKS, A), jnp.float32), 'Wv': w(ks[3], (NUM_BLOCKS, D, A)), 'bv': jnp.zeros((NUM_BLOCKS, A), jnp.float32), 'Wo': w(ks[4], (NUM_BLOCKS, A, D)), 'bo': jnp.zeros((NUM_BLOCKS, D), jnp.float32), 'ln1_s': jnp.ones((NUM_BLOCKS, D), jnp.float32), 'ln1_b': jnp.zeros((NUM_BLOCKS, D), jnp.float32), 'W1': w(ks[5], (NUM_BLOCKS, D, FF)), 'b1': jnp.zeros((NUM_BLOCKS, FF), jnp.float32), 'W2': w(ks[6], (NUM_BLOCKS, FF, D)), 'b2': jnp.zeros((NUM_BLOCKS, D), jnp.float32), 'ln2_s': jnp.ones((NUM_BLOCKS, D), jnp.float32), 'ln2_b': jnp.zeros((NUM_BLOCKS, D), jnp.float32)}
    _L0_attn_all = _L0_attn_setup()
    _L0_attn_in = {k: v for k, v in _L0_attn_all.items() if k in ('Wq', 'bq', 'Wk', 'bk', 'Wv', 'bv', 'Wo', 'bo', 'ln1_s', 'ln1_b', 'W1', 'b1', 'W2', 'b2', 'ln2_s', 'ln2_b')}
    del _L0_attn_all

    def _L0_ffn_setup():
        import jax, jax.numpy as jnp
        import numpy as np
        D_MODEL = 256
        EXPERT_DIM = 128
        N_EXPERTS = 8
        TOP_K = 2

        def _sq_relu(h):
            return jnp.square(jax.nn.relu(h))
        key = jax.random.key(seed)
        ks = jax.random.split(key, 6)
        s = 0.02
        x = jax.random.normal(ks[0], (2, 512, D_MODEL), dtype=jnp.float32)
        Ws1 = jax.random.normal(ks[1], (D_MODEL, EXPERT_DIM), dtype=jnp.float32) * s
        Ws2 = jax.random.normal(ks[2], (EXPERT_DIM, D_MODEL), dtype=jnp.float32) * s
        W1 = jax.random.normal(ks[3], (N_EXPERTS, D_MODEL, EXPERT_DIM), dtype=jnp.float32) * s
        W2 = jax.random.normal(ks[4], (N_EXPERTS, EXPERT_DIM, D_MODEL), dtype=jnp.float32) * s
        Wr = jax.random.normal(ks[5], (D_MODEL, N_EXPERTS), dtype=jnp.float32) * s
        return {'x': x, 'Ws1': Ws1, 'Ws2': Ws2, 'W1': W1, 'W2': W2, 'Wr': Wr}
    _L0_ffn_all = _L0_ffn_setup()
    _L0_ffn_in = {k: v for k, v in _L0_ffn_all.items() if k in ('Ws1', 'Ws2', 'W1', 'W2', 'Wr')}
    del _L0_ffn_all

    def _L1_attn_setup():
        import jax, jax.numpy as jnp
        import numpy as np
        DIM = 256
        NUM_HEADS = 16
        DIM_HEAD = DIM // NUM_HEADS
        NORM = DIM_HEAD ** (-0.5)
        key = jax.random.key(seed)
        k0, k1, k2, k3 = jax.random.split(key, 4)
        B, N = (2, 512)
        x = jax.random.normal(k0, (B, N, DIM), dtype=jnp.float32)
        Wq = jax.random.normal(k1, (NUM_HEADS, DIM_HEAD, DIM_HEAD), dtype=jnp.float32) * DIM_HEAD ** (-0.5)
        Wp = jax.random.normal(k2, (DIM, DIM), dtype=jnp.float32) * DIM ** (-0.5)
        bp = jax.random.normal(k3, (DIM,), dtype=jnp.float32) * 0.01
        return {'x': x, 'Wq': Wq, 'Wp': Wp, 'bp': bp}
    _L1_attn_all = _L1_attn_setup()
    _L1_attn_in = {k: v for k, v in _L1_attn_all.items() if k in ('Wq', 'Wp', 'bp')}
    del _L1_attn_all

    def _L1_ffn_setup():
        import jax, jax.numpy as jnp
        import numpy as np
        E, K, NG, TG = (64, 8, 8, 4)
        CAP = 256
        SCALE = 2.5

        def _route(x_flat, gate_weight, e_bias):
            T = x_flat.shape[0]
            logits = x_flat.astype(jnp.float32) @ gate_weight.astype(jnp.float32).T
            scores = jax.nn.sigmoid(logits)
            sfc = scores + e_bias[None, :]
            group_scores = jax.lax.top_k(sfc.reshape(T, NG, E // NG), 2)[0].sum(-1)
            _, gidx = jax.lax.top_k(group_scores, TG)
            gmask = jnp.zeros((T, NG), jnp.float32).at[jnp.arange(T)[:, None], gidx].set(1.0)
            smask = jnp.repeat(gmask, E // NG, axis=1)
            tmp = jnp.where(smask > 0, sfc, 0.0)
            _, topk_idx = jax.lax.top_k(tmp, K)
            topk_w = jnp.take_along_axis(scores, topk_idx, axis=1)
            topk_w = topk_w / (topk_w.sum(-1, keepdims=True) + 1e-20)
            return (topk_idx, topk_w * SCALE)

        def _moe_forward(hidden_states, gate_weight, e_bias, w1, w2, w3, shared_gate, shared_up, shared_down):
            B, S, H = hidden_states.shape
            T = B * S
            x = hidden_states.reshape(T, H)
            topk_idx, topk_w = _route(x, gate_weight, e_bias)
            Sk = T * K
            flat_e = topk_idx.reshape(-1)
            order = jnp.argsort(flat_e)
            sorted_e = flat_e[order]
            counts = jax.ops.segment_sum(jnp.ones((Sk,), jnp.int32), flat_e, num_segments=E)
            offsets = jnp.cumsum(counts) - counts
            pos = jnp.arange(Sk) - offsets[sorted_e]
            tok_sorted = x[order // K]
            xe = jnp.zeros((E, CAP, H), x.dtype).at[sorted_e, pos].set(tok_sorted, mode='drop')
            h = jax.nn.silu(jnp.einsum('ech,efh->ecf', xe, w1)) * jnp.einsum('ech,efh->ecf', xe, w3)
            ye = jnp.einsum('ecf,ehf->ech', h, w2)
            pos_c = jnp.minimum(pos, CAP - 1)
            vals = ye[sorted_e, pos_c]
            vals = jnp.where((pos < CAP)[:, None], vals, 0.0)
            flat_w = topk_w.reshape(-1)[order].astype(vals.dtype)
            flat_t = (jnp.arange(Sk) // K)[order]
            out = jax.ops.segment_sum(vals * flat_w[:, None], flat_t, num_segments=T)
            shared = jax.nn.silu(x @ shared_gate.T) * (x @ shared_up.T) @ shared_down.T
            return (out + shared).reshape(B, S, H)
        key = jax.random.key(seed)
        ks = jax.random.split(key, 9)
        B, S, H, F = (1, 512, 256, 128)
        bound = 1.0 / 32.0
        return {'hidden_states': jax.random.normal(ks[0], (B, S, H), jnp.float32), 'gate_weight': jax.random.uniform(ks[1], (E, H), jnp.float32, -bound, bound), 'e_bias': jnp.zeros((E,), jnp.float32), 'w1': jax.random.normal(ks[2], (E, F, H), jnp.float32) * 0.02, 'w2': jax.random.normal(ks[3], (E, H, F), jnp.float32) * 0.02, 'w3': jax.random.normal(ks[4], (E, F, H), jnp.float32) * 0.02, 'shared_gate': jax.random.normal(ks[5], (2 * F, H), jnp.float32) * 0.02, 'shared_up': jax.random.normal(ks[6], (2 * F, H), jnp.float32) * 0.02, 'shared_down': jax.random.normal(ks[7], (H, 2 * F), jnp.float32) * 0.02}
    _L1_ffn_all = _L1_ffn_setup()
    _L1_ffn_in = {k: v for k, v in _L1_ffn_all.items() if k in ('gate_weight', 'e_bias', 'w1', 'w2', 'w3', 'shared_gate', 'shared_up', 'shared_down')}
    del _L1_ffn_all
    return {'x': x, 'L0_tok_head_weight_proj': _L0_tok_in['head_weight_proj'], 'L0_tok_head_weight': _L0_tok_in['head_weight'], 'L0_tok_tail_weight_proj_0': _L0_tok_in['tail_weight_proj_0'], 'L0_tok_tail_weight_0': _L0_tok_in['tail_weight_0'], 'L0_tok_tail_weight_proj_1': _L0_tok_in['tail_weight_proj_1'], 'L0_tok_tail_weight_1': _L0_tok_in['tail_weight_1'], 'L0_attn_Wq': _L0_attn_in['Wq'], 'L0_attn_bq': _L0_attn_in['bq'], 'L0_attn_Wk': _L0_attn_in['Wk'], 'L0_attn_bk': _L0_attn_in['bk'], 'L0_attn_Wv': _L0_attn_in['Wv'], 'L0_attn_bv': _L0_attn_in['bv'], 'L0_attn_Wo': _L0_attn_in['Wo'], 'L0_attn_bo': _L0_attn_in['bo'], 'L0_attn_ln1_s': _L0_attn_in['ln1_s'], 'L0_attn_ln1_b': _L0_attn_in['ln1_b'], 'L0_attn_W1': _L0_attn_in['W1'], 'L0_attn_b1': _L0_attn_in['b1'], 'L0_attn_W2': _L0_attn_in['W2'], 'L0_attn_b2': _L0_attn_in['b2'], 'L0_attn_ln2_s': _L0_attn_in['ln2_s'], 'L0_attn_ln2_b': _L0_attn_in['ln2_b'], 'L0_ffn_Ws1': _L0_ffn_in['Ws1'], 'L0_ffn_Ws2': _L0_ffn_in['Ws2'], 'L0_ffn_W1': _L0_ffn_in['W1'], 'L0_ffn_W2': _L0_ffn_in['W2'], 'L0_ffn_Wr': _L0_ffn_in['Wr'], 'L1_attn_Wq': _L1_attn_in['Wq'], 'L1_attn_Wp': _L1_attn_in['Wp'], 'L1_attn_bp': _L1_attn_in['bp'], 'L1_ffn_gate_weight': _L1_ffn_in['gate_weight'], 'L1_ffn_e_bias': _L1_ffn_in['e_bias'], 'L1_ffn_w1': _L1_ffn_in['w1'], 'L1_ffn_w2': _L1_ffn_in['w2'], 'L1_ffn_w3': _L1_ffn_in['w3'], 'L1_ffn_shared_gate': _L1_ffn_in['shared_gate'], 'L1_ffn_shared_up': _L1_ffn_in['shared_up'], 'L1_ffn_shared_down': _L1_ffn_in['shared_down']}

def reference(x, L0_tok_head_weight_proj, L0_tok_head_weight, L0_tok_tail_weight_proj_0, L0_tok_tail_weight_0, L0_tok_tail_weight_proj_1, L0_tok_tail_weight_1, L0_attn_Wq, L0_attn_bq, L0_attn_Wk, L0_attn_bk, L0_attn_Wv, L0_attn_bv, L0_attn_Wo, L0_attn_bo, L0_attn_ln1_s, L0_attn_ln1_b, L0_attn_W1, L0_attn_b1, L0_attn_W2, L0_attn_b2, L0_attn_ln2_s, L0_attn_ln2_b, L0_ffn_Ws1, L0_ffn_Ws2, L0_ffn_W1, L0_ffn_W2, L0_ffn_Wr, L1_attn_Wq, L1_attn_Wp, L1_attn_bp, L1_ffn_gate_weight, L1_ffn_e_bias, L1_ffn_w1, L1_ffn_w2, L1_ffn_w3, L1_ffn_shared_gate, L1_ffn_shared_up, L1_ffn_shared_down):
    import jax
    import jax.numpy as jnp

    def _L0_tok_ref(x, head_weight_proj, head_weight, tail_weight_proj_0, tail_weight_0, tail_weight_proj_1, tail_weight_1):
        import jax, jax.numpy as jnp
        import numpy as np
        HIDDEN = 256
        CUTOFFS = [5000, 20000, 50000]
        PROJECT_FACTOR = 4
        NUM_TAILS = len(CUTOFFS) - 1
        CUTOFF_ENDS = [0] + CUTOFFS
        BATCH, SEQ = (8, 256)

        def _glorot(key, shape):
            fan_in, fan_out = shape
            limit = np.sqrt(6.0 / (fan_in + fan_out)).astype(np.float32)
            return jax.random.uniform(key, shape, jnp.float32, -limit, limit)
        tables = [head_weight.T[:CUTOFFS[0]], tail_weight_0.T, tail_weight_1.T]
        projs = [head_weight_proj.T, tail_weight_proj_0.T, tail_weight_proj_1.T]
        y = jnp.zeros(x.shape + (HIDDEN,), dtype=jnp.float32)
        for i in range(len(CUTOFF_ENDS) - 1):
            l_idx, r_idx = (CUTOFF_ENDS[i], CUTOFF_ENDS[i + 1])
            mask = (x >= l_idx) & (x < r_idx)
            idx = jnp.where(mask, x - l_idx, 0)
            emb = tables[i][idx]
            proj = jnp.einsum('bsd,dh->bsh', emb, projs[i])
            y = y + jnp.where(mask[..., None], proj, 0.0)
        emb_scale = jnp.asarray(HIDDEN ** 0.5, y.dtype)
        return y * emb_scale

    def _L0_attn_ref(x, Wq, bq, Wk, bk, Wv, bv, Wo, bo, ln1_s, ln1_b, W1, b1, W2, b2, ln2_s, ln2_b):
        import jax, jax.numpy as jnp
        import numpy as np
        NUM_BLOCKS = 4
        B, S, D = (4, 1024, 256)
        A, FF = (256, 1024)
        LN_EPS = 1e-06

        def _ln(x, s, b):
            m = jnp.mean(x, axis=-1, keepdims=True)
            v = jnp.mean(jnp.square(x - m), axis=-1, keepdims=True)
            return (x - m) * jax.lax.rsqrt(v + LN_EPS) * s + b
        for i in range(NUM_BLOCKS):
            residual = x
            q = x @ Wq[i] + bq[i]
            k = x @ Wk[i] + bk[i]
            v = x @ Wv[i] + bv[i]
            Q = jax.nn.elu(q) + 1.0
            K = jax.nn.elu(k) + 1.0
            KV = jnp.einsum('nsh,nsh->nh', K, v, precision='highest')
            Ksum = jnp.sum(K, axis=1)
            Z = 1.0 / (Q * Ksum[:, None, :] + 1e-06)
            V = Q * KV[:, None, :] * Z
            a = jax.nn.gelu(V @ Wo[i] + bo[i])
            a = jax.nn.gelu(a)
            x = _ln(a + residual, ln1_s[i], ln1_b[i])
            residual = x
            h = jax.nn.gelu(x @ W1[i] + b1[i])
            f = jax.nn.gelu(h @ W2[i] + b2[i])
            x = _ln(f + residual, ln2_s[i], ln2_b[i])
        return x

    def _L0_ffn_ref(x, Ws1, Ws2, W1, W2, Wr):
        import jax, jax.numpy as jnp
        import numpy as np
        D_MODEL = 256
        EXPERT_DIM = 128
        N_EXPERTS = 8
        TOP_K = 2

        def _sq_relu(h):
            return jnp.square(jax.nn.relu(h))
        shape = x.shape
        xf = x.reshape(-1, D_MODEL)
        out_shared = _sq_relu(xf @ Ws1) @ Ws2
        logits = xf @ Wr
        top_vals, top_idx = jax.lax.top_k(logits, TOP_K)
        rw = jax.nn.softmax(top_vals.astype(jnp.float32), axis=-1).astype(x.dtype)
        onehot = jax.nn.one_hot(top_idx, N_EXPERTS, dtype=x.dtype)
        prob = jnp.einsum('tk,tke->te', rw, onehot)
        prob = jnp.trunc(prob)
        h = _sq_relu(jnp.einsum('td,edf->tef', xf, W1))
        y = jnp.einsum('tef,efd->ted', h, W2)
        out_routed = jnp.einsum('ted,te->td', y, prob)
        return (out_shared + out_routed).reshape(shape)

    def _L1_attn_ref(x, Wq, Wp, bp):
        import jax, jax.numpy as jnp
        import numpy as np
        DIM = 256
        NUM_HEADS = 16
        DIM_HEAD = DIM // NUM_HEADS
        NORM = DIM_HEAD ** (-0.5)
        B, N, D = x.shape
        xh = x.reshape(B, N, NUM_HEADS, DIM_HEAD)
        q = jnp.einsum('bnhd,hed->bnhe', xh, Wq)
        scores = jnp.einsum('bnhe,bmhe->bhnm', q, q)
        scores = scores / NORM
        attn = jax.nn.softmax(scores, axis=-1)
        res = jnp.einsum('bhnm,bmhe->bnhe', attn, q)
        y = res.reshape(B, N, D)
        y = y @ Wp.T + bp
        return y

    def _L1_ffn_ref(hidden_states, gate_weight, e_bias, w1, w2, w3, shared_gate, shared_up, shared_down):
        import jax, jax.numpy as jnp
        import numpy as np
        E, K, NG, TG = (64, 8, 8, 4)
        CAP = 256
        SCALE = 2.5

        def _route(x_flat, gate_weight, e_bias):
            T = x_flat.shape[0]
            logits = x_flat.astype(jnp.float32) @ gate_weight.astype(jnp.float32).T
            scores = jax.nn.sigmoid(logits)
            sfc = scores + e_bias[None, :]
            group_scores = jax.lax.top_k(sfc.reshape(T, NG, E // NG), 2)[0].sum(-1)
            _, gidx = jax.lax.top_k(group_scores, TG)
            gmask = jnp.zeros((T, NG), jnp.float32).at[jnp.arange(T)[:, None], gidx].set(1.0)
            smask = jnp.repeat(gmask, E // NG, axis=1)
            tmp = jnp.where(smask > 0, sfc, 0.0)
            _, topk_idx = jax.lax.top_k(tmp, K)
            topk_w = jnp.take_along_axis(scores, topk_idx, axis=1)
            topk_w = topk_w / (topk_w.sum(-1, keepdims=True) + 1e-20)
            return (topk_idx, topk_w * SCALE)

        def _moe_forward(hidden_states, gate_weight, e_bias, w1, w2, w3, shared_gate, shared_up, shared_down):
            B, S, H = hidden_states.shape
            T = B * S
            x = hidden_states.reshape(T, H)
            topk_idx, topk_w = _route(x, gate_weight, e_bias)
            Sk = T * K
            flat_e = topk_idx.reshape(-1)
            order = jnp.argsort(flat_e)
            sorted_e = flat_e[order]
            counts = jax.ops.segment_sum(jnp.ones((Sk,), jnp.int32), flat_e, num_segments=E)
            offsets = jnp.cumsum(counts) - counts
            pos = jnp.arange(Sk) - offsets[sorted_e]
            tok_sorted = x[order // K]
            xe = jnp.zeros((E, CAP, H), x.dtype).at[sorted_e, pos].set(tok_sorted, mode='drop')
            h = jax.nn.silu(jnp.einsum('ech,efh->ecf', xe, w1)) * jnp.einsum('ech,efh->ecf', xe, w3)
            ye = jnp.einsum('ecf,ehf->ech', h, w2)
            pos_c = jnp.minimum(pos, CAP - 1)
            vals = ye[sorted_e, pos_c]
            vals = jnp.where((pos < CAP)[:, None], vals, 0.0)
            flat_w = topk_w.reshape(-1)[order].astype(vals.dtype)
            flat_t = (jnp.arange(Sk) // K)[order]
            out = jax.ops.segment_sum(vals * flat_w[:, None], flat_t, num_segments=T)
            shared = jax.nn.silu(x @ shared_gate.T) * (x @ shared_up.T) @ shared_down.T
            return (out + shared).reshape(B, S, H)
        return _moe_forward(hidden_states, gate_weight, e_bias, w1, w2, w3, shared_gate, shared_up, shared_down)
    h = _L0_tok_ref(x, L0_tok_head_weight_proj, L0_tok_head_weight, L0_tok_tail_weight_proj_0, L0_tok_tail_weight_0, L0_tok_tail_weight_proj_1, L0_tok_tail_weight_1)
    h = h + _L0_attn_ref(_layernorm(h, axis=-1), L0_attn_Wq, L0_attn_bq, L0_attn_Wk, L0_attn_bk, L0_attn_Wv, L0_attn_bv, L0_attn_Wo, L0_attn_bo, L0_attn_ln1_s, L0_attn_ln1_b, L0_attn_W1, L0_attn_b1, L0_attn_W2, L0_attn_b2, L0_attn_ln2_s, L0_attn_ln2_b)
    h = h + _L0_ffn_ref(_layernorm(h, axis=-1), L0_ffn_Ws1, L0_ffn_Ws2, L0_ffn_W1, L0_ffn_W2, L0_ffn_Wr)
    h = h + _L1_attn_ref(_layernorm(h, axis=-1), L1_attn_Wq, L1_attn_Wp, L1_attn_bp)
    h = h + _L1_ffn_ref(_layernorm(h, axis=-1), L1_ffn_gate_weight, L1_ffn_e_bias, L1_ffn_w1, L1_ffn_w2, L1_ffn_w3, L1_ffn_shared_gate, L1_ffn_shared_up, L1_ffn_shared_down)
    return h

_drawn_inputs = setup_inputs


def setup_inputs(seed=0):
    import zlib

    import numpy as np

    out = dict(_drawn_inputs(seed))
    spreads = {'L0_attn_bq': (0.0, 2.0),
     'L0_attn_bk': (0.0, 0.8),
     'L0_attn_bv': (0.0, 0.27),
     'L0_attn_bo': (0.0, 0.1),
     'L0_attn_ln1_s': (1.0, 0.2),
     'L0_attn_ln1_b': (0.0, 0.1),
     'L0_attn_b1': (0.0, 0.1),
     'L0_attn_b2': (0.0, 0.1),
     'L0_attn_ln2_s': (1.0, 0.2),
     'L0_attn_ln2_b': (0.0, 0.1),
     'L1_ffn_e_bias': (0.0, 0.8)}
    factors = {'L0_attn_Wq': 64.0,
     'L0_attn_Wk': 8.0,
     'L1_attn_bp': 8.0,
     'L1_ffn_gate_weight': 8.0,
     'L1_ffn_w1': 8.0,
     'L1_ffn_w2': 8.0,
     'L1_ffn_w3': 8.0,
     'L1_ffn_shared_gate': 6.398,
     'L1_ffn_shared_up': 6.5,
     'L1_ffn_shared_down': 6.401}
    for name, (base, spread) in spreads.items():
        noise = np.random.default_rng([zlib.crc32(name.encode()), seed]).standard_normal(out[name].shape)
        drawn = base * np.exp(spread * noise) if base else spread * noise
        out[name] = jnp.asarray(drawn.astype(out[name].dtype))
    for name, factor in factors.items():
        out[name] = (out[name] * factor).astype(out[name].dtype)
    return out
```

```python
import numpy as np
import concourse.bass as bass
from concourse import mybir
from contextlib import ExitStack

F32 = mybir.dt.float32
BF16 = mybir.dt.bfloat16
I32 = mybir.dt.int32
U32 = mybir.dt.uint32
ALU = mybir.AluOpType
ACT = mybir.ActivationFunctionType
AX = mybir.AxisListType

P = 128
T = 2048
D = 256
KD = D // P
NT = T // P
CH = 512
NC = T // CH
TPC = CH // P
SEQ = 256
CUTS = [0, 5000, 20000, 50000]
EMB = [256, 64, 16]
EOFF = [0, 256, 320]
EW = sum(EMB)
BLOCKS = 4
FF = 1024
KF = FF // P
VEC = {}
for _name, _n in (("bq", 2), ("bk", 2), ("bv", 2), ("bo", 2), ("b1", 8), ("b2", 2),
                  ("ln1_s", 2), ("ln1_b", 2), ("ln2_s", 2), ("ln2_b", 2)):
    VEC[_name] = sum(n for _, n in VEC.values()), _n
NVEC = sum(n for _, n in VEC.values())
SCALE_EMB = 16.0


class Chain:

    def __init__(self, eng, sem, base=0):
        self.eng, self.sem, self.base, self.n = eng, sem, base, 0

    def link(self, ins):
        self.n += 1
        ins.then_inc(self.sem, 1)
        self.eng.wait_ge(self.sem, self.base + self.n)


def make_identity(nc, ident, made, eng):
    eng.memset(ident[:, :], 0.0).then_inc(made, 1)
    eng.wait_ge(made, 1)
    eng.affine_select(out=ident[:, :], in_=ident[:, :], compare_op=ALU.not_equal, fill=1.0,
                      base=0, pattern=[[-1, P]], channel_multiplier=1).then_inc(made, 1)
    eng.wait_ge(made, 2)


def normalise(dve, chain, src, stats, mv, veps, eps, veps_ready, rstd_ready, rstd_count, rstd, dst, carrier):
    n = src.shape[1]
    for j in range(n):
        last = dve.bn_stats(stats[:, j, :], src[:, j, :])
    chain.link(last)
    dve.memset(carrier[:, :], 0.0)
    for j in range(n):
        last = dve.bn_aggr(mv[:, j, :], stats[:, j, :])
    chain.link(last)
    dve.tensor_scalar(veps[:, 0:n], mv[:, 0:n, 1], eps, None, ALU.add).then_inc(veps_ready, 1)
    dve.wait_ge(rstd_ready, rstd_count)
    for j in range(n):
        last = dve.tensor_scalar(dst[:, j, :], src[:, j, :], mv[:, j, 0:1], rstd[:, j:j + 1],
                                 ALU.subtract, ALU.mult)
    return last


def embed_phase(nc, ctx0, g, a):
    ctx = ExitStack()
    with ctx:
        def sb(name, shape, dt=F32):
            return ctx.enter_context(nc.sbuf_tensor(name, shape, dt))

        def pb(name, shape, dt=F32):
            return ctx.enter_context(nc.psum_tensor(name, shape, dt))

        def sem(name):
            return ctx.enter_context(nc.semaphore(name))

        ids = sb("e_ids", [P, NT], I32)
        idx = sb("e_idx", [P, 3, NT], I32)
        rows = sb("e_rows", [P, NT, EW])
        proj = sb("e_proj", [P, 3, D])
        rowsT = sb("e_rowsT", [P, 2, 3, P])
        stats = sb("e_stats", [P, TPC, 6])
        mv = sb("e_mv", [P, TPC, 2])
        veps = sb("e_veps", [P, TPC])
        rstd = sb("e_rstd", [P, TPC])
        mhalf = sb("e_mhalf", [P, TPC])
        xn = sb("e_xn", [P, TPC, D])
        pT = [pb(f"e_pT{i}", [P, 512]) for i in range(2)]
        pY = [pb(f"e_pY{i}", [P, 512]) for i in range(2)]
        pX = [pb(f"e_pX{i}", [P, CH]) for i in range(KD)]

        s_ids = sem("e_ids_loaded")
        s_proj = sem("e_proj_loaded")
        s_zero = sem("e_rows_zeroed")
        s_idx = sem("e_idx_ready")
        s_id = sem("e_ident_made")
        s_g = [sem(f"e_gathered{c}") for c in range(NC)]
        s_t = sem("e_rows_transposed")
        s_tc = sem("e_rowsT_ready")
        s_y = sem("e_projected")
        s_h = sem("e_h_ready")
        s_ve = sem("e_veps_ready")
        s_rs = sem("e_rstd_ready")
        s_xn = sem("e_xn_ready")
        s_xt = sem("e_xn_transposed")
        s_xc = sem("e_xT_ready")
        s_dve = sem("e_dve_steps")
        s_mh = sem("e_mhalf_made")

        block = ctx.enter_context(nc.Block())
        ident, h, XT = g["ident"], g["h"], g["XT"]
        tables = [a["head_rows"], a["tail0_rows"], a["tail1_rows"]]

        @block.sync
        def _(sp):
            with nc.allow_non_contiguous_dma(reason="token ids, one per partition"):
                sp.dma_start(ids[:, :], a["x"].rearrange("(t p) -> p t", p=P)).then_inc(s_ids, 16)
            sp.dma_start(proj[:, 0:2, :], a["head_proj"].rearrange("(k p) n -> p k n", p=P)).then_inc(s_proj, 16)
            sp.dma_start(proj[0:EMB[1], 2, :], a["tail0_proj"]).then_inc(s_proj, 16)
            sp.dma_start(proj[EMB[1]:EMB[1] + EMB[2], 2, :], a["tail1_proj"]).then_inc(s_proj, 16)

        @block.gpsimd
        def _(pool):
            make_identity(nc, ident, s_id, pool)
            pool.memset(g["ones"][:, :], 1.0)
            pool.memset(mhalf[:, :], -0.5).then_inc(s_mh, 1)
            pool.wait_ge(s_idx, 1)
            pool.wait_ge(s_zero, 1)
            for t in range(NT):
                for i in range(3):
                    pool.indirect_dma_start(
                        rows[:, t, EOFF[i]:EOFF[i] + EMB[i]], None, tables[i][:, :],
                        bass.IndirectOffsetOnAxis(ap=idx[:, i, t:t + 1].bitcast(U32), axis=0),
                        bounds_check=CUTS[i + 1] - CUTS[i] - 1, oob_is_err=False,
                    ).then_inc(s_g[t // TPC], 16)
            for c in range(NC):
                pool.wait_ge(s_ve, c + 1)
                if c == 0:
                    pool.wait_ge(s_mh, 1)
                pool.tensor_tensor(rstd[:, :], veps[:, :], mhalf[:, :], ALU.pow).then_inc(s_rs, 1)

        @block.vector
        def _(dve):
            chain = Chain(dve, s_dve)
            dve.memset(rows[:, :, :], 0.0).then_inc(s_zero, 1)
            dve.wait_ge(s_ids, 16)
            for i in range(3):
                last = dve.tensor_scalar(idx[:, i, :], ids[:, :], float(-CUTS[i]), None, ALU.add)
            last.then_inc(s_idx, 1)
            for c in range(NC):
                dve.wait_ge(s_h, TPC * (c + 1))
                if c:
                    dve.wait_ge(s_xt, c)
                hc = h[:, c * TPC:(c + 1) * TPC, :]
                normalise(dve, chain, hc, stats, mv, veps, 1e-5, s_ve, s_rs, c + 1, rstd, xn, g["carrier"]).then_inc(s_xn, 1)

        @block.tensor
        def _(pe):
            pe.wait_ge(s_id, 2)
            for c in range(NC):
                pe.wait_ge(s_g[c], 16 * 3 * TPC)
                for j in range(TPC):
                    t = c * TPC + j
                    if t >= 2:
                        pe.wait_ge(s_tc, t - 1)
                    for k in range(3):
                        w = P if k < 2 else EW - 2 * P
                        last = pe.transpose(pT[t % 2][0:w, k * P:(k + 1) * P],
                                            rows[:, t, k * P:k * P + w], ident[:, :])
                    last.then_inc(s_t, 1)
                    if c == 0 and j == 0:
                        pe.wait_ge(s_proj, 48)
                    pe.wait_ge(s_tc, t + 1)
                    for k in range(3):
                        w = P if k < 2 else EW - 2 * P
                        last = pe.matmul(pY[t % 2][:, 0:D], rowsT[0:w, t % 2, k, :], proj[0:w, k, :],
                                         start=(k == 0), stop=(k == 2))
                    last.then_inc(s_y, 1)
                pe.wait_ge(s_xn, c + 1)
                if c:
                    pe.wait_ge(s_xc, c)
                for j in range(TPC):
                    for k in range(KD):
                        last = pe.transpose(pX[k][:, j * P:(j + 1) * P], xn[:, j, k * P:(k + 1) * P], ident[:, :])
                last.then_inc(s_xt, 1)

        @block.scalar
        def _(act):
            for c in range(NC):
                for j in range(TPC):
                    t = c * TPC + j
                    act.wait_ge(s_t, t + 1)
                    if t >= 2:
                        act.wait_ge(s_y, t - 1)
                    act.activation(rowsT[:, t % 2, 0:2, :], pT[t % 2][:, 0:2 * P].rearrange("p (k q) -> p k q", k=2), ACT.Copy)
                    w = EW - 2 * P
                    act.activation(rowsT[0:w, t % 2, 2, :], pT[t % 2][0:w, 2 * P:3 * P], ACT.Copy).then_inc(s_tc, 1)
                    act.wait_ge(s_y, t + 1)
                    act.activation(h[:, t, :], pY[t % 2][:, 0:D], ACT.Copy, scale=SCALE_EMB).then_inc(s_h, 1)
                act.wait_ge(s_xt, c + 1)
                for k in range(KD):
                    last = act.activation(XT[:, k, c * CH:(c + 1) * CH], pX[k][:, :], ACT.Copy)
                last.then_inc(s_xc, 1)


ITEMS = BLOCKS * NC
RING = 4
PER_STEP = 3 * KD + KF + KD + KD
STEPS_BEFORE, LOOPS = 2, (ITEMS - 4) // NC


def products_before(s):
    return 0 if s == 0 else 4 * KD + PER_STEP * (s - 1)


def steps(eng, body):
    for s in range(STEPS_BEFORE):
        body(s, 0)
    with eng.Fori(0, LOOPS) as l:
        for s in range(STEPS_BEFORE, STEPS_BEFORE + NC):
            body(s, l)
    for s in range(STEPS_BEFORE + NC * LOOPS, ITEMS + 2):
        body(s, 0)


def blocks_phase(nc, ctx0, g, a):
    ctx = ExitStack()
    with ctx:
        def sb(name, shape, dt=F32):
            return ctx.enter_context(nc.sbuf_tensor(name, shape, dt))

        def pb(name, shape, dt=F32):
            return ctx.enter_context(nc.psum_tensor(name, shape, dt))

        def sem(name):
            return ctx.enter_context(nc.semaphore(name))

        ident, XT = g["ident"], g["XT"]
        X1T = sb("b_X1T", [P, KD, T])
        wqkv = sb("b_wqkv", [P, 3, KD, D])
        wo = sb("b_wo", [P, KD, D])
        w1 = sb("b_w1", [P, KD, FF])
        w2 = sb("b_w2", [P, KF, D])
        vec = sb("b_vec", [P, BLOCKS * NVEC])
        cur = sb("b_cur", [P, NVEC])
        ncur = sb("b_ncur", [P, 2 * KD])
        nqk = sb("b_nqk", [P, 2, KD, CH])
        eqk = sb("b_eqk", [P, 2, KD, CH])
        em1 = sb("b_em1", [P, 2, KD, CH])
        rqk = sb("b_rqk", [P, 2, KD, CH])
        vv = sb("b_vv", [P, KD, CH])
        Q = sb("b_Q", [P, KD, CH])
        K = sb("b_K", [P, KD, CH])
        prod = sb("b_prod", [P, SEQ])
        ksum = sb("b_ksum", [P, 2 * KD])
        kv = sb("b_kv", [P, 2 * KD])
        den = sb("b_den", [P, KD, CH])
        rec = sb("b_rec", [P, KD, CH])
        mix = sb("b_mix", [P, KD, CH])
        a1 = sb("b_a1", [P, KD, CH])
        a2 = sb("b_a2", [P, KD, CH])
        H = sb("b_H", [P, KF, CH])
        ffo = sb("b_ffo", [P, KD, CH])
        s1 = sb("b_s1", [P, KD, CH])
        s2 = sb("b_s2", [P, KD, CH])
        xn = [sb(f"b_xn{i}", [P, TPC, D]) for i in range(2)]
        stats = sb("b_stats", [P, TPC, 6])
        mv = sb("b_mv", [P, TPC, 2])
        veps = sb("b_veps", [P, TPC])
        rstd = sb("b_rstd", [P, TPC])
        mhalf = sb("b_mhalf", [P, TPC])
        ring = [pb(f"b_ring{i}", [P, CH]) for i in range(RING)]
        pN = pb("b_pN", [P, TPC, D])
        pR = [pb(f"b_pR{i}", [P, CH]) for i in range(KD)]

        s_vec = sem("b_vec_loaded")
        s_wqkv = sem("b_wqkv_loaded")
        s_wo = sem("b_wo_loaded")
        s_w1 = sem("b_w1_loaded")
        s_w2 = sem("b_w2_loaded")
        s_full = sem("b_ring_full")
        s_free = sem("b_ring_free")
        s_qkv = sem("b_qkv_ready")
        s_mix = sem("b_mix_ready")
        s_a = sem("b_a_ready")
        s_a1 = sem("b_a1_ready")
        s_s1 = sem("b_s1_ready")
        s_s2 = sem("b_s2_ready")
        s_h = sem("b_h_ready")
        s_ff = sem("b_ffo_ready")
        s_n = sem("b_rows_natural")
        s_nf = sem("b_pN_free")
        s_ve = sem("b_veps_ready")
        s_rs = sem("b_rstd_ready")
        s_xn1 = sem("b_xn1_ready")
        s_xn2 = sem("b_xn2_ready")
        s_r1 = sem("b_ln1_returned")
        s_r2 = sem("b_ln2_returned")
        s_x1 = sem("b_x1_ready")
        s_x = sem("b_x_ready")
        s_dve = sem("b_dve_steps")
        s_mh = sem("b_mhalf_made")
        s_cur = sem("b_columns_copied")

        block = ctx.enter_context(nc.Block())

        def ln1(s):
            return 1 <= s <= ITEMS

        def ln2(s):
            return 2 <= s <= ITEMS + 1

        def columns_by(s):
            return sum((x % NC == 0 and x < ITEMS) + (ln1(x) and x % NC == 1) + (ln2(x) and x % NC == 2)
                       for x in range(s + 1))

        def norms_before(s):
            return sum(ln1(x) + ln2(x) for x in range(s))

        @block.sync
        def _(sp):
            def load(b, wait):
                if wait:
                    sp.wait_ge(s_full, products_before(NC - 1) + 3 * KD + NC * PER_STEP * (b - 1))
                sp.dma_start(wqkv[:, :, :, :], a["wqkv"][bass.ds(b, 1), :, :, :].rearrange("b j (k p) n -> p (b j) k n", p=P)).then_inc(s_wqkv, 16)
                if wait:
                    sp.wait_ge(s_full, products_before(NC) + NC * PER_STEP * (b - 1))
                sp.dma_start(wo[:, :, :], a["wo"][bass.ds(b, 1), :, :].rearrange("b (k p) n -> p (b k) n", p=P)).then_inc(s_wo, 16)
                if wait:
                    sp.wait_ge(s_full, products_before(NC) + 3 * KD + KF + NC * PER_STEP * (b - 1))
                sp.dma_start(w1[:, :, :], a["w1"][bass.ds(b, 1), :, :].rearrange("b (k p) n -> p (b k) n", p=P)).then_inc(s_w1, 16)
                if wait:
                    sp.wait_ge(s_full, products_before(NC) + 3 * KD + KF + KD + NC * PER_STEP * (b - 1))
                sp.dma_start(w2[:, :, :], a["w2"][bass.ds(b, 1), :, :].rearrange("b (k p) n -> p (b k) n", p=P)).then_inc(s_w2, 16)

            sp.dma_start(vec[:, :], a["vec"]).then_inc(s_vec, 16)
            load(0, False)
            with sp.Fori(1, BLOCKS) as b:
                load(b, True)

        @block.tensor
        def _(pe):
            def body(s, l):
                r = [products_before(min(s, ITEMS))]
                if s > ITEMS:
                    r[0] += KF + KD
                at = NC * PER_STEP * l
                loaded = 16 * (l + s // NC + 1)
                loaded1 = 16 * (l + (s - 1) // NC + 1)

                def product(n_k, lhsT, rhs, ready=None):
                    bank = ring[r[0] % RING]
                    pe.wait_ge(s_free, at + r[0] + 1)
                    for k in range(n_k):
                        if ready:
                            ready(k)
                        last = pe.matmul(bank[:, :], lhsT(k), rhs(k), start=(k == 0), stop=(k == n_k - 1))
                    last.then_inc(s_full, 1)
                    r[0] += 1

                def qkv(j):
                    c = s % NC
                    for m in range(KD):
                        product(KD, lambda k: wqkv[:, j, k, m * P:(m + 1) * P], lambda k: XT[:, k, c * CH:(c + 1) * CH])

                def to_rows(src, n):
                    if n:
                        pe.wait_ge(s_nf, 2 * NC * l + n)
                    for j in range(TPC):
                        for k in range(KD):
                            last = pe.transpose(pN[:, j, k * P:(k + 1) * P], src[:, k, j * P:(j + 1) * P], ident[:, :])
                    last.then_inc(s_n, 1)

                def to_columns(src, done):
                    for j in range(TPC):
                        for k in range(KD):
                            last = pe.transpose(pR[k][:, j * P:(j + 1) * P], src[:, j, k * P:(k + 1) * P], ident[:, :])
                    last.then_inc(done, 1)

                n = norms_before(s)
                if s < ITEMS:
                    if s % NC == 0:
                        pe.wait_ge(s_wqkv, loaded)
                    if s >= NC:
                        pe.wait_ge(s_x, NC * l + s - NC + 1)
                    qkv(0)
                if ln1(s):
                    pe.wait_ge(s_s1, NC * l + s)
                    to_rows(s1, n)
                    n += 1
                if s < ITEMS:
                    qkv(1)
                if ln2(s):
                    pe.wait_ge(s_s2, NC * l + s - 1)
                    to_rows(s2, n)
                if s < ITEMS:
                    qkv(2)
                if ln1(s):
                    pe.wait_ge(s_xn1, NC * l + s)
                    if s >= 3:
                        pe.wait_ge(s_x, NC * l + s - 2)
                    to_columns(xn[0], s_r1)
                    c = (s - 1) % NC
                    if c == 0:
                        pe.wait_ge(s_w1, loaded1)
                    pe.wait_ge(s_x1, NC * l + s)
                    for f in range(KF):
                        product(KD, lambda k: w1[:, k, f * P:(f + 1) * P], lambda k: X1T[:, k, c * CH:(c + 1) * CH])
                if ln2(s):
                    pe.wait_ge(s_xn2, NC * l + s - 1)
                    pe.wait_ge(s_x1, min(ITEMS, s) + NC * l)
                    to_columns(xn[1], s_r2)
                if ln1(s):
                    if (s - 1) % NC == 0:
                        pe.wait_ge(s_w2, loaded1)
                    for m in range(KD):
                        product(KF, lambda k: w2[:, k, m * P:(m + 1) * P], lambda k: H[:, k, :],
                                (lambda k: pe.wait_ge(s_h, KF * (NC * l + s - 1) + k + 1)) if m == 0 else None)
                if s < ITEMS:
                    if s % NC == 0:
                        pe.wait_ge(s_wo, loaded)
                    pe.wait_ge(s_mix, NC * l + s + 1)
                    for m in range(KD):
                        product(KD, lambda k: wo[:, k, m * P:(m + 1) * P], lambda k: mix[:, k, :])

            steps(pe, body)

        @block.scalar
        def _(act):
            act.wait_ge(s_vec, 16)
            for i in range(RING):
                act.sem_inc(s_free, 1)

            def body(s, l):
                r = [products_before(min(s, ITEMS))]
                if s > ITEMS:
                    r[0] += KF + KD
                at = NC * PER_STEP * l

                def col(name, m):
                    return cur[:, VEC[name][0] + m:VEC[name][0] + m + 1]

                def columns(i, first, last):
                    if i % NC == 0:
                        lo, n = VEC[first][0], VEC[last][0] + VEC[last][1] - VEC[first][0]
                        act.activation(cur[:, lo:lo + n], vec[:, bass.ds((l + i // NC) * NVEC + lo, n)], ACT.Copy)\
                           .then_inc(s_cur, 1)

                if s < ITEMS:
                    if s % NC == 0:
                        act.activation(ncur[:, :], vec[:, bass.ds((l + s // NC) * NVEC, 2 * KD)], ACT.Copy, scale=-1.0)
                    columns(s, "bq", "bo")
                if ln1(s):
                    columns(s - 1, "b1", "ln1_b")
                if ln2(s):
                    columns(s - 2, "ln2_s", "ln2_b")
                if s % NC < 3:
                    act.wait_ge(s_cur, columns_by(s) + 3 * l)

                def full():
                    act.wait_ge(s_full, at + r[0] + 1)
                    r[0] += 1
                    return ring[(r[0] - 1) % RING]

                if s < ITEMS:
                    for j, name in enumerate(("bq", "bk")):
                        for m in range(KD):
                            bank = full()
                            act.activation(nqk[:, j, m, :], bank[:, :], ACT.Relu, scale=-1.0,
                                           bias=ncur[:, KD * j + m:KD * j + m + 1])
                            act.activation(rqk[:, j, m, :], bank[:, :], ACT.Relu, bias=col(name, m)).then_inc(s_free, 1)
                    act.wait_ge(s_free, RING + at + r[0])
                    act.activation(eqk[:, :, :, :], nqk[:, :, :, :], ACT.Exp, scale=-1.0)
                    for m in range(KD):
                        bank = full()
                        act.activation(vv[:, m, :], bank[:, :], ACT.Identity, bias=col("bv", m)).then_inc(s_free, 1)
                    act.activation(prod[0:1, 0:1], vec[0:1, 0:1], ACT.Copy).then_inc(s_qkv, 1)
                if ln1(s):
                    act.wait_ge(s_r1, NC * l + s)
                    c = (s - 1) % NC
                    for m in range(KD):
                        last = act.activation(X1T[:, m, c * CH:(c + 1) * CH], pR[m][:, :], ACT.Identity,
                                              bias=col("ln1_b", m), scale=col("ln1_s", m))
                    last.then_inc(s_x1, 1)
                    for f in range(KF):
                        bank = full()
                        act.activation(H[:, f, :], bank[:, :], ACT.Gelu_apprx_tanh, bias=col("b1", f)).then_inc(s_h, 1)
                        act.wait_ge(s_h, KF * (NC * l + s - 1) + f + 1)
                        act.sem_inc(s_free, 1)
                if ln2(s):
                    act.wait_ge(s_r2, NC * l + s - 1)
                    c = (s - 2) % NC
                    for m in range(KD):
                        last = act.activation(XT[:, m, c * CH:(c + 1) * CH], pR[m][:, :], ACT.Identity,
                                              bias=col("ln2_b", m), scale=col("ln2_s", m))
                    last.then_inc(s_x, 1)
                if ln1(s):
                    for m in range(KD):
                        bank = full()
                        act.activation(ffo[:, m, :], bank[:, :], ACT.Gelu_apprx_tanh, bias=col("b2", m)).then_inc(s_ff, 1)
                        act.wait_ge(s_ff, KD * (NC * l + s - 1) + m + 1)
                        act.sem_inc(s_free, 1)
                if s < ITEMS:
                    for m in range(KD):
                        bank = full()
                        act.activation(a1[:, m, :], bank[:, :], ACT.Gelu_apprx_tanh, bias=col("bo", m)).then_inc(s_free, 1)
                    act.wait_ge(s_free, RING + at + r[0])
                    act.activation(a2[:, :, :], a1[:, :, :], ACT.Gelu_apprx_tanh).then_inc(s_a, 1)

            steps(act, body)

        @block.gpsimd
        def _(pool):
            pool.memset(mhalf[:, :], -0.5).then_inc(s_mh, 1)
            pool.wait_ge(s_mh, 1)
            with pool.Fori(0, 2 * ITEMS) as n:
                pool.wait_ge(s_ve, n + 1)
                pool.tensor_tensor(rstd[:, :], veps[:, :], mhalf[:, :], ALU.pow).then_inc(s_rs, 1)

        @block.vector
        def _(dve):
            def chain_at(s, l):
                before = sum(2 * ln1(x) + 2 * ln2(x) + 5 * (x < ITEMS) for x in range(s))
                return before + 9 * NC * l

            def body(s, l):
                chain = Chain(dve, s_dve, chain_at(s, l))
                n = norms_before(s)
                if ln2(s):
                    dve.wait_ge(s_ff, KD * (NC * l + s - 1))
                    c = (s - 2) % NC
                    dve.tensor_tensor(s2[:, :, :], ffo[:, :, :], X1T[:, :, c * CH:(c + 1) * CH], ALU.add).then_inc(s_s2, 1)
                if ln1(s):
                    dve.wait_ge(s_a, NC * l + s)
                    c = (s - 1) % NC
                    dve.tensor_tensor(s1[:, :, :], a2[:, :, :], XT[:, :, c * CH:(c + 1) * CH], ALU.add).then_inc(s_s1, 1)
                    n += 1
                    dve.wait_ge(s_n, 2 * NC * l + n)
                    last = normalise(dve, chain, pN, stats, mv, veps, 1e-6, s_ve, s_rs, 2 * NC * l + n, rstd, xn[0], g["carrier"])
                    last.then_inc(s_xn1, 1)
                    dve.wait_ge(s_xn1, NC * l + s)
                    dve.sem_inc(s_nf, 1)
                if ln2(s):
                    n += 1
                    dve.wait_ge(s_n, 2 * NC * l + n)
                    last = normalise(dve, chain, pN, stats, mv, veps, 1e-6, s_ve, s_rs, 2 * NC * l + n, rstd, xn[1], g["carrier"])
                    last.then_inc(s_xn2, 1)
                    dve.wait_ge(s_xn2, NC * l + s - 1)
                    dve.sem_inc(s_nf, 1)
                if s < ITEMS:
                    dve.wait_ge(s_qkv, NC * l + s + 1)
                    chain.link(dve.tensor_scalar(em1[:, :, :, :], eqk[:, :, :, :], -1.0, None, ALU.add))
                    for m in range(KD):
                        for b in range(2):
                            o = slice(b * SEQ, (b + 1) * SEQ)
                            last = dve.scalar_tensor_tensor(K[:, m, o], em1[:, 1, m, o], 1.0, rqk[:, 1, m, o],
                                                            ALU.add, ALU.add, accum_out=ksum[:, 2 * m + b:2 * m + b + 1])
                    last = dve.scalar_tensor_tensor(Q[:, :, :], em1[:, 0, :, :], 1.0, rqk[:, 0, :, :], ALU.add, ALU.add)
                    chain.link(last)
                    for m in range(KD):
                        for b in range(2):
                            o = slice(b * SEQ, (b + 1) * SEQ)
                            dve.scalar_tensor_tensor(g["junk"][:, 2 * m + b, :], K[:, m, o], 1.0, vv[:, m, o], ALU.mult, ALU.mult,
                                                     accum_out=kv[:, 2 * m + b:2 * m + b + 1])
                            last = dve.tensor_scalar(den[:, m, o], Q[:, m, o], ksum[:, 2 * m + b:2 * m + b + 1], 1e-6,
                                                     ALU.mult, ALU.add)
                    chain.link(last)
                    chain.link(dve.reciprocal(rec[:, :, :], den[:, :, :]))
                    for m in range(KD):
                        for b in range(2):
                            o = slice(b * SEQ, (b + 1) * SEQ)
                            last = dve.scalar_tensor_tensor(mix[:, m, o], Q[:, m, o], kv[:, 2 * m + b:2 * m + b + 1],
                                                            rec[:, m, o], ALU.mult, ALU.mult)
                    last.then_inc(s_mix, 1)
                    chain.n += 1
                    dve.sem_inc(s_dve, 1)
                want = 2 * ln1(s) + 2 * ln2(s) + 5 * (s < ITEMS)
                assert chain.n == want, (s, chain.n, want)

            steps(dve, body)


def to_rows(pe, out, src, col, ident):
    for j in range(TPC):
        for k in range(KD):
            last = pe.transpose(out[:, j, k * P:(k + 1) * P], src[:, k, col + j * P:col + (j + 1) * P], ident[:, :])
    return last


def to_columns(pe, out, src, ident):
    for j in range(TPC):
        for k in range(KD):
            last = pe.transpose(out[k][:, j * P:(j + 1) * P], src[:, j, k * P:(k + 1) * P], ident[:, :])
    return last


EXPERTS0 = 8


def shared0_phase(nc, ctx0, g, a):
    ctx = ExitStack()
    with ctx:
        def sb(name, shape, dt=F32):
            return ctx.enter_context(nc.sbuf_tensor(name, shape, dt))

        def pb(name, shape, dt=F32):
            return ctx.enter_context(nc.psum_tensor(name, shape, dt))

        def sem(name):
            return ctx.enter_context(nc.semaphore(name))

        ident, h, XT, prob = g["ident"], g["h"], g["XT"], g["prob"]
        ws1 = sb("f_ws1", [P, KD, P])
        ws2 = sb("f_ws2", [P, D])
        wr = sb("f_wr", [P, KD, EXPERTS0])
        stats = sb("f_stats", [P, TPC, 6])
        mv = sb("f_mv", [P, TPC, 2])
        veps = sb("f_veps", [P, TPC])
        rstd = sb("f_rstd", [P, TPC])
        mhalf = sb("f_mhalf", [P, TPC])
        xn = sb("f_xn", [P, TPC, D])
        relu = sb("f_relu", [P, CH])
        act2 = sb("f_act2", [P, CH])
        top = sb("f_top", [P, TPC, 8])
        gap = sb("f_gap", [P, TPC])
        egap = sb("f_egap", [P, TPC])
        tot = sb("f_tot", [P, TPC])
        rw = sb("f_rw", [P, TPC])
        whole = sb("f_whole", [P, TPC])
        most = sb("f_most", [P, 1])
        pN = pb("f_pN", [P, TPC, D])
        pR = [pb(f"f_pR{i}", [P, CH]) for i in range(KD)]
        pL = pb("f_pL", [P, 512])
        pH = pb("f_pH", [P, CH])
        pD = pb("f_pD", [P, TPC, D])

        s_w = sem("f_weights_loaded")
        s_mh = sem("f_mhalf_made")
        s_n = sem("f_rows_natural")
        s_nr = sem("f_rows_added")
        s_ve = sem("f_veps_ready")
        s_rs = sem("f_rstd_ready")
        s_xn = sem("f_xn_ready")
        s_r = sem("f_xn_transposed")
        s_x = sem("f_xT_ready")
        s_h1 = sem("f_hidden_done")
        s_re = sem("f_relu_ready")
        s_sq = sem("f_square_ready")
        s_l = sem("f_logits_done")
        s_gap = sem("f_gap_ready")
        s_eg = sem("f_exp_gap_ready")
        s_lr = sem("f_logits_read")
        s_d = sem("f_down_done")
        s_ha = sem("f_h_added")
        s_dve = sem("f_dve_steps")
        s_mo = sem("f_most_ready")
        s_c = sem("f_count_done")

        block = ctx.enter_context(nc.Block())

        @block.sync
        def _(sp):
            sp.dma_start(ws1[:, :, :], a["ws1"].rearrange("(k p) n -> p k n", p=P)).then_inc(s_w, 16)
            sp.dma_start(ws2[:, :], a["ws2"]).then_inc(s_w, 16)
            sp.dma_start(wr[:, :, :], a["wr"].rearrange("(k p) n -> p k n", p=P)).then_inc(s_w, 16)

        @block.tensor
        def _(pe):
            to_rows(pe, pN, XT, 0, ident).then_inc(s_n, 1)
            for c in range(NC):
                pe.wait_ge(s_xn, c + 1)
                if c:
                    pe.wait_ge(s_x, c)
                to_columns(pe, pR, xn, ident).then_inc(s_r, 1)
                if c + 1 < NC:
                    pe.wait_ge(s_nr, c + 1)
                    to_rows(pe, pN, XT, (c + 1) * CH, ident).then_inc(s_n, 1)
                pe.wait_ge(s_x, c + 1)
                if c == 0:
                    pe.wait_ge(s_w, 48)
                if c:
                    pe.wait_ge(s_re, c)
                for k in range(KD):
                    last = pe.matmul(pH[:, :], ws1[:, k, :], XT[:, k, c * CH:(c + 1) * CH], start=(k == 0), stop=(k == KD - 1))
                last.then_inc(s_h1, 1)
                if c:
                    pe.wait_ge(s_lr, c)
                for j in range(TPC):
                    for k in range(KD):
                        last = pe.matmul(pL[:, j * EXPERTS0:(j + 1) * EXPERTS0], XT[:, k, c * CH + j * P:c * CH + (j + 1) * P],
                                         wr[:, k, :], start=(k == 0), stop=(k == KD - 1))
                last.then_inc(s_l, 1)
                pe.wait_ge(s_sq, c + 1)
                if c:
                    pe.wait_ge(s_ha, c)
                for j in range(TPC):
                    last = pe.matmul(pD[:, j, :], act2[:, j * P:(j + 1) * P], ws2[:, :], start=True, stop=True)
                last.then_inc(s_d, 1)
            pe.wait_ge(s_mo, 1)
            pe.matmul(pL[:, 0:1], g["ones"][:, :], most[:, :], start=True, stop=True).then_inc(s_c, 1)

        @block.scalar
        def _(act):
            for c in range(NC):
                act.wait_ge(s_r, c + 1)
                for k in range(KD):
                    last = act.activation(XT[:, k, c * CH:(c + 1) * CH], pR[k][:, :], ACT.Copy)
                last.then_inc(s_x, 1)
                act.wait_ge(s_h1, c + 1)
                act.activation(relu[:, :], pH[:, :], ACT.Relu).then_inc(s_re, 1)
                act.wait_ge(s_gap, c + 1)
                act.activation(egap[:, :], gap[:, :], ACT.Exp).then_inc(s_eg, 1)

        @block.gpsimd
        def _(pool):
            pool.memset(mhalf[:, :], -0.5).then_inc(s_mh, 1)
            pool.wait_ge(s_mh, 1)
            for c in range(NC):
                pool.wait_ge(s_ve, c + 1)
                pool.tensor_tensor(rstd[:, :], veps[:, :], mhalf[:, :], ALU.pow).then_inc(s_rs, 1)

        @block.vector
        def _(dve):
            chain = Chain(dve, s_dve)
            for c in range(NC):
                hc = h[:, c * TPC:(c + 1) * TPC, :]
                dve.wait_ge(s_n, c + 1)
                dve.tensor_tensor(hc, hc, pN[:, :, :], ALU.add).then_inc(s_nr, 1)
                dve.wait_ge(s_nr, c + 1)
                if c:
                    dve.wait_ge(s_r, c)
                normalise(dve, chain, hc, stats, mv, veps, 1e-5, s_ve, s_rs, c + 1, rstd, xn, g["carrier"]).then_inc(s_xn, 1)
                dve.wait_ge(s_re, c + 1)
                dve.tensor_tensor(act2[:, :], relu[:, :], relu[:, :], ALU.mult).then_inc(s_sq, 1)
                dve.wait_ge(s_l, c + 1)
                for j in range(TPC):
                    last = dve.max(top[:, j, :], pL[:, j * EXPERTS0:(j + 1) * EXPERTS0])
                chain.link(last)
                dve.tensor_tensor(gap[:, :], top[:, :, 1], top[:, :, 0], ALU.subtract).then_inc(s_gap, 1)
                dve.wait_ge(s_eg, c + 1)
                chain.link(dve.tensor_scalar(tot[:, :], egap[:, :], 1.0, None, ALU.add))
                chain.link(dve.reciprocal(rw[:, :], tot[:, :]))
                chain.link(dve.tensor_scalar(whole[:, :], rw[:, :], 1.0, None, ALU.is_ge))
                for j in range(TPC):
                    last = dve.tensor_scalar(prob[:, c * TPC + j, :], pL[:, j * EXPERTS0:(j + 1) * EXPERTS0],
                                             top[:, j, 0:1], whole[:, j:j + 1], ALU.is_equal, ALU.mult)
                last.then_inc(s_lr, 1)
                dve.wait_ge(s_d, c + 1)
                dve.tensor_tensor(hc, hc, pD[:, :, :], ALU.add).then_inc(s_ha, 1)
            dve.wait_ge(s_lr, NC)
            dve.tensor_reduce(most[:, :], prob[:, :, :], AX.XY, ALU.max).then_inc(s_mo, 1)
            dve.wait_ge(s_c, 1)
            dve.tensor_copy(g["routed"][:, :], pL[:, 0:1]).then_inc(s_mo, 1)
            dve.wait_ge(s_mo, 2)
            dve.wait_ge(s_ha, NC)


def routed0_phase(nc, ctx0, g, a):
    ctx = ExitStack()
    with ctx:
        def sb(name, shape, dt=F32):
            return ctx.enter_context(nc.sbuf_tensor(name, shape, dt))

        def sem(name):
            return ctx.enter_context(nc.semaphore(name))

        h, XT, prob, flag = g["h"], g["XT"], g["prob"], g["routed"]
        w1 = sb("r_w1", [P, KD, P])
        w2 = sb("r_w2", [P, D])
        pe_col = sb("r_col", [P, NT])
        relu = sb("r_relu", [P, CH])
        act2 = sb("r_act2", [P, CH])
        pH = ctx.enter_context(nc.psum_tensor("r_pH", [P, CH], F32))
        pD = ctx.enter_context(nc.psum_tensor("r_pD", [P, TPC, D], F32))
        s_w = sem("r_weights_loaded")
        s_h1 = sem("r_hidden_done")
        s_re = sem("r_relu_ready")
        s_sq = sem("r_square_ready")
        s_d = sem("r_down_done")
        s_ha = sem("r_h_added")
        s_pr = sem("r_prob_ready")
        block = ctx.enter_context(nc.Block())

        @block.sync
        def _(sp):
            any_routed = sp.value_load(flag[0:1, 0:1], min_val=0, max_val=P)
            with sp.If(any_routed > 0):
                with sp.Fori(0, EXPERTS0) as e:
                    sp.wait_ge(s_d, NC * e + 1)
                    sp.dma_start(w1[:, :, :], a["w1r"][bass.ds(e, 1), :, :].rearrange("e (k p) n -> p (e k) n", p=P)).then_inc(s_w, 16)
                    sp.dma_start(w2[:, :], a["w2r"][bass.ds(e, 1), :, :].rearrange("e p n -> p (e n)")).then_inc(s_w, 16)
                sp.nop()

        @block.tensor
        def _(pe):
            any_routed = pe.value_load(flag[0:1, 0:1], min_val=0, max_val=P)
            with pe.If(any_routed > 0):
                pe.sem_inc(s_d, 1)
                with pe.Fori(0, EXPERTS0) as e:
                    pe.wait_ge(s_w, 32 * e + 32)
                    for c in range(NC):
                        for k in range(KD):
                            last = pe.matmul(pH[:, :], w1[:, k, :], XT[:, k, c * CH:(c + 1) * CH], start=(k == 0), stop=(k == KD - 1))
                        last.then_inc(s_h1, 1)
                        pe.wait_ge(s_sq, NC * e + c + 1)
                        pe.wait_ge(s_ha, NC * e + c + 1)
                        for j in range(TPC):
                            last = pe.matmul(pD[:, j, :], act2[:, j * P:(j + 1) * P], w2[:, :], start=True, stop=True)
                        last.then_inc(s_d, 1)
                pe.nop()

        @block.scalar
        def _(act):
            any_routed = act.value_load(flag[0:1, 0:1], min_val=0, max_val=P)
            with act.If(any_routed > 0):
                with act.Fori(0, EXPERTS0) as e:
                    for c in range(NC):
                        act.wait_ge(s_h1, NC * e + c + 1)
                        act.activation(relu[:, :], pH[:, :], ACT.Relu).then_inc(s_re, 1)
                act.nop()

        @block.vector
        def _(dve):
            any_routed = dve.value_load(flag[0:1, 0:1], min_val=0, max_val=P)
            with dve.If(any_routed > 0):
                dve.sem_inc(s_ha, 1)
                with dve.Fori(0, EXPERTS0) as e:
                    dve.tensor_copy(pe_col[:, :], prob[:, :, bass.ds(e, 1)]).then_inc(s_pr, 1)
                    dve.wait_ge(s_pr, e + 1)
                    for c in range(NC):
                        dve.wait_ge(s_re, NC * e + c + 1)
                        dve.tensor_tensor(act2[:, :], relu[:, :], relu[:, :], ALU.mult).then_inc(s_sq, 1)
                        dve.wait_ge(s_d, NC * e + c + 2)
                        for j in range(TPC):
                            t = c * TPC + j
                            last = dve.scalar_tensor_tensor(h[:, t, :], pD[:, j, :], pe_col[:, t:t + 1], h[:, t, :],
                                                            ALU.mult, ALU.add)
                        last.then_inc(s_ha, 1)
                        dve.wait_ge(s_ha, NC * e + c + 2)
                dve.nop()


HEADS = 16
DH = 16
HG = HEADS // 4
HEADS_C = 2 * HEADS


def attention_phase(nc, ctx0, g, a):
    ctx = ExitStack()
    with ctx:
        def sb(name, shape, dt=F32):
            return ctx.enter_context(nc.sbuf_tensor(name, shape, dt))

        def pb(name, shape, dt=F32):
            return ctx.enter_context(nc.psum_tensor(name, shape, dt))

        def sem(name):
            return ctx.enter_context(nc.semaphore(name))

        ident, h = g["ident"], g["h"]
        wq_heads = sb("a_wq_heads", [P, HG, P])
        wq_rows = sb("a_wq_rows", [P, KD, P])
        wp = sb("a_wp", [P, KD, D])
        bp = sb("a_bp", [1, D])
        one = sb("a_one", [1, P])
        hc = sb("a_hc", [P, TPC, D])
        stats = sb("a_stats", [P, TPC, 6])
        mv = sb("a_mv", [P, TPC, 2])
        veps = sb("a_veps", [P, TPC])
        rstd = sb("a_rstd", [P, TPC])
        mhalf = sb("a_mhalf", [P, TPC])
        xn = sb("a_xn", [P, TPC, D])
        xT = sb("a_xT", [P, KD, CH])
        qT = sb("a_qT", [P, HG, CH])
        q4T = sb("a_q4T", [P, HG, CH])
        qn = sb("a_qn", [P, TPC, D])
        nmax = sb("a_nmax", [P, HEADS_C, 2])
        rsum = sb("a_rsum", [P, 2, 2, HEADS])
        rrec = sb("a_rrec", [P, 2, 2, HEADS])
        E = sb("a_E", [P, 3, 2, SEQ])
        ET = sb("a_ET", [P, 2, 2, SEQ])
        y = sb("a_y", [P, TPC, D])
        yT = sb("a_yT", [P, KD, CH])
        pS = [pb(f"a_pS{i}", [P, 2, SEQ]) for i in range(4)]
        pE = [pb(f"a_pE{i}", [P, 2, SEQ]) for i in range(2)]
        pO = [pb(f"a_pO{i}", [P, 2, D]) for i in range(2)]

        s_z = sem("a_weights_zeroed")
        s_w = sem("a_weights_loaded")
        s_mh = sem("a_constants_made")
        s_dve = sem("a_dve_steps")
        s_ve = sem("a_veps_ready")
        s_rs = sem("a_rstd_ready")
        s_xn = sem("a_xn_ready")
        s_r = sem("a_xn_transposed")
        s_x = sem("a_xT_ready")
        s_q = sem("a_q_projected")
        s_qe = sem("a_q_ready")
        s_qn = sem("a_qn_projected")
        s_qne = sem("a_qn_ready")
        s_s = sem("a_scores_done")
        s_m = sem("a_max_ready")
        s_e = sem("a_exp_ready")
        s_t = sem("a_exp_transposed")
        s_et = sem("a_expT_ready")
        s_o = sem("a_heads_done")
        s_y = sem("a_y_ready")
        s_yt = sem("a_y_transposed")
        s_yte = sem("a_yT_ready")
        s_p = sem("a_projected")
        s_h = sem("a_h_added")

        block = ctx.enter_context(nc.Block())

        @block.sync
        def _(sp):
            sp.wait_ge(s_z, 2)
            for hd in range(HEADS):
                p0 = hd % 8 * DH
                sp.dma_start(wq_heads[p0:p0 + DH, hd // 4, hd % 4 * 32:hd % 4 * 32 + DH], a["wq1"][hd]).then_inc(s_w, 16)
                sp.dma_start(wq_rows[p0:p0 + DH, hd // 8, p0:p0 + DH], a["wq1"][hd]).then_inc(s_w, 16)
            sp.dma_start(wp[:, :, :], a["wp"].rearrange("(k p) n -> p k n", p=P)).then_inc(s_w, 16)
            sp.dma_start(bp[:, :], a["bp"].rearrange("(o n) -> o n", o=1)).then_inc(s_w, 16)

        @block.gpsimd
        def _(pool):
            pool.memset(wq_heads[:, :, :], 0.0).then_inc(s_z, 1)
            pool.memset(wq_rows[:, :, :], 0.0).then_inc(s_z, 1)
            pool.memset(one[:, :], 1.0).then_inc(s_mh, 1)
            pool.memset(mhalf[:, :], -0.5).then_inc(s_mh, 1)
            pool.wait_ge(s_mh, 2)
            with pool.Fori(0, NC) as l:
                pool.wait_ge(s_ve, l + 1)
                pool.tensor_tensor(rstd[:, :], veps[:, :], mhalf[:, :], ALU.pow).then_inc(s_rs, 1)

        @block.tensor
        def _(pe):
            pe.wait_ge(s_mh, 2)
            pe.wait_ge(s_w, 16 * (2 * HEADS + 2))
            with pe.Fori(0, NC) as l:
                n0 = HEADS_C * l
                pe.wait_ge(s_xn, l + 1)
                to_columns(pe, [pS[0][:, :, :].rearrange("p a b -> p (a b)"), pS[1][:, :, :].rearrange("p a b -> p (a b)")],
                           xn, ident).then_inc(s_r, 1)
                pe.wait_ge(s_x, l + 1)
                for gr in range(HG):
                    bank = (pS + pE)[2 + gr]
                    pe.matmul(bank[:, :, :].rearrange("p a b -> p (a b)"), wq_heads[:, gr, :], xT[:, gr // 2, :],
                              start=True, stop=True).then_inc(s_q, 1)
                for j in range(TPC):
                    for k in range(KD):
                        last = pe.matmul(pO[j // 2][:, j % 2, k * P:(k + 1) * P], xT[:, k, j * P:(j + 1) * P], wq_rows[:, k, :],
                                         start=True, stop=True)
                last.then_inc(s_qn, 1)
                pe.wait_ge(s_qe, HG * l + HG)
                pe.wait_ge(s_qne, l + 1)
                for n in range(HEADS_C + 3):
                    if n < HEADS_C:
                        sq, hd = n // HEADS, n % HEADS
                        j, gr = hd % 4, hd // 4
                        if n >= 4:
                            pe.wait_ge(s_e, n0 + n - 3)
                        for nt in range(2):
                            o = sq * SEQ + nt * P
                            last = pe.matmul(pS[n % 4][:, nt, :], qT[32 * j:32 * j + DH, gr, o:o + P],
                                             q4T[32 * j:32 * j + DH, gr, sq * SEQ:(sq + 1) * SEQ], start=True, stop=True,
                                             tile_position=(32 * j, 0))
                        last.then_inc(s_s, 1)
                    if 2 <= n < HEADS_C + 2:
                        m = n - 2
                        pe.wait_ge(s_e, n0 + m + 1)
                        if m >= 2:
                            pe.wait_ge(s_et, n0 + m - 1)
                        for nt in range(2):
                            for mt in range(2):
                                last = pe.transpose(pE[m % 2][:, mt, nt * P:(nt + 1) * P], E[:, m % 3, nt, mt * P:(mt + 1) * P],
                                                    ident[:, :])
                        last.then_inc(s_t, 1)
                    if n >= 3:
                        m = n - 3
                        sq, hd = m // HEADS, m % HEADS
                        pe.wait_ge(s_et, n0 + m + 1)
                        for nt in range(2):
                            for mt in range(2):
                                last = pe.matmul(pO[sq][:, nt, hd * DH:(hd + 1) * DH], ET[:, m % 2, mt, nt * P:(nt + 1) * P],
                                                 qn[:, 2 * sq + mt, hd * DH:(hd + 1) * DH], start=(mt == 0), stop=(mt == 1))
                        last.then_inc(s_o, 1)
                pe.wait_ge(s_y, 2 * l + 2)
                to_columns(pe, [pS[0][:, :, :].rearrange("p a b -> p (a b)"), pS[1][:, :, :].rearrange("p a b -> p (a b)")],
                           y, ident).then_inc(s_yt, 1)
                pe.wait_ge(s_yte, l + 1)
                for j in range(TPC):
                    bank = pS[2 + j // 2][:, j % 2, :]
                    for k in range(KD):
                        pe.matmul(bank, yT[:, k, j * P:(j + 1) * P], wp[:, k, :], start=(k == 0), stop=False)
                    last = pe.matmul(bank, one[:, :], bp[:, :], start=False, stop=True)
                last.then_inc(s_p, 1)

        @block.scalar
        def _(act):
            with act.Fori(0, NC) as l:
                n0 = HEADS_C * l
                act.wait_ge(s_r, l + 1)
                for k in range(KD):
                    last = act.activation(xT[:, k, :], pS[k][:, :, :].rearrange("p a b -> p (a b)"), ACT.Copy)
                last.then_inc(s_x, 1)
                for gr in range(HG):
                    bank = (pS + pE)[2 + gr][:, :, :].rearrange("p a b -> p (a b)")
                    act.wait_ge(s_q, HG * l + gr + 1)
                    act.activation(qT[:, gr, :], bank, ACT.Copy)
                    act.activation(q4T[:, gr, :], bank, ACT.Copy, scale=4.0).then_inc(s_qe, 1)
                for n in range(HEADS_C):
                    sq, hd = n // HEADS, n % HEADS
                    act.wait_ge(s_m, n0 + n + 1)
                    if n >= 3:
                        act.wait_ge(s_t, n0 + n - 2)
                    for nt in range(2):
                        last = act.activation(E[:, n % 3, nt, :], pS[n % 4][:, nt, :], ACT.Exp, bias=nmax[:, n, nt:nt + 1],
                                              accum_out=rsum[:, sq, nt, hd:hd + 1])
                    last.then_inc(s_e, 1)
                act.wait_ge(s_yt, l + 1)
                for k in range(KD):
                    last = act.activation(yT[:, k, :], pS[k][:, :, :].rearrange("p a b -> p (a b)"), ACT.Copy)
                last.then_inc(s_yte, 1)

        @block.vector
        def _(dve):
            with dve.Fori(0, NC) as l:
                n0 = HEADS_C * l
                chain = Chain(dve, s_dve, 5 * l)
                hl = h[:, bass.ds(l * TPC, TPC), :]
                chain.link(dve.tensor_copy(hc[:, :, :], hl))
                normalise(dve, chain, hc, stats, mv, veps, 1e-5, s_ve, s_rs, l + 1, rstd, xn, g["carrier"]).then_inc(s_xn, 1)
                dve.wait_ge(s_qn, l + 1)
                for i in range(2):
                    last = dve.tensor_copy(qn[:, 2 * i:2 * i + 2, :], pO[i][:, :, :])
                last.then_inc(s_qne, 1)
                for n in range(HEADS_C + 2):
                    if n < HEADS_C:
                        dve.wait_ge(s_s, n0 + n + 1)
                        dve.tensor_reduce(nmax[:, n, :], pS[n % 4][:, :, :], AX.X, ALU.max, negate=True).then_inc(s_m, 1)
                    if n >= 2:
                        m = n - 2
                        dve.wait_ge(s_t, n0 + m + 1)
                        if m >= 2:
                            dve.wait_ge(s_o, n0 + m - 1)
                        dve.tensor_copy(ET[:, m % 2, :, :], pE[m % 2][:, :, :]).then_inc(s_et, 1)
                dve.wait_ge(s_e, n0 + HEADS_C)
                chain.link(dve.reciprocal(rrec[:, :, :, :], rsum[:, :, :, :]))
                dve.wait_ge(s_o, n0 + HEADS_C)
                for sq in range(2):
                    r = rrec[:, sq, :, :].rearrange("p a b -> p (a b)").unsqueeze(2).to_broadcast([P, 2 * HEADS, DH])
                    dve.tensor_tensor(y[:, 2 * sq:2 * sq + 2, :].rearrange("p a (h d) -> p (a h) d", d=DH),
                                      pO[sq][:, :, :].rearrange("p a (h d) -> p (a h) d", d=DH), r, ALU.mult).then_inc(s_y, 1)
                dve.wait_ge(s_p, l + 1)
                for i in range(2):
                    last = dve.tensor_tensor(h[:, bass.ds(l * TPC + 2 * i, 2), :], hc[:, 2 * i:2 * i + 2, :], pS[2 + i][:, :, :], ALU.add)
                chain.link(last)


NEXP = 64
TOPK = 8
CAP = 256
NG = 8
TG = 4
EPG = NEXP // NG
ROUTE_SCALE = 2.5
SLOTS = NEXP * CAP
ST = SLOTS // P
SPE = CAP // P
KS = 2
HID = 128


def router_phase(nc, ctx0, g, a):
    ctx = ExitStack()
    with ctx:
        def sb(name, shape, dt=F32):
            return ctx.enter_context(nc.sbuf_tensor(name, shape, dt))

        def pb(name, shape, dt=F32):
            return ctx.enter_context(nc.psum_tensor(name, shape, dt))

        def sem(name):
            return ctx.enter_context(nc.semaphore(name))

        ident, h, idx, wk = g["ident"], g["h"], g["idx"], g["wk"]
        gate = sb("m_gate", [P, KD, NEXP])
        sgate = sb("m_sgate", [P, KD, KS * P])
        sup = sb("m_sup", [P, KD, KS * P])
        sdown = sb("m_sdown", [P, KS, D])
        ebias = sb("m_ebias", [P, NEXP])
        hc = sb("m_hc", [P, TPC, D])
        stats = sb("m_stats", [P, TPC, 6])
        mv = sb("m_mv", [P, TPC, 2])
        veps = sb("m_veps", [P, TPC])
        rstd = sb("m_rstd", [P, TPC])
        mhalf = sb("m_mhalf", [P, TPC])
        xn = sb("m_xn", [P, TPC, D])
        xT = sb("m_xT", [P, KD, CH])
        ones_b = sb("m_ones_b", [P, P], BF16)
        before = sb("m_before", [P, P], BF16)
        lower = sb("m_lower", [P, NG, NG])
        first_i = sb("m_first_i", [P, NEXP], I32)
        first = sb("m_first", [P, NEXP])
        tok_i = sb("m_tok_i", [P, NT], I32)
        tok = sb("m_tok", [P, NT])
        zeros = sb("m_zeros", [P, ST])
        score = sb("m_score", [P, TPC, NEXP])
        sfc = sb("m_sfc", [P, TPC, NEXP])
        top2 = sb("m_top2", [P, TPC * NG, 8])
        gs = sb("m_gs", [P, TPC, NG])
        gt = sb("m_gt", [P, TPC, NG * NG])
        eq = sb("m_eq", [P, TPC, NG * NG])
        eql = sb("m_eql", [P, TPC, NG * NG])
        rank = sb("m_rank", [P, TPC * NG])
        keep = sb("m_keep", [P, TPC * NG])
        kept = sb("m_kept", [P, TPC, NEXP])
        cand = sb("m_cand", [P, TPC, NEXP])
        v8 = sb("m_v8", [P, TPC, 8])
        rest = sb("m_rest", [P, TPC, NEXP])
        M = sb("m_M", [P, TPC, NEXP])
        Mb = sb("m_Mb", [P, TPC, NEXP], BF16)
        w = sb("m_w", [P, TPC, NEXP])
        wsum = sb("m_wsum", [P, TPC])
        wsum2 = sb("m_wsum2", [P, TPC])
        wrec = sb("m_wrec", [P, TPC])
        wfull = sb("m_wfull", [P, TPC, NEXP])
        valid = sb("m_valid", [P, TPC, NEXP])
        slot = sb("m_slot", [P, TPC, NEXP])
        slot1 = sb("m_slot1", [P, TPC, NEXP])
        wv = sb("m_wv", [P, TPC, NEXP])
        s8 = sb("m_s8", [P, TPC, TOPK])
        wkc = sb("m_wkc", [P, TPC, TOPK])
        junk = sb("m_junk", [P, TPC * TOPK, NEXP])
        mch = sb("m_mch", [P, NEXP])
        cum = [sb("m_cum", [P, NEXP]), sb("m_cumb", [P, NEXP], BF16)]
        sg = sb("m_sg", [P, KS, CH])
        sgg = sb("m_sgg", [P, KS, CH])
        hid = sb("m_hid", [P, KS, CH])
        pR = [pb(f"m_pR{i}", [P, CH]) for i in range(KD)]
        pG = pb("m_pG", [P, TPC, NEXP])
        pP = pb("m_pP", [P, TPC, NEXP])
        pA = [pb(f"m_pA{i}", [P, CH]) for i in range(2 * KS)]

        s_w = sem("m_weights_loaded")
        s_z = sem("m_zeros_made")
        s_zd = sem("m_list_zeroed")
        s_c = sem("m_constants_made")
        s_cc = sem("m_constants_cast")
        s_dve = sem("m_dve_steps")
        s_ve = sem("m_veps_ready")
        s_rs = sem("m_rstd_ready")
        s_xn = sem("m_xn_ready")
        s_xd = sem("m_rows_stored")
        s_r = sem("m_xn_transposed")
        s_x = sem("m_xT_ready")
        s_l = sem("m_logits_done")
        s_sc = sem("m_scores_ready")
        s_m = sem("m_mask_ready")
        s_p = sem("m_ranks_done")
        s_ix = sem("m_slots_ready")
        s_sl = sem("m_list_written")
        s_a = sem("m_shared_done")
        s_sg = sem("m_sigmoid_ready")
        s_hd = sem("m_hidden_ready")
        s_d = sem("m_down_done")
        s_h = sem("m_h_added")

        block = ctx.enter_context(nc.Block())

        @block.sync
        def _(sp):
            sp.dma_start(gate[:, :, :], a["gate"].rearrange("(k p) n -> p k n", p=P)).then_inc(s_w, 16)
            sp.dma_start(sgate[:, :, :], a["sgate"].rearrange("(k p) n -> p k n", p=P)).then_inc(s_w, 16)
            sp.dma_start(sup[:, :, :], a["sup"].rearrange("(k p) n -> p k n", p=P)).then_inc(s_w, 16)
            sp.dma_start(sdown[:, :, :], a["sdown"].rearrange("(k p) n -> p k n", p=P)).then_inc(s_w, 16)
            sp.dma_start(ebias[:, :], a["ebias"].rearrange("(o n) -> o n", o=1).to_broadcast([P, NEXP])).then_inc(s_w, 16)
            sp.wait_ge(s_z, 1)
            sp.dma_start(g["slots"].rearrange("(s p) o -> s (p o)", p=P), zeros[:, :]).then_inc(s_zd, 16)
            sp.sem_inc(s_xd, 16)
            with sp.Fori(0, NC) as l:
                sp.wait_ge(s_xn, l + 1)
                sp.dma_start(g["xrows"][bass.ds(l * CH, CH), :].rearrange("(j p) d -> p j d", p=P), xn[:, :, :]).then_inc(s_xd, 16)
            sp.wait_ge(s_xd, 16 * NC + 16)
            sp.wait_ge(s_zd, 16)

        @block.gpsimd
        def _(pool):
            pool.memset(zeros[:, :], 0.0).then_inc(s_z, 1)
            pool.memset(mhalf[:, :], -0.5).then_inc(s_c, 1)
            pool.memset(ones_b[:, :], 1.0).then_inc(s_c, 1)
            pool.memset(before[:, :], 1.0).then_inc(s_c, 1)
            pool.memset(lower[:, :, :], 1.0).then_inc(s_c, 1)
            pool.wait_ge(s_c, 4)
            pool.affine_select(out=before[:, :], in_=before[:, :], compare_op=ALU.is_gt, fill=0.0, base=0,
                               pattern=[[1, P]], channel_multiplier=-1).then_inc(s_c, 1)
            pool.affine_select(out=lower[:, :, :], in_=lower[:, :, :], compare_op=ALU.is_gt, fill=0.0, base=0,
                               pattern=[[1, NG], [-1, NG]], channel_multiplier=0).then_inc(s_c, 1)
            pool.iota(first_i[:, :], [[CAP, NEXP]], base=1, channel_multiplier=0).then_inc(s_c, 1)
            pool.iota(tok_i[:, :], [[P, NT]], base=0, channel_multiplier=1).then_inc(s_c, 1)
            pool.wait_ge(s_zd, 16)
            pool.wait_ge(s_cc, 2)
            for c in range(NC):
                pool.wait_ge(s_ve, c + 1)
                pool.tensor_tensor(rstd[:, :], veps[:, :], mhalf[:, :], ALU.pow).then_inc(s_rs, 1)
                pool.wait_ge(s_ix, c + 1)
                for t in range(c * TPC, (c + 1) * TPC):
                    for k in range(TOPK):
                        pool.indirect_dma_start(
                            g["slots"][:, :], bass.IndirectOffsetOnAxis(ap=idx[:, t, k:k + 1].bitcast(U32), axis=0),
                            tok[:, t:t + 1], None, bounds_check=SLOTS - 1, oob_is_err=False).then_inc(s_sl, 16)
            pool.wait_ge(s_sl, 16 * NT * TOPK)

        @block.tensor
        def _(pe):
            pe.wait_ge(s_c, 8)
            pe.wait_ge(s_w, 80)
            with pe.Fori(0, NC) as l:
                pe.wait_ge(s_xn, l + 1)
                pe.wait_ge(s_h, l + 1)
                to_columns(pe, pR, xn, ident).then_inc(s_r, 1)
                pe.wait_ge(s_x, l + 1)
                for j in range(TPC):
                    for k in range(KD):
                        last = pe.matmul(pG[:, j, :], xT[:, k, j * P:(j + 1) * P], gate[:, k, :], start=(k == 0), stop=(k == KD - 1))
                last.then_inc(s_l, 1)
                for f in range(KS):
                    for i, wt in enumerate((sgate, sup)):
                        for k in range(KD):
                            last = pe.matmul(pA[2 * f + i][:, :], wt[:, k, f * P:(f + 1) * P], xT[:, k, :],
                                             start=(k == 0), stop=(k == KD - 1))
                    last.then_inc(s_a, 1)
                pe.wait_ge(s_m, l + 1)
                for j in range(TPC):
                    pe.matmul(pP[:, j, :], before[:, :], Mb[:, j, :], start=True, stop=False)
                    for i in range(j):
                        pe.matmul(pP[:, j, :], ones_b[:, :], Mb[:, i, :], start=False, stop=False)
                    last = pe.matmul(pP[:, j, :], ones_b[:, :], cum[1][:, :], start=False, stop=True)
                last.then_inc(s_p, 1)
                pe.wait_ge(s_hd, l + 1)
                for j in range(TPC):
                    for f in range(KS):
                        last = pe.matmul(pR[j // 2][:, j % 2 * D:(j % 2 + 1) * D], hid[:, f, j * P:(j + 1) * P], sdown[:, f, :],
                                         start=(f == 0), stop=(f == KS - 1))
                last.then_inc(s_d, 1)

        @block.scalar
        def _(act):
            with act.Fori(0, NC) as l:
                act.wait_ge(s_r, l + 1)
                for k in range(KD):
                    last = act.activation(xT[:, k, :], pR[k][:, :], ACT.Copy)
                last.then_inc(s_x, 1)
                act.wait_ge(s_l, l + 1)
                act.activation(score[:, :, :], pG[:, :, :], ACT.Sigmoid).then_inc(s_sc, 1)
                for f in range(KS):
                    act.wait_ge(s_a, KS * l + f + 1)
                    act.activation(sg[:, f, :], pA[2 * f][:, :], ACT.Sigmoid).then_inc(s_sg, 1)

        @block.vector
        def _(dve):
            dve.wait_ge(s_c, 8)
            dve.tensor_copy(first[:, :], first_i[:, :]).then_inc(s_cc, 1)
            dve.tensor_copy(tok[:, :], tok_i[:, :]).then_inc(s_cc, 1)
            dve.memset(cum[0][:, :], 0.0).then_inc(s_cc, 1)
            dve.memset(cum[1][:, :], 0.0).then_inc(s_cc, 1)
            dve.wait_ge(s_cc, 4)
            dve.wait_ge(s_w, 80)
            dve.sem_inc(s_h, 1)
            with dve.Fori(0, NC) as l:
                LINKS = 26
                chain = Chain(dve, s_dve, LINKS * l)
                link = chain.link
                link(dve.tensor_copy(hc[:, :, :], h[:, bass.ds(l * TPC, TPC), :]))
                dve.wait_ge(s_xd, 16 * l + 16)
                normalise(dve, chain, hc, stats, mv, veps, 1e-5, s_ve, s_rs, l + 1, rstd, xn, g["carrier"]).then_inc(s_xn, 1)
                dve.wait_ge(s_sc, l + 1)
                link(dve.tensor_tensor(sfc[:, :, :], score[:, :, :],
                                       ebias[:, :].unsqueeze(1).to_broadcast([P, TPC, NEXP]), ALU.add))
                by_group = sfc[:, :, :].rearrange("p t (g e) -> p (t g) e", g=NG)
                dve.memset(g["carrier"][:, :], 0.0)
                for i in range(TPC * NG):
                    last = dve.max(top2[:, i, :], by_group[:, i, :])
                link(last)
                link(dve.tensor_tensor(gs[:, :, :].rearrange("p t g -> p (t g)"), top2[:, :, 0], top2[:, :, 1], ALU.add))
                other = gs[:, :, :].unsqueeze(2).to_broadcast([P, TPC, NG, NG])
                own = gs[:, :, :].unsqueeze(3).to_broadcast([P, TPC, NG, NG])
                sq4 = "p t (g o) -> p t g o"
                dve.tensor_tensor(gt[:, :, :].rearrange(sq4, g=NG), other, own, ALU.is_gt)
                link(dve.tensor_tensor(eq[:, :, :].rearrange(sq4, g=NG), other, own, ALU.is_equal))
                low = lower[:, :, :].rearrange("p g o -> p (g o)").unsqueeze(1).to_broadcast([P, TPC, NG * NG])
                link(dve.tensor_tensor(eql[:, :, :], eq[:, :, :], low, ALU.mult))
                link(dve.tensor_tensor(gt[:, :, :], gt[:, :, :], eql[:, :, :], ALU.add))
                link(dve.tensor_reduce(rank[:, :], gt[:, :, :].rearrange("p t (g o) -> p (t g) o", o=NG), AX.X, ALU.add))
                link(dve.tensor_scalar(keep[:, :], rank[:, :], TG - 0.5, None, ALU.is_lt))
                link(dve.tensor_tensor(kept[:, :, :].rearrange("p t (g e) -> p (t g) e", g=NG), by_group,
                                       keep[:, :].unsqueeze(2).to_broadcast([P, TPC * NG, EPG]), ALU.mult))
                link(dve.tensor_scalar(cand[:, :, :], kept[:, :, :], 0.0, None, ALU.add))
                dve.memset(g["carrier"][:, :], 0.0)
                for j in range(TPC):
                    last = dve.max(v8[:, j, :], cand[:, j, :])
                link(last)
                dve.memset(g["carrier"][:, :], 0.0)
                for j in range(TPC):
                    last = dve.match_replace(rest[:, j, :], v8[:, j, :], cand[:, j, :], -3.0e38)
                link(last)
                link(dve.tensor_tensor(M[:, :, :], rest[:, :, :], cand[:, :, :], ALU.not_equal))
                dve.tensor_copy(Mb[:, :, :], M[:, :, :]).then_inc(s_m, 1)
                link(dve.tensor_tensor(w[:, :, :], score[:, :, :], M[:, :, :], ALU.mult))
                link(dve.tensor_reduce(wsum[:, :], w[:, :, :], AX.X, ALU.add))
                link(dve.tensor_scalar(wsum2[:, :], wsum[:, :], 1e-20, 1.0 / ROUTE_SCALE, ALU.add, ALU.mult))
                link(dve.reciprocal(wrec[:, :], wsum2[:, :]))
                link(dve.tensor_tensor(wfull[:, :, :], w[:, :, :], wrec[:, :].unsqueeze(2).to_broadcast([P, TPC, NEXP]), ALU.mult))
                dve.wait_ge(s_p, l + 1)
                dve.tensor_tensor(slot[:, :, :], pP[:, :, :], first[:, :].unsqueeze(1).to_broadcast([P, TPC, NEXP]), ALU.add)
                link(dve.scalar_tensor_tensor(valid[:, :, :], pP[:, :, :], float(CAP), M[:, :, :], ALU.is_lt, ALU.mult))
                dve.tensor_tensor(wv[:, :, :], wfull[:, :, :], valid[:, :, :], ALU.mult)
                dve.tensor_reduce(mch[:, :], M[:, :, :].rearrange("p t e -> p e t"), AX.X, ALU.add)
                link(dve.tensor_tensor(slot1[:, :, :], slot[:, :, :], valid[:, :, :], ALU.mult))
                dve.memset(g["carrier"][:, :], 0.0)
                for j in range(TPC):
                    last = dve.max(s8[:, j, :], slot1[:, j, :])
                link(last)
                dve.tensor_scalar(idx[:, bass.ds(l * TPC, TPC), :], s8[:, :, :], -1.0, None, ALU.add).then_inc(s_ix, 1)
                dve.tensor_tensor(cum[0][:, :], cum[0][:, :], mch[:, :], ALU.add)
                for j in range(TPC):
                    for k in range(TOPK):
                        last = dve.scalar_tensor_tensor(junk[:, TOPK * j + k, :], slot1[:, j, :], s8[:, j, k:k + 1], wv[:, j, :],
                                                        ALU.is_equal, ALU.mult, accum_out=wkc[:, j, k:k + 1])
                link(last)
                dve.tensor_copy(wk[:, bass.ds(l * TPC, TPC), :], wkc[:, :, :])
                dve.tensor_copy(cum[1][:, :], cum[0][:, :])
                for f in range(KS):
                    dve.wait_ge(s_sg, KS * l + f + 1)
                    last = dve.tensor_tensor(sgg[:, f, :], sg[:, f, :], pA[2 * f][:, :], ALU.mult)
                link(last)
                for f in range(KS):
                    last = dve.tensor_tensor(hid[:, f, :], sgg[:, f, :], pA[2 * f + 1][:, :], ALU.mult)
                last.then_inc(s_hd, 1)
                dve.wait_ge(s_d, l + 1)
                for i in range(2):
                    last = dve.tensor_tensor(h[:, bass.ds(l * TPC + 2 * i, 2), :], hc[:, 2 * i:2 * i + 2, :],
                                             pR[i][:, :].rearrange("p (a b) -> p a b", a=2), ALU.add)
                last.then_inc(s_h, 1)
                dve.wait_ge(s_h, l + 2)
                assert chain.n == LINKS, chain.n


RINGX = 4


def expert_steps(eng, body):
    for s in range(2):
        body(s, 0)
    with eng.Fori(0, (NEXP - 4) // RINGX) as l:
        for s in range(2, 2 + RINGX):
            body(s, l)
    for s in range(NEXP - 2, NEXP + 2):
        body(s, 0)


def experts_phase(nc, ctx0, g, a):
    ctx = ExitStack()
    with ctx:
        def sb(name, shape, dt=F32):
            return ctx.enter_context(nc.sbuf_tensor(name, shape, dt))

        def pb(name, shape, dt=F32):
            return ctx.enter_context(nc.psum_tensor(name, shape, dt))

        def sem(name):
            return ctx.enter_context(nc.semaphore(name))

        ident = g["ident"]
        WCOL = 2 * KD * HID + D
        wt = sb("x_wt", [P, RINGX, WCOL])
        lst = sb("x_lst", [P, P])
        lstT = sb("x_lstT", [P, P], I32)
        rows = sb("x_rows", [P, RINGX, SPE, D])
        rowsT = sb("x_rowsT", [P, RINGX, KD * CAP])
        sg = sb("x_sg", [P, RINGX, CAP])
        sgg = sb("x_sgg", [P, RINGX, CAP])
        hid = sb("x_hid", [P, RINGX, CAP])
        ye = sb("x_ye", [P, RINGX, SPE, D])
        pX = [pb(f"x_pX{i}", [P, KD * CAP]) for i in range(2)]
        pU = [pb(f"x_pU{i}", [P, 2, CAP]) for i in range(2)]
        pY = [pb(f"x_pY{i}", [P, SPE, D]) for i in range(2)]

        s_wt = [sem(f"x_weights{i}_loaded") for i in range(RINGX)]
        s_ls = sem("x_list_loaded")
        s_lt = sem("x_list_transposed")
        s_li = sem("x_list_ready")
        s_rw = [sem(f"x_rows{i}_gathered") for i in range(RINGX)]
        s_t = sem("x_rows_transposed")
        s_xt = sem("x_rowsT_ready")
        s_u = sem("x_gate_up_done")
        s_sg = sem("x_sigmoid_ready")
        s_g1 = sem("x_silu_ready")
        s_hd = sem("x_hidden_ready")
        s_y = sem("x_down_done")
        s_ye = sem("x_ye_ready")
        s_yd = [sem(f"x_ye{i}_stored") for i in range(RINGX)]

        block = ctx.enter_context(nc.Block())

        @block.sync
        def _(sp):
            sp.dma_start(lst[:, :], g["slots"].rearrange("(s p) o -> s (p o)", p=P)).then_inc(s_ls, 16)
            for i in range(RINGX):
                sp.dma_start(wt[:, i, :], a["wexp"][i]).then_inc(s_wt[i], 16)
            with sp.Fori(1, NEXP // RINGX) as r:
                for i in range(RINGX):
                    sp.wait_ge(s_y, RINGX * r + i - RINGX + 1)
                    sp.dma_start(wt[:, i, :], a["wexp"][bass.ds(RINGX * r + i, 1), :, :].rearrange("e p n -> p (e n)")).then_inc(s_wt[i], 16)

        @block.gpsimd
        def _(pool):
            pool.wait_ge(s_li, 1)
            for e in range(NEXP):
                if e >= RINGX:
                    pool.wait_ge(s_t, e - RINGX + 1)
                for i in range(SPE):
                    pool.indirect_dma_start(
                        rows[:, e % RINGX, i, :], None, g["xrows"][:, :],
                        bass.IndirectOffsetOnAxis(ap=lstT[:, SPE * e + i:SPE * e + i + 1].bitcast(U32), axis=0),
                        bounds_check=T - 1, oob_is_err=False).then_inc(s_rw[e % RINGX], 16)

        @block.tensor
        def _(pe):
            pe.wait_ge(s_ls, 16)
            pe.transpose(pX[0][:, 0:P], lst[:, :], ident[:, :]).then_inc(s_lt, 1)
            pe.wait_ge(s_li, 1)

            def body(s, l):
                i0 = RINGX * l
                if s < NEXP:
                    pe.wait_ge(s_rw[s % RINGX], 16 * SPE * (l + s // RINGX + 1))
                    for i in range(SPE):
                        for k in range(KD):
                            last = pe.transpose(pX[s % 2][:, k * CAP + i * P:k * CAP + (i + 1) * P],
                                                rows[:, s % RINGX, i, k * P:(k + 1) * P], ident[:, :])
                    last.then_inc(s_t, 1)
                if 1 <= s <= NEXP:
                    e = s - 1
                    pe.wait_ge(s_wt[e % RINGX], 16 * (l + e // RINGX + 1))
                    pe.wait_ge(s_xt, i0 + e + 1)
                    for u in range(2):
                        for k in range(KD):
                            o = (u * KD + k) * HID
                            last = pe.matmul(pU[e % 2][:, u, :], wt[:, e % RINGX, o:o + HID],
                                             rowsT[:, e % RINGX, k * CAP:(k + 1) * CAP], start=(k == 0), stop=(k == KD - 1))
                    last.then_inc(s_u, 1)
                if 2 <= s:
                    e = s - 2
                    pe.wait_ge(s_hd, i0 + e + 1)
                    pe.wait_ge(s_ye, i0 + e + 1)
                    for i in range(SPE):
                        last = pe.matmul(pY[e % 2][:, i, :], hid[:, e % RINGX, i * P:(i + 1) * P],
                                         wt[:, e % RINGX, 2 * KD * HID:], start=True, stop=True)
                    last.then_inc(s_y, 1)

            expert_steps(pe, body)

        @block.scalar
        def _(act):
            def body(s, l):
                i0 = RINGX * l
                if s < NEXP:
                    act.wait_ge(s_t, i0 + s + 1)
                    act.activation(rowsT[:, s % RINGX, :], pX[s % 2][:, :], ACT.Copy).then_inc(s_xt, 1)
                if 1 <= s <= NEXP:
                    e = s - 1
                    act.wait_ge(s_u, i0 + e + 1)
                    act.activation(sg[:, e % RINGX, :], pU[e % 2][:, 0, :], ACT.Sigmoid).then_inc(s_sg, 1)
                if 2 <= s:
                    e = s - 2
                    act.wait_ge(s_y, i0 + e + 1)
                    act.wait_ge(s_yd[e % RINGX], 16 * (l + e // RINGX + 1))
                    act.activation(ye[:, e % RINGX, :, :], pY[e % 2][:, :, :], ACT.Copy).then_inc(s_ye, 1)
                    act.wait_ge(s_ye, i0 + e + 3)
                    act.dma_start(g["yrows"][bass.ds((i0 + e) * CAP, CAP), :].rearrange("(i p) d -> p i d", p=P),
                                  ye[:, e % RINGX, :, :]).then_inc(s_yd[e % RINGX], 16)

            for i in range(RINGX):
                act.sem_inc(s_yd[i], 16)
            for i in range(2):
                act.sem_inc(s_ye, 1)
            expert_steps(act, body)
            for i in range(RINGX):
                act.wait_ge(s_yd[i], 16 * NEXP // RINGX + 16)

        @block.vector
        def _(dve):
            dve.wait_ge(s_lt, 1)
            dve.tensor_copy(lstT[:, :], pX[0][:, 0:P]).then_inc(s_li, 1)

            def body(s, l):
                if 1 <= s <= NEXP:
                    e = s - 1
                    n = RINGX * l + e + 1
                    dve.wait_ge(s_sg, n)
                    dve.tensor_tensor(sgg[:, e % RINGX, :], sg[:, e % RINGX, :], pU[e % 2][:, 0, :], ALU.mult).then_inc(s_g1, 1)
                    dve.wait_ge(s_g1, n)
                    dve.tensor_tensor(hid[:, e % RINGX, :], sgg[:, e % RINGX, :], pU[e % 2][:, 1, :], ALU.mult).then_inc(s_hd, 1)

            expert_steps(dve, body)


def combine_phase(nc, ctx0, g, a, out):
    ctx = ExitStack()
    with ctx:
        def sem(name):
            return ctx.enter_context(nc.semaphore(name))

        h, idx, wk = g["h"], g["idx"], g["wk"]
        yg = ctx.enter_context(nc.sbuf_tensor("c_yg", [P, 2, TOPK, D], F32))
        s_z = sem("c_zeroed")
        s_g = [sem(f"c_rows{i}_gathered") for i in range(2)]
        s_a = sem("c_rows_added")
        s_o = sem("c_out_stored")
        block = ctx.enter_context(nc.Block())

        @block.gpsimd
        def _(pool):
            pool.wait_ge(s_z, 1)
            for t in range(NT):
                if t >= 2:
                    pool.wait_ge(s_a, TOPK * (t - 1))
                for k in range(TOPK):
                    pool.indirect_dma_start(
                        yg[:, t % 2, k, :], None, g["yrows"][:, :],
                        bass.IndirectOffsetOnAxis(ap=idx[:, t, k:k + 1].bitcast(U32), axis=0),
                        bounds_check=SLOTS - 1, oob_is_err=False).then_inc(s_g[t % 2], 16)

        @block.vector
        def _(dve):
            dve.memset(yg[:, :, :, :], 0.0).then_inc(s_z, 1)
            for t in range(NT):
                dve.wait_ge(s_g[t % 2], 16 * TOPK * (t // 2 + 1))
                for k in range(TOPK):
                    dve.scalar_tensor_tensor(h[:, t, :], yg[:, t % 2, k, :], wk[:, t, k:k + 1], h[:, t, :],
                                             ALU.mult, ALU.add).then_inc(s_a, 1)
                    dve.wait_ge(s_a, TOPK * t + k + 1)

        @block.sync
        def _(sp):
            for t in range(NT):
                sp.wait_ge(s_a, TOPK * (t + 1))
                sp.dma_start(out[t * P:(t + 1) * P, :], h[:, t, :]).then_inc(s_o, 16)
            sp.wait_ge(s_o, 16 * NT)


def build(nc, a, out):
    ctx = ExitStack()
    with ctx:
        g = {}
        g["ident"] = ctx.enter_context(nc.sbuf_tensor("ident", [P, P], F32))
        g["ones"] = ctx.enter_context(nc.sbuf_tensor("ones", [P, P], F32))
        g["h"] = ctx.enter_context(nc.sbuf_tensor("h", [P, NT, D], F32))
        g["XT"] = ctx.enter_context(nc.sbuf_tensor("XT", [P, KD, T], F32))
        g["prob"] = ctx.enter_context(nc.sbuf_tensor("prob", [P, NT, EXPERTS0], F32))
        g["routed"] = ctx.enter_context(nc.sbuf_tensor("routed", [P, 1], I32))
        g["idx"] = ctx.enter_context(nc.sbuf_tensor("idx", [P, NT, TOPK], I32))
        g["wk"] = ctx.enter_context(nc.sbuf_tensor("wk", [P, NT, TOPK], F32))
        g["xrows"] = nc.dram_tensor("xrows", (T, D), F32, kind="Internal").ap()
        g["slots"] = nc.dram_tensor("slots", (SLOTS, 1), F32, kind="Internal").ap()
        g["yrows"] = nc.dram_tensor("yrows", (SLOTS, D), F32, kind="Internal").ap()
        g["carrier"] = ctx.enter_context(nc.sbuf_tensor("carrier", [P, 1], F32))
        g["junk"] = ctx.enter_context(nc.sbuf_tensor("junk", [P, 4, SEQ], F32))
        embed_phase(nc, ctx, g, a)
        blocks_phase(nc, ctx, g, a)
        shared0_phase(nc, ctx, g, a)
        routed0_phase(nc, ctx, g, a)
        attention_phase(nc, ctx, g, a)
        router_phase(nc, ctx, g, a)
        experts_phase(nc, ctx, g, a)
        combine_phase(nc, ctx, g, a, out)



def kernel(**inputs):
    import concourse.bacc as bacc
    from concourse.bass_utils import run_bass_kernel_spmd

    i = {k: np.asarray(v) for k, v in inputs.items()}
    A = "L0_attn_"

    def cols(v):
        return v.reshape(BLOCKS, -1, P).transpose(0, 2, 1)

    w1, w3 = (i["L1_ffn_" + n].transpose(0, 2, 1).reshape(NEXP, KD, P, HID).transpose(0, 2, 1, 3).reshape(NEXP, P, KD * HID)
              for n in ("w1", "w3"))
    experts = np.concatenate([w1, w3, i["L1_ffn_w2"].transpose(0, 2, 1)], 2)

    arrays = {
        "x": i["x"].reshape(T),
        "head_rows": i["L0_tok_head_weight"].T[:CUTS[1]],
        "tail0_rows": i["L0_tok_tail_weight_0"].T,
        "tail1_rows": i["L0_tok_tail_weight_1"].T,
        "head_proj": i["L0_tok_head_weight_proj"].T,
        "tail0_proj": i["L0_tok_tail_weight_proj_0"].T,
        "tail1_proj": i["L0_tok_tail_weight_proj_1"].T,
        "wqkv": np.stack([i[A + "Wq"], i[A + "Wk"], i[A + "Wv"]], 1),
        "wo": i[A + "Wo"], "w1": i[A + "W1"], "w2": i[A + "W2"],
        "ws1": i["L0_ffn_Ws1"], "ws2": i["L0_ffn_Ws2"], "wr": i["L0_ffn_Wr"],
        "w1r": i["L0_ffn_W1"], "w2r": i["L0_ffn_W2"],
        "gate": i["L1_ffn_gate_weight"].T, "ebias": i["L1_ffn_e_bias"],
        "sgate": i["L1_ffn_shared_gate"].T, "sup": i["L1_ffn_shared_up"].T, "sdown": i["L1_ffn_shared_down"].T,
        "wexp": experts,
        "wq1": i["L1_attn_Wq"].transpose(0, 2, 1), "wp": i["L1_attn_Wp"].T, "bp": i["L1_attn_bp"],
        "vec": np.concatenate([cols(i[A + n]) for n in VEC], 2).transpose(1, 0, 2).reshape(P, BLOCKS * NVEC),
    }
    nc = bacc.Bacc("TRN2", target_bir_lowering=False, num_devices=1)
    arrays = {"in_" + k: np.ascontiguousarray(v) for k, v in arrays.items()}
    aps = {k[3:]: nc.dram_tensor(k, v.shape, mybir.dt.from_np(v.dtype), kind="ExternalInput").ap()
           for k, v in arrays.items()}
    out = nc.dram_tensor("out", (T, D), F32, kind="ExternalOutput").ap()
    build(nc, aps, out)
    r = run_bass_kernel_spmd(nc, [arrays], core_ids=[0])
    return r.results[0]["out"].reshape(8, 256, 256)
```

```python
import numpy as np
import concourse.bass as bass
from concourse import mybir
from contextlib import ExitStack

F32 = mybir.dt.float32
BF16 = mybir.dt.bfloat16
I32 = mybir.dt.int32
U32 = mybir.dt.uint32
ALU = mybir.AluOpType
ACT = mybir.ActivationFunctionType
AX = mybir.AxisListType

P = 128
T = 2048
D = 256
KD = D // P
NT = T // P
CH = 512
NC = T // CH
TPC = CH // P
SEQ = 256
CUTS = [0, 5000, 20000, 50000]
EMB = [256, 64, 16]
EOFF = [0, 256, 320]
EW = sum(EMB)
BLOCKS = 4
FF = 1024
KF = FF // P
VEC = {}
for _name, _n in (("bq", 2), ("bk", 2), ("bv", 2), ("bo", 2), ("b1", 8), ("b2", 2),
                  ("ln1_s", 2), ("ln1_b", 2), ("ln2_s", 2), ("ln2_b", 2)):
    VEC[_name] = sum(n for _, n in VEC.values()), _n
NVEC = sum(n for _, n in VEC.values())
SCALE_EMB = 16.0


class Chain:

    def __init__(self, eng, sem, base=0):
        self.eng, self.sem, self.base, self.n = eng, sem, base, 0

    def link(self, ins):
        self.n += 1
        ins.then_inc(self.sem, 1)
        self.eng.wait_ge(self.sem, self.base + self.n)


def make_identity(nc, ident, made, eng):
    eng.memset(ident[:, :], 0.0).then_inc(made, 1)
    eng.wait_ge(made, 1)
    eng.affine_select(out=ident[:, :], in_=ident[:, :], compare_op=ALU.not_equal, fill=1.0,
                      base=0, pattern=[[-1, P]], channel_multiplier=1).then_inc(made, 1)
    eng.wait_ge(made, 2)


def normalise(dve, chain, src, stats, mv, veps, eps, veps_ready, rstd_ready, rstd_count, rstd, dst, carrier):
    n = src.shape[1]
    for j in range(n):
        last = dve.bn_stats(stats[:, j, :], src[:, j, :])
    chain.link(last)
    dve.memset(carrier[:, :], 0.0)
    for j in range(n):
        last = dve.bn_aggr(mv[:, j, :], stats[:, j, :])
    chain.link(last)
    dve.tensor_scalar(veps[:, 0:n], mv[:, 0:n, 1], eps, None, ALU.add).then_inc(veps_ready, 1)
    dve.wait_ge(rstd_ready, rstd_count)
    for j in range(n):
        last = dve.tensor_scalar(dst[:, j, :], src[:, j, :], mv[:, j, 0:1], rstd[:, j:j + 1],
                                 ALU.subtract, ALU.mult)
    return last


def embed_phase(nc, ctx0, g, a):
    ctx = ExitStack()
    with nc.cleanup_on_exit(), ctx:
        def sb(name, shape, dt=F32):
            return ctx.enter_context(nc.sbuf_tensor(name, shape, dt))

        def pb(name, shape, dt=F32):
            return ctx.enter_context(nc.psum_tensor(name, shape, dt))

        def sem(name):
            return nc.alloc_semaphore(name)

        ids = sb("e_ids", [P, NT], I32)
        idx = sb("e_idx", [P, 3, NT], I32)
        rows = sb("e_rows", [P, NT, EW])
        proj = sb("e_proj", [P, 3, D])
        rowsT = sb("e_rowsT", [P, 2, 3, P])
        stats = sb("e_stats", [P, TPC, 6])
        mv = sb("e_mv", [P, TPC, 2])
        veps = sb("e_veps", [P, TPC])
        rstd = sb("e_rstd", [P, TPC])
        mhalf = sb("e_mhalf", [P, TPC])
        xn = sb("e_xn", [P, TPC, D])
        pT = [pb(f"e_pT{i}", [P, 512]) for i in range(2)]
        pY = [pb(f"e_pY{i}", [P, 512]) for i in range(2)]
        pX = [pb(f"e_pX{i}", [P, CH]) for i in range(KD)]

        s_ids = sem("e_ids_loaded")
        s_proj = sem("e_proj_loaded")
        s_zero = sem("e_rows_zeroed")
        s_idx = sem("e_idx_ready")
        s_id = sem("e_ident_made")
        s_g = [sem(f"e_gathered{c}") for c in range(NC)]
        s_t = sem("e_rows_transposed")
        s_tc = sem("e_rowsT_ready")
        s_y = sem("e_projected")
        s_h = sem("e_h_ready")
        s_ve = sem("e_veps_ready")
        s_rs = sem("e_rstd_ready")
        s_xn = sem("e_xn_ready")
        s_xt = sem("e_xn_transposed")
        s_xc = sem("e_xT_ready")
        s_dve = sem("e_dve_steps")
        s_mh = sem("e_mhalf_made")

        block = ctx.enter_context(nc.Block())
        ident, h, XT = g["ident"], g["h"], g["XT"]
        tables = [a["head_rows"], a["tail0_rows"], a["tail1_rows"]]

        @block.sync
        def _(sp):
            with nc.allow_non_contiguous_dma(reason="token ids, one per partition"):
                sp.dma_start(ids[:, :], a["x"].rearrange("(t p) -> p t", p=P)).then_inc(s_ids, 16)
            sp.dma_start(proj[:, 0:2, :], a["head_proj"].rearrange("(k p) n -> p k n", p=P)).then_inc(s_proj, 16)
            sp.dma_start(proj[0:EMB[1], 2, :], a["tail0_proj"]).then_inc(s_proj, 16)
            sp.dma_start(proj[EMB[1]:EMB[1] + EMB[2], 2, :], a["tail1_proj"]).then_inc(s_proj, 16)

        @block.gpsimd
        def _(pool):
            make_identity(nc, ident, s_id, pool)
            pool.memset(g["ones"][:, :], 1.0)
            pool.memset(mhalf[:, :], -0.5).then_inc(s_mh, 1)
            pool.wait_ge(s_idx, 1)
            pool.wait_ge(s_zero, 1)
            for t in range(NT):
                for i in range(3):
                    pool.indirect_dma_start(
                        rows[:, t, EOFF[i]:EOFF[i] + EMB[i]], None, tables[i][:, :],
                        bass.IndirectOffsetOnAxis(ap=idx[:, i, t:t + 1].bitcast(U32), axis=0),
                        bounds_check=CUTS[i + 1] - CUTS[i] - 1, oob_is_err=False,
                    ).then_inc(s_g[t // TPC], 16)
            for c in range(NC):
                pool.wait_ge(s_ve, c + 1)
                if c == 0:
                    pool.wait_ge(s_mh, 1)
                pool.tensor_tensor(rstd[:, :], veps[:, :], mhalf[:, :], ALU.pow).then_inc(s_rs, 1)

        @block.vector
        def _(dve):
            chain = Chain(dve, s_dve)
            dve.memset(rows[:, :, :], 0.0).then_inc(s_zero, 1)
            dve.wait_ge(s_ids, 16)
            for i in range(3):
                last = dve.tensor_scalar(idx[:, i, :], ids[:, :], float(-CUTS[i]), None, ALU.add)
            last.then_inc(s_idx, 1)
            for c in range(NC):
                dve.wait_ge(s_h, TPC * (c + 1))
                if c:
                    dve.wait_ge(s_xt, c)
                hc = h[:, c * TPC:(c + 1) * TPC, :]
                normalise(dve, chain, hc, stats, mv, veps, 1e-5, s_ve, s_rs, c + 1, rstd, xn, g["carrier"]).then_inc(s_xn, 1)

        @block.tensor
        def _(pe):
            pe.wait_ge(s_id, 2)
            for c in range(NC):
                pe.wait_ge(s_g[c], 16 * 3 * TPC)
                for j in range(TPC):
                    t = c * TPC + j
                    if t >= 2:
                        pe.wait_ge(s_tc, t - 1)
                    for k in range(3):
                        w = P if k < 2 else EW - 2 * P
                        last = pe.transpose(pT[t % 2][0:w, k * P:(k + 1) * P],
                                            rows[:, t, k * P:k * P + w], ident[:, :])
                    last.then_inc(s_t, 1)
                    if c == 0 and j == 0:
                        pe.wait_ge(s_proj, 48)
                    pe.wait_ge(s_tc, t + 1)
                    for k in range(3):
                        w = P if k < 2 else EW - 2 * P
                        last = pe.matmul(pY[t % 2][:, 0:D], rowsT[0:w, t % 2, k, :], proj[0:w, k, :],
                                         start=(k == 0), stop=(k == 2))
                    last.then_inc(s_y, 1)
                pe.wait_ge(s_xn, c + 1)
                if c:
                    pe.wait_ge(s_xc, c)
                for j in range(TPC):
                    for k in range(KD):
                        last = pe.transpose(pX[k][:, j * P:(j + 1) * P], xn[:, j, k * P:(k + 1) * P], ident[:, :])
                last.then_inc(s_xt, 1)

        @block.scalar
        def _(act):
            for c in range(NC):
                for j in range(TPC):
                    t = c * TPC + j
                    act.wait_ge(s_t, t + 1)
                    if t >= 2:
                        act.wait_ge(s_y, t - 1)
                    act.activation(rowsT[:, t % 2, 0:2, :], pT[t % 2][:, 0:2 * P].rearrange("p (k q) -> p k q", k=2), ACT.Copy)
                    w = EW - 2 * P
                    act.activation(rowsT[0:w, t % 2, 2, :], pT[t % 2][0:w, 2 * P:3 * P], ACT.Copy).then_inc(s_tc, 1)
                    act.wait_ge(s_y, t + 1)
                    act.activation(h[:, t, :], pY[t % 2][:, 0:D], ACT.Copy, scale=SCALE_EMB).then_inc(s_h, 1)
                act.wait_ge(s_xt, c + 1)
                for k in range(KD):
                    last = act.activation(XT[:, k, c * CH:(c + 1) * CH], pX[k][:, :], ACT.Copy)
                last.then_inc(s_xc, 1)


ITEMS = BLOCKS * NC
RING = 4
PER_STEP = 3 * KD + KF + KD + KD
STEPS_BEFORE, LOOPS = 2, (ITEMS - 4) // NC


def products_before(s):
    return 0 if s == 0 else 4 * KD + PER_STEP * (s - 1)


def steps(eng, body):
    for s in range(STEPS_BEFORE):
        body(s, 0)
    with eng.Fori(0, LOOPS) as l:
        for s in range(STEPS_BEFORE, STEPS_BEFORE + NC):
            body(s, l)
    for s in range(STEPS_BEFORE + NC * LOOPS, ITEMS + 2):
        body(s, 0)


def blocks_phase(nc, ctx0, g, a):
    ctx = ExitStack()
    with nc.cleanup_on_exit(), ctx:
        def sb(name, shape, dt=F32):
            return ctx.enter_context(nc.sbuf_tensor(name, shape, dt))

        def pb(name, shape, dt=F32):
            return ctx.enter_context(nc.psum_tensor(name, shape, dt))

        def sem(name):
            return nc.alloc_semaphore(name)

        ident, XT = g["ident"], g["XT"]
        X1T = sb("b_X1T", [P, KD, T])
        wqkv = sb("b_wqkv", [P, 3, KD, D])
        wo = sb("b_wo", [P, KD, D])
        w1 = sb("b_w1", [P, KD, FF])
        w2 = sb("b_w2", [P, KF, D])
        vec = sb("b_vec", [P, BLOCKS * NVEC])
        cur = sb("b_cur", [P, NVEC])
        ncur = sb("b_ncur", [P, 2 * KD])
        nqk = sb("b_nqk", [P, 2, KD, CH])
        eqk = sb("b_eqk", [P, 2, KD, CH])
        em1 = sb("b_em1", [P, 2, KD, CH])
        rqk = sb("b_rqk", [P, 2, KD, CH])
        vv = sb("b_vv", [P, KD, CH])
        Q = sb("b_Q", [P, KD, CH])
        K = sb("b_K", [P, KD, CH])
        prod = sb("b_prod", [P, SEQ])
        ksum = sb("b_ksum", [P, 2 * KD])
        kv = sb("b_kv", [P, 2 * KD])
        den = sb("b_den", [P, KD, CH])
        rec = sb("b_rec", [P, KD, CH])
        mix = sb("b_mix", [P, KD, CH])
        a1 = sb("b_a1", [P, KD, CH])
        a2 = sb("b_a2", [P, KD, CH])
        H = sb("b_H", [P, KF, CH])
        ffo = sb("b_ffo", [P, KD, CH])
        s1 = sb("b_s1", [P, KD, CH])
        s2 = sb("b_s2", [P, KD, CH])
        xn = [sb(f"b_xn{i}", [P, TPC, D]) for i in range(2)]
        stats = sb("b_stats", [P, TPC, 6])
        mv = sb("b_mv", [P, TPC, 2])
        veps = sb("b_veps", [P, TPC])
        rstd = sb("b_rstd", [P, TPC])
        mhalf = sb("b_mhalf", [P, TPC])
        ring = [pb(f"b_ring{i}", [P, CH]) for i in range(RING)]
        pN = pb("b_pN", [P, TPC, D])
        pR = [pb(f"b_pR{i}", [P, CH]) for i in range(KD)]

        s_vec = sem("b_vec_loaded")
        s_wqkv = sem("b_wqkv_loaded")
        s_wo = sem("b_wo_loaded")
        s_w1 = sem("b_w1_loaded")
        s_w2 = sem("b_w2_loaded")
        s_full = sem("b_ring_full")
        s_free = sem("b_ring_free")
        s_qkv = sem("b_qkv_ready")
        s_mix = sem("b_mix_ready")
        s_a = sem("b_a_ready")
        s_a1 = sem("b_a1_ready")
        s_s1 = sem("b_s1_ready")
        s_s2 = sem("b_s2_ready")
        s_h = sem("b_h_ready")
        s_ff = sem("b_ffo_ready")
        s_n = sem("b_rows_natural")
        s_nf = sem("b_pN_free")
        s_ve = sem("b_veps_ready")
        s_rs = sem("b_rstd_ready")
        s_xn1 = sem("b_xn1_ready")
        s_xn2 = sem("b_xn2_ready")
        s_r1 = sem("b_ln1_returned")
        s_r2 = sem("b_ln2_returned")
        s_x1 = sem("b_x1_ready")
        s_x = sem("b_x_ready")
        s_dve = sem("b_dve_steps")
        s_mh = sem("b_mhalf_made")
        s_cur = sem("b_columns_copied")

        block = ctx.enter_context(nc.Block())

        def ln1(s):
            return 1 <= s <= ITEMS

        def ln2(s):
            return 2 <= s <= ITEMS + 1

        def columns_by(s):
            return sum((x % NC == 0 and x < ITEMS) + (ln1(x) and x % NC == 1) + (ln2(x) and x % NC == 2)
                       for x in range(s + 1))

        def norms_before(s):
            return sum(ln1(x) + ln2(x) for x in range(s))

        @block.sync
        def _(sp):
            def load(b, wait):
                if wait:
                    sp.wait_ge(s_full, products_before(NC - 1) + 3 * KD + NC * PER_STEP * (b - 1))
                sp.dma_start(wqkv[:, :, :, :], a["wqkv"][bass.ds(b, 1), :, :, :].rearrange("b j (k p) n -> p (b j) k n", p=P)).then_inc(s_wqkv, 16)
                if wait:
                    sp.wait_ge(s_full, products_before(NC) + NC * PER_STEP * (b - 1))
                sp.dma_start(wo[:, :, :], a["wo"][bass.ds(b, 1), :, :].rearrange("b (k p) n -> p (b k) n", p=P)).then_inc(s_wo, 16)
                if wait:
                    sp.wait_ge(s_full, products_before(NC) + 3 * KD + KF + NC * PER_STEP * (b - 1))
                sp.dma_start(w1[:, :, :], a["w1"][bass.ds(b, 1), :, :].rearrange("b (k p) n -> p (b k) n", p=P)).then_inc(s_w1, 16)
                if wait:
                    sp.wait_ge(s_full, products_before(NC) + 3 * KD + KF + KD + NC * PER_STEP * (b - 1))
                sp.dma_start(w2[:, :, :], a["w2"][bass.ds(b, 1), :, :].rearrange("b (k p) n -> p (b k) n", p=P)).then_inc(s_w2, 16)

            sp.dma_start(vec[:, :], a["vec"]).then_inc(s_vec, 16)
            load(0, False)
            with sp.Fori(1, BLOCKS) as b:
                load(b, True)

        @block.tensor
        def _(pe):
            def body(s, l):
                r = [products_before(min(s, ITEMS))]
                if s > ITEMS:
                    r[0] += KF + KD
                at = NC * PER_STEP * l
                loaded = 16 * (l + s // NC + 1)
                loaded1 = 16 * (l + (s - 1) // NC + 1)

                def product(n_k, lhsT, rhs, ready=None):
                    bank = ring[r[0] % RING]
                    pe.wait_ge(s_free, at + r[0] + 1)
                    for k in range(n_k):
                        if ready:
                            ready(k)
                        last = pe.matmul(bank[:, :], lhsT(k), rhs(k), start=(k == 0), stop=(k == n_k - 1))
                    last.then_inc(s_full, 1)
                    r[0] += 1

                def qkv(j):
                    c = s % NC
                    for m in range(KD):
                        product(KD, lambda k: wqkv[:, j, k, m * P:(m + 1) * P], lambda k: XT[:, k, c * CH:(c + 1) * CH])

                def to_rows(src, n):
                    if n:
                        pe.wait_ge(s_nf, 2 * NC * l + n)
                    for j in range(TPC):
                        for k in range(KD):
                            last = pe.transpose(pN[:, j, k * P:(k + 1) * P], src[:, k, j * P:(j + 1) * P], ident[:, :])
                    last.then_inc(s_n, 1)

                def to_columns(src, done):
                    for j in range(TPC):
                        for k in range(KD):
                            last = pe.transpose(pR[k][:, j * P:(j + 1) * P], src[:, j, k * P:(k + 1) * P], ident[:, :])
                    last.then_inc(done, 1)

                n = norms_before(s)
                if s < ITEMS:
                    if s % NC == 0:
                        pe.wait_ge(s_wqkv, loaded)
                    if s >= NC:
                        pe.wait_ge(s_x, NC * l + s - NC + 1)
                    qkv(0)
                if ln1(s):
                    pe.wait_ge(s_s1, NC * l + s)
                    to_rows(s1, n)
                    n += 1
                if s < ITEMS:
                    qkv(1)
                if ln2(s):
                    pe.wait_ge(s_s2, NC * l + s - 1)
                    to_rows(s2, n)
                if s < ITEMS:
                    qkv(2)
                if ln1(s):
                    pe.wait_ge(s_xn1, NC * l + s)
                    if s >= 3:
                        pe.wait_ge(s_x, NC * l + s - 2)
                    to_columns(xn[0], s_r1)
                    c = (s - 1) % NC
                    if c == 0:
                        pe.wait_ge(s_w1, loaded1)
                    pe.wait_ge(s_x1, NC * l + s)
                    for f in range(KF):
                        product(KD, lambda k: w1[:, k, f * P:(f + 1) * P], lambda k: X1T[:, k, c * CH:(c + 1) * CH])
                if ln2(s):
                    pe.wait_ge(s_xn2, NC * l + s - 1)
                    pe.wait_ge(s_x1, min(ITEMS, s) + NC * l)
                    to_columns(xn[1], s_r2)
                if ln1(s):
                    if (s - 1) % NC == 0:
                        pe.wait_ge(s_w2, loaded1)
                    for m in range(KD):
                        product(KF, lambda k: w2[:, k, m * P:(m + 1) * P], lambda k: H[:, k, :],
                                (lambda k: pe.wait_ge(s_h, KF * (NC * l + s - 1) + k + 1)) if m == 0 else None)
                if s < ITEMS:
                    if s % NC == 0:
                        pe.wait_ge(s_wo, loaded)
                    pe.wait_ge(s_mix, NC * l + s + 1)
                    for m in range(KD):
                        product(KD, lambda k: wo[:, k, m * P:(m + 1) * P], lambda k: mix[:, k, :])

            steps(pe, body)

        @block.scalar
        def _(act):
            act.wait_ge(s_vec, 16)
            for i in range(RING):
                act.sem_inc(s_free, 1)

            def body(s, l):
                r = [products_before(min(s, ITEMS))]
                if s > ITEMS:
                    r[0] += KF + KD
                at = NC * PER_STEP * l

                def col(name, m):
                    return cur[:, VEC[name][0] + m:VEC[name][0] + m + 1]

                def columns(i, first, last):
                    if i % NC == 0:
                        lo, n = VEC[first][0], VEC[last][0] + VEC[last][1] - VEC[first][0]
                        act.activation(cur[:, lo:lo + n], vec[:, bass.ds((l + i // NC) * NVEC + lo, n)], ACT.Copy)\
                           .then_inc(s_cur, 1)

                if s < ITEMS:
                    if s % NC == 0:
                        act.activation(ncur[:, :], vec[:, bass.ds((l + s // NC) * NVEC, 2 * KD)], ACT.Copy, scale=-1.0)
                    columns(s, "bq", "bo")
                if ln1(s):
                    columns(s - 1, "b1", "ln1_b")
                if ln2(s):
                    columns(s - 2, "ln2_s", "ln2_b")
                if s % NC < 3:
                    act.wait_ge(s_cur, columns_by(s) + 3 * l)

                def full():
                    act.wait_ge(s_full, at + r[0] + 1)
                    r[0] += 1
                    return ring[(r[0] - 1) % RING]

                if s < ITEMS:
                    for j, name in enumerate(("bq", "bk")):
                        for m in range(KD):
                            bank = full()
                            act.activation(nqk[:, j, m, :], bank[:, :], ACT.Relu, scale=-1.0,
                                           bias=ncur[:, KD * j + m:KD * j + m + 1])
                            act.activation(rqk[:, j, m, :], bank[:, :], ACT.Relu, bias=col(name, m)).then_inc(s_free, 1)
                    act.wait_ge(s_free, RING + at + r[0])
                    act.activation(eqk[:, :, :, :], nqk[:, :, :, :], ACT.Exp, scale=-1.0)
                    for m in range(KD):
                        bank = full()
                        act.activation(vv[:, m, :], bank[:, :], ACT.Identity, bias=col("bv", m)).then_inc(s_free, 1)
                    act.activation(prod[0:1, 0:1], vec[0:1, 0:1], ACT.Copy).then_inc(s_qkv, 1)
                if ln1(s):
                    act.wait_ge(s_r1, NC * l + s)
                    c = (s - 1) % NC
                    for m in range(KD):
                        last = act.activation(X1T[:, m, c * CH:(c + 1) * CH], pR[m][:, :], ACT.Identity,
                                              bias=col("ln1_b", m), scale=col("ln1_s", m))
                    last.then_inc(s_x1, 1)
                    for f in range(KF):
                        bank = full()
                        act.activation(H[:, f, :], bank[:, :], ACT.Gelu_apprx_tanh, bias=col("b1", f)).then_inc(s_h, 1)
                        act.wait_ge(s_h, KF * (NC * l + s - 1) + f + 1)
                        act.sem_inc(s_free, 1)
                if ln2(s):
                    act.wait_ge(s_r2, NC * l + s - 1)
                    c = (s - 2) % NC
                    for m in range(KD):
                        last = act.activation(XT[:, m, c * CH:(c + 1) * CH], pR[m][:, :], ACT.Identity,
                                              bias=col("ln2_b", m), scale=col("ln2_s", m))
                    last.then_inc(s_x, 1)
                if ln1(s):
                    for m in range(KD):
                        bank = full()
                        act.activation(ffo[:, m, :], bank[:, :], ACT.Gelu_apprx_tanh, bias=col("b2", m)).then_inc(s_ff, 1)
                        act.wait_ge(s_ff, KD * (NC * l + s - 1) + m + 1)
                        act.sem_inc(s_free, 1)
                if s < ITEMS:
                    for m in range(KD):
                        bank = full()
                        act.activation(a1[:, m, :], bank[:, :], ACT.Gelu_apprx_tanh, bias=col("bo", m)).then_inc(s_free, 1)
                    act.wait_ge(s_free, RING + at + r[0])
                    act.activation(a2[:, :, :], a1[:, :, :], ACT.Gelu_apprx_tanh).then_inc(s_a, 1)

            steps(act, body)

        @block.gpsimd
        def _(pool):
            pool.memset(mhalf[:, :], -0.5).then_inc(s_mh, 1)
            pool.wait_ge(s_mh, 1)
            with pool.Fori(0, 2 * ITEMS) as n:
                pool.wait_ge(s_ve, n + 1)
                pool.tensor_tensor(rstd[:, :], veps[:, :], mhalf[:, :], ALU.pow).then_inc(s_rs, 1)

        @block.vector
        def _(dve):
            def chain_at(s, l):
                before = sum(2 * ln1(x) + 2 * ln2(x) + 5 * (x < ITEMS) for x in range(s))
                return before + 9 * NC * l

            def body(s, l):
                chain = Chain(dve, s_dve, chain_at(s, l))
                n = norms_before(s)
                if ln2(s):
                    dve.wait_ge(s_ff, KD * (NC * l + s - 1))
                    c = (s - 2) % NC
                    dve.tensor_tensor(s2[:, :, :], ffo[:, :, :], X1T[:, :, c * CH:(c + 1) * CH], ALU.add).then_inc(s_s2, 1)
                if ln1(s):
                    dve.wait_ge(s_a, NC * l + s)
                    c = (s - 1) % NC
                    dve.tensor_tensor(s1[:, :, :], a2[:, :, :], XT[:, :, c * CH:(c + 1) * CH], ALU.add).then_inc(s_s1, 1)
                    n += 1
                    dve.wait_ge(s_n, 2 * NC * l + n)
                    last = normalise(dve, chain, pN, stats, mv, veps, 1e-6, s_ve, s_rs, 2 * NC * l + n, rstd, xn[0], g["carrier"])
                    last.then_inc(s_xn1, 1)
                    dve.wait_ge(s_xn1, NC * l + s)
                    dve.sem_inc(s_nf, 1)
                if ln2(s):
                    n += 1
                    dve.wait_ge(s_n, 2 * NC * l + n)
                    last = normalise(dve, chain, pN, stats, mv, veps, 1e-6, s_ve, s_rs, 2 * NC * l + n, rstd, xn[1], g["carrier"])
                    last.then_inc(s_xn2, 1)
                    dve.wait_ge(s_xn2, NC * l + s - 1)
                    dve.sem_inc(s_nf, 1)
                if s < ITEMS:
                    dve.wait_ge(s_qkv, NC * l + s + 1)
                    chain.link(dve.tensor_scalar(em1[:, :, :, :], eqk[:, :, :, :], -1.0, None, ALU.add))
                    for m in range(KD):
                        for b in range(2):
                            o = slice(b * SEQ, (b + 1) * SEQ)
                            last = dve.scalar_tensor_tensor(K[:, m, o], em1[:, 1, m, o], 1.0, rqk[:, 1, m, o],
                                                            ALU.add, ALU.add, accum_out=ksum[:, 2 * m + b:2 * m + b + 1])
                    last = dve.scalar_tensor_tensor(Q[:, :, :], em1[:, 0, :, :], 1.0, rqk[:, 0, :, :], ALU.add, ALU.add)
                    chain.link(last)
                    for m in range(KD):
                        for b in range(2):
                            o = slice(b * SEQ, (b + 1) * SEQ)
                            dve.scalar_tensor_tensor(g["junk"][:, 2 * m + b, :], K[:, m, o], 1.0, vv[:, m, o], ALU.mult, ALU.mult,
                                                     accum_out=kv[:, 2 * m + b:2 * m + b + 1])
                            last = dve.tensor_scalar(den[:, m, o], Q[:, m, o], ksum[:, 2 * m + b:2 * m + b + 1], 1e-6,
                                                     ALU.mult, ALU.add)
                    chain.link(last)
                    chain.link(dve.reciprocal(rec[:, :, :], den[:, :, :]))
                    for m in range(KD):
                        for b in range(2):
                            o = slice(b * SEQ, (b + 1) * SEQ)
                            last = dve.scalar_tensor_tensor(mix[:, m, o], Q[:, m, o], kv[:, 2 * m + b:2 * m + b + 1],
                                                            rec[:, m, o], ALU.mult, ALU.mult)
                    last.then_inc(s_mix, 1)
                    chain.n += 1
                    dve.sem_inc(s_dve, 1)
                want = 2 * ln1(s) + 2 * ln2(s) + 5 * (s < ITEMS)
                assert chain.n == want, (s, chain.n, want)

            steps(dve, body)


def to_rows(pe, out, src, col, ident):
    for j in range(TPC):
        for k in range(KD):
            last = pe.transpose(out[:, j, k * P:(k + 1) * P], src[:, k, col + j * P:col + (j + 1) * P], ident[:, :])
    return last


def to_columns(pe, out, src, ident):
    for j in range(TPC):
        for k in range(KD):
            last = pe.transpose(out[k][:, j * P:(j + 1) * P], src[:, j, k * P:(k + 1) * P], ident[:, :])
    return last


EXPERTS0 = 8


def shared0_phase(nc, ctx0, g, a):
    ctx = ExitStack()
    with ctx:
        def sb(name, shape, dt=F32):
            return ctx.enter_context(nc.sbuf_tensor(name, shape, dt))

        def pb(name, shape, dt=F32):
            return ctx.enter_context(nc.psum_tensor(name, shape, dt))

        def sem(name):
            return ctx.enter_context(nc.semaphore(name))

        ident, h, XT, prob = g["ident"], g["h"], g["XT"], g["prob"]
        ws1 = sb("f_ws1", [P, KD, P])
        ws2 = sb("f_ws2", [P, D])
        wr = sb("f_wr", [P, KD, EXPERTS0])
        stats = sb("f_stats", [P, TPC, 6])
        mv = sb("f_mv", [P, TPC, 2])
        veps = sb("f_veps", [P, TPC])
        rstd = sb("f_rstd", [P, TPC])
        mhalf = sb("f_mhalf", [P, TPC])
        xn = sb("f_xn", [P, TPC, D])
        relu = sb("f_relu", [P, CH])
        act2 = sb("f_act2", [P, CH])
        top = sb("f_top", [P, TPC, 8])
        gap = sb("f_gap", [P, TPC])
        egap = sb("f_egap", [P, TPC])
        tot = sb("f_tot", [P, TPC])
        rw = sb("f_rw", [P, TPC])
        whole = sb("f_whole", [P, TPC])
        most = sb("f_most", [P, 1])
        pN = pb("f_pN", [P, TPC, D])
        pR = [pb(f"f_pR{i}", [P, CH]) for i in range(KD)]
        pL = pb("f_pL", [P, 512])
        pH = pb("f_pH", [P, CH])
        pD = pb("f_pD", [P, TPC, D])

        s_w = sem("f_weights_loaded")
        s_mh = sem("f_mhalf_made")
        s_n = sem("f_rows_natural")
        s_nr = sem("f_rows_added")
        s_ve = sem("f_veps_ready")
        s_rs = sem("f_rstd_ready")
        s_xn = sem("f_xn_ready")
        s_r = sem("f_xn_transposed")
        s_x = sem("f_xT_ready")
        s_h1 = sem("f_hidden_done")
        s_re = sem("f_relu_ready")
        s_sq = sem("f_square_ready")
        s_l = sem("f_logits_done")
        s_gap = sem("f_gap_ready")
        s_eg = sem("f_exp_gap_ready")
        s_lr = sem("f_logits_read")
        s_d = sem("f_down_done")
        s_ha = sem("f_h_added")
        s_dve = sem("f_dve_steps")
        s_mo = sem("f_most_ready")
        s_c = sem("f_count_done")

        block = ctx.enter_context(nc.Block())

        @block.sync
        def _(sp):
            sp.dma_start(ws1[:, :, :], a["ws1"].rearrange("(k p) n -> p k n", p=P)).then_inc(s_w, 16)
            sp.dma_start(ws2[:, :], a["ws2"]).then_inc(s_w, 16)
            sp.dma_start(wr[:, :, :], a["wr"].rearrange("(k p) n -> p k n", p=P)).then_inc(s_w, 16)

        @block.tensor
        def _(pe):
            to_rows(pe, pN, XT, 0, ident).then_inc(s_n, 1)
            for c in range(NC):
                pe.wait_ge(s_xn, c + 1)
                if c:
                    pe.wait_ge(s_x, c)
                to_columns(pe, pR, xn, ident).then_inc(s_r, 1)
                if c + 1 < NC:
                    pe.wait_ge(s_nr, c + 1)
                    to_rows(pe, pN, XT, (c + 1) * CH, ident).then_inc(s_n, 1)
                pe.wait_ge(s_x, c + 1)
                if c == 0:
                    pe.wait_ge(s_w, 48)
                if c:
                    pe.wait_ge(s_re, c)
                for k in range(KD):
                    last = pe.matmul(pH[:, :], ws1[:, k, :], XT[:, k, c * CH:(c + 1) * CH], start=(k == 0), stop=(k == KD - 1))
                last.then_inc(s_h1, 1)
                if c:
                    pe.wait_ge(s_lr, c)
                for j in range(TPC):
                    for k in range(KD):
                        last = pe.matmul(pL[:, j * EXPERTS0:(j + 1) * EXPERTS0], XT[:, k, c * CH + j * P:c * CH + (j + 1) * P],
                                         wr[:, k, :], start=(k == 0), stop=(k == KD - 1))
                last.then_inc(s_l, 1)
                pe.wait_ge(s_sq, c + 1)
                if c:
                    pe.wait_ge(s_ha, c)
                for j in range(TPC):
                    last = pe.matmul(pD[:, j, :], act2[:, j * P:(j + 1) * P], ws2[:, :], start=True, stop=True)
                last.then_inc(s_d, 1)
            pe.wait_ge(s_mo, 1)
            pe.matmul(pL[:, 0:1], g["ones"][:, :], most[:, :], start=True, stop=True).then_inc(s_c, 1)

        @block.scalar
        def _(act):
            for c in range(NC):
                act.wait_ge(s_r, c + 1)
                for k in range(KD):
                    last = act.activation(XT[:, k, c * CH:(c + 1) * CH], pR[k][:, :], ACT.Copy)
                last.then_inc(s_x, 1)
                act.wait_ge(s_h1, c + 1)
                act.activation(relu[:, :], pH[:, :], ACT.Relu).then_inc(s_re, 1)
                act.wait_ge(s_gap, c + 1)
                act.activation(egap[:, :], gap[:, :], ACT.Exp).then_inc(s_eg, 1)

        @block.gpsimd
        def _(pool):
            pool.memset(mhalf[:, :], -0.5).then_inc(s_mh, 1)
            pool.wait_ge(s_mh, 1)
            for c in range(NC):
                pool.wait_ge(s_ve, c + 1)
                pool.tensor_tensor(rstd[:, :], veps[:, :], mhalf[:, :], ALU.pow).then_inc(s_rs, 1)

        @block.vector
        def _(dve):
            chain = Chain(dve, s_dve)
            for c in range(NC):
                hc = h[:, c * TPC:(c + 1) * TPC, :]
                dve.wait_ge(s_n, c + 1)
                dve.tensor_tensor(hc, hc, pN[:, :, :], ALU.add).then_inc(s_nr, 1)
                dve.wait_ge(s_nr, c + 1)
                if c:
                    dve.wait_ge(s_r, c)
                normalise(dve, chain, hc, stats, mv, veps, 1e-5, s_ve, s_rs, c + 1, rstd, xn, g["carrier"]).then_inc(s_xn, 1)
                dve.wait_ge(s_re, c + 1)
                dve.tensor_tensor(act2[:, :], relu[:, :], relu[:, :], ALU.mult).then_inc(s_sq, 1)
                dve.wait_ge(s_l, c + 1)
                for j in range(TPC):
                    last = dve.max(top[:, j, :], pL[:, j * EXPERTS0:(j + 1) * EXPERTS0])
                chain.link(last)
                dve.tensor_tensor(gap[:, :], top[:, :, 1], top[:, :, 0], ALU.subtract).then_inc(s_gap, 1)
                dve.wait_ge(s_eg, c + 1)
                chain.link(dve.tensor_scalar(tot[:, :], egap[:, :], 1.0, None, ALU.add))
                chain.link(dve.reciprocal(rw[:, :], tot[:, :]))
                chain.link(dve.tensor_scalar(whole[:, :], rw[:, :], 1.0, None, ALU.is_ge))
                for j in range(TPC):
                    last = dve.tensor_scalar(prob[:, c * TPC + j, :], pL[:, j * EXPERTS0:(j + 1) * EXPERTS0],
                                             top[:, j, 0:1], whole[:, j:j + 1], ALU.is_equal, ALU.mult)
                last.then_inc(s_lr, 1)
                dve.wait_ge(s_d, c + 1)
                dve.tensor_tensor(hc, hc, pD[:, :, :], ALU.add).then_inc(s_ha, 1)
            dve.wait_ge(s_lr, NC)
            dve.tensor_reduce(most[:, :], prob[:, :, :], AX.XY, ALU.max).then_inc(s_mo, 1)
            dve.wait_ge(s_c, 1)
            dve.tensor_copy(g["routed"][:, :], pL[:, 0:1]).then_inc(s_mo, 1)
            dve.wait_ge(s_mo, 2)
            dve.wait_ge(s_ha, NC)


def routed0_phase(nc, ctx0, g, a):
    ctx = ExitStack()
    with ctx:
        def sb(name, shape, dt=F32):
            return ctx.enter_context(nc.sbuf_tensor(name, shape, dt))

        def sem(name):
            return ctx.enter_context(nc.semaphore(name))

        h, XT, prob, flag = g["h"], g["XT"], g["prob"], g["routed"]
        w1 = sb("r_w1", [P, KD, P])
        w2 = sb("r_w2", [P, D])
        pe_col = sb("r_col", [P, NT])
        relu = sb("r_relu", [P, CH])
        act2 = sb("r_act2", [P, CH])
        pH = ctx.enter_context(nc.psum_tensor("r_pH", [P, CH], F32))
        pD = ctx.enter_context(nc.psum_tensor("r_pD", [P, TPC, D], F32))
        s_w = sem("r_weights_loaded")
        s_h1 = sem("r_hidden_done")
        s_re = sem("r_relu_ready")
        s_sq = sem("r_square_ready")
        s_d = sem("r_down_done")
        s_ha = sem("r_h_added")
        s_pr = sem("r_prob_ready")
        block = ctx.enter_context(nc.Block())

        @block.sync
        def _(sp):
            any_routed = sp.value_load(flag[0:1, 0:1], min_val=0, max_val=P)
            with sp.If(any_routed > 0):
                with sp.Fori(0, EXPERTS0) as e:
                    sp.wait_ge(s_d, NC * e + 1)
                    sp.dma_start(w1[:, :, :], a["w1r"][bass.ds(e, 1), :, :].rearrange("e (k p) n -> p (e k) n", p=P)).then_inc(s_w, 16)
                    sp.dma_start(w2[:, :], a["w2r"][bass.ds(e, 1), :, :].rearrange("e p n -> p (e n)")).then_inc(s_w, 16)
                sp.nop()

        @block.tensor
        def _(pe):
            any_routed = pe.value_load(flag[0:1, 0:1], min_val=0, max_val=P)
            with pe.If(any_routed > 0):
                pe.sem_inc(s_d, 1)
                with pe.Fori(0, EXPERTS0) as e:
                    pe.wait_ge(s_w, 32 * e + 32)
                    for c in range(NC):
                        for k in range(KD):
                            last = pe.matmul(pH[:, :], w1[:, k, :], XT[:, k, c * CH:(c + 1) * CH], start=(k == 0), stop=(k == KD - 1))
                        last.then_inc(s_h1, 1)
                        pe.wait_ge(s_sq, NC * e + c + 1)
                        pe.wait_ge(s_ha, NC * e + c + 1)
                        for j in range(TPC):
                            last = pe.matmul(pD[:, j, :], act2[:, j * P:(j + 1) * P], w2[:, :], start=True, stop=True)
                        last.then_inc(s_d, 1)
                pe.nop()

        @block.scalar
        def _(act):
            any_routed = act.value_load(flag[0:1, 0:1], min_val=0, max_val=P)
            with act.If(any_routed > 0):
                with act.Fori(0, EXPERTS0) as e:
                    for c in range(NC):
                        act.wait_ge(s_h1, NC * e + c + 1)
                        act.activation(relu[:, :], pH[:, :], ACT.Relu).then_inc(s_re, 1)
                act.nop()

        @block.vector
        def _(dve):
            any_routed = dve.value_load(flag[0:1, 0:1], min_val=0, max_val=P)
            with dve.If(any_routed > 0):
                dve.sem_inc(s_ha, 1)
                with dve.Fori(0, EXPERTS0) as e:
                    dve.tensor_copy(pe_col[:, :], prob[:, :, bass.ds(e, 1)]).then_inc(s_pr, 1)
                    dve.wait_ge(s_pr, e + 1)
                    for c in range(NC):
                        dve.wait_ge(s_re, NC * e + c + 1)
                        dve.tensor_tensor(act2[:, :], relu[:, :], relu[:, :], ALU.mult).then_inc(s_sq, 1)
                        dve.wait_ge(s_d, NC * e + c + 2)
                        for j in range(TPC):
                            t = c * TPC + j
                            last = dve.scalar_tensor_tensor(h[:, t, :], pD[:, j, :], pe_col[:, t:t + 1], h[:, t, :],
                                                            ALU.mult, ALU.add)
                        last.then_inc(s_ha, 1)
                        dve.wait_ge(s_ha, NC * e + c + 2)
                dve.nop()


HEADS = 16
DH = 16
SEQS = T // SEQ
SPLIT = 3
LEFT = (0, 0, 1, 1, 0, 2, 1, 2)
RIGHT = (0, 1, 0, 1, 2, 0, 2, 1)
QUAD = 4
HW = P // QUAD
RING = 3


def queries_phase(nc, ctx0, g, a):
    ctx = ExitStack()
    with ctx:
        def sb(name, shape, dt=F32):
            return ctx.enter_context(nc.sbuf_tensor(name, shape, dt))

        def pb(name, shape, dt=F32):
            return ctx.enter_context(nc.psum_tensor(name, shape, dt))

        def sem(name):
            return ctx.enter_context(nc.semaphore(name))

        ident, h, qn = g["ident"], g["h"], g["qn"]
        wq = sb("q_wq", [P, KD, P])
        stats = sb("q_stats", [P, TPC, 6])
        mv = sb("q_mv", [P, TPC, 2])
        veps = sb("q_veps", [P, TPC])
        rstd = sb("q_rstd", [P, TPC])
        mhalf = sb("q_mhalf", [P, TPC])
        xn = sb("q_xn", [P, 2, TPC, D])
        xT = sb("q_xT", [P, 2, KD, CH])
        part = sb("q_part", [P, 2, SPLIT, KD, CH], BF16)
        rest = sb("q_rest", [P, KD, CH])
        pR = [pb(f"q_pR{i}", [P, CH]) for i in range(KD)]
        pQ = [pb(f"q_pQ{i}", [P, CH]) for i in range(KD)]
        pN = [pb(f"q_pN{i}", [P, 2, D]) for i in range(2)]

        s_z = sem("q_weights_zeroed")
        s_w = sem("q_weights_loaded")
        s_c = sem("q_constants_made")
        s_dve = sem("q_dve_steps")
        s_ve = sem("q_veps_ready")
        s_rs = sem("q_rstd_ready")
        s_xn = sem("q_xn_ready")
        s_r = sem("q_xn_transposed")
        s_x = sem("q_xT_ready")
        s_q = sem("q_projected")
        s_n = sem("q_rows_projected")
        s_p1 = sem("q_part1_ready")
        s_r1 = sem("q_rest_ready")
        s_p2 = sem("q_part2_ready")
        s_p3 = sem("q_part3_ready")
        s_ne = sem("q_rows_ready")
        s_st = [sem(f"q_parts{i}_stored") for i in range(2)]

        block = ctx.enter_context(nc.Block())

        @block.sync
        def _(sp):
            sp.wait_ge(s_z, 1)
            for hd in range(HEADS):
                p0 = hd % 8 * DH
                sp.dma_start(wq[p0:p0 + DH, hd // 8, p0:p0 + DH], a["wq1"][hd]).then_inc(s_w, 16)
            for c in range(NC):
                sp.wait_ge(s_p3, c + 1)
                for i in range(SPLIT):
                    sp.dma_start(g["qparts"][i].rearrange("(k p) t -> p k t", p=P)[:, :, c * CH:(c + 1) * CH],
                                 part[:, c % 2, i, :, :]).then_inc(s_st[c % 2], 16)
            for i in range(2):
                sp.wait_ge(s_st[i], 16 * SPLIT * NC // 2)

        @block.gpsimd
        def _(pool):
            pool.memset(wq[:, :, :], 0.0).then_inc(s_z, 1)
            pool.memset(mhalf[:, :], -0.5).then_inc(s_c, 1)
            sel = g["sel"]
            pool.memset(sel[:, :, :], 0.0).then_inc(s_c, 1)
            for i in range(SPLIT):
                pool.wait_ge(s_c, 2 + i)
                pool.affine_select(out=sel[:, :, :], in_=sel[:, :, :], compare_op=ALU.not_equal, fill=1.0,
                                   base=-HEADS * i, pattern=[[-1, HEADS], [0, P]], channel_multiplier=1).then_inc(s_c, 1)
            for c in range(NC):
                pool.wait_ge(s_ve, c + 1)
                pool.tensor_tensor(rstd[:, :], veps[:, :], mhalf[:, :], ALU.pow).then_inc(s_rs, 1)
            pool.wait_ge(s_c, 2 + SPLIT)

        @block.tensor
        def _(pe):
            pe.wait_ge(s_w, 16 * HEADS)
            for c in range(NC):
                pe.wait_ge(s_xn, c + 1)
                if c:
                    pe.wait_ge(s_x, c)
                to_columns(pe, pR, xn[:, c % 2, :, :], ident).then_inc(s_r, 1)
                pe.wait_ge(s_x, c + 1)
                if c:
                    pe.wait_ge(s_r1, c)
                for k in range(KD):
                    last = pe.matmul(pQ[k][:, :], wq[:, k, :], xT[:, c % 2, k, :], start=True, stop=True)
                last.then_inc(s_q, 1)
                if c:
                    pe.wait_ge(s_ne, c)
                for j in range(TPC):
                    for k in range(KD):
                        last = pe.matmul(pN[j // 2][:, j % 2, k * P:(k + 1) * P], xT[:, c % 2, k, j * P:(j + 1) * P], wq[:, k, :],
                                         start=True, stop=True)
                last.then_inc(s_n, 1)

        @block.scalar
        def _(act):
            for c in range(NC):
                act.wait_ge(s_r, c + 1)
                for k in range(KD):
                    last = act.activation(xT[:, c % 2, k, :], pR[k][:, :], ACT.Copy)
                last.then_inc(s_x, 1)
                act.wait_ge(s_q, c + 1)
                if c >= 2:
                    act.wait_ge(s_st[c % 2], 16 * SPLIT * (c // 2))
                for k in range(KD):
                    last = act.activation(part[:, c % 2, 0, k, :], pQ[k][:, :], ACT.Copy)
                last.then_inc(s_p1, 1)
                act.wait_ge(s_r1, c + 1)
                act.activation(part[:, c % 2, 1, :, :], rest[:, :, :], ACT.Copy).then_inc(s_p2, 1)

        @block.vector
        def _(dve):
            chain = Chain(dve, s_dve)

            def norm(c):
                hl = h[:, c * TPC:(c + 1) * TPC, :]
                normalise(dve, chain, hl, stats, mv, veps, 1e-5, s_ve, s_rs, c + 1, rstd, xn[:, c % 2, :, :], g["carrier"])\
                    .then_inc(s_xn, 1)

            dve.tensor_copy(g["ident_b"][:, :], ident[:, :]).then_inc(s_dve, 1)
            chain.n += 1
            norm(0)
            for c in range(NC):
                if c + 1 < NC:
                    if c >= 1:
                        dve.wait_ge(s_r, c)
                    norm(c + 1)
                dve.wait_ge(s_p1, c + 1)
                if c:
                    dve.wait_ge(s_p3, c)
                for k in range(KD):
                    last = dve.tensor_tensor(rest[:, k, :], pQ[k][:, :], part[:, c % 2, 0, k, :], ALU.subtract)
                last.then_inc(s_r1, 1)
                dve.wait_ge(s_n, c + 1)
                for i in range(2):
                    last = dve.tensor_copy(qn[:, c * TPC + 2 * i:c * TPC + 2 * i + 2, :, :],
                                           pN[i][:, :, :].rearrange("p a (h d) -> p a h d", d=DH))
                last.then_inc(s_ne, 1)
                dve.wait_ge(s_p2, c + 1)
                dve.wait_ge(s_r1, c + 1)
                dve.tensor_tensor(part[:, c % 2, 2, :, :], rest[:, :, :], part[:, c % 2, 1, :, :], ALU.subtract).then_inc(s_p3, 1)
            dve.wait_ge(s_ne, NC)


def attention_phase(nc, ctx0, g, a):
    ctx = ExitStack()
    with ctx:
        def sb(name, shape, dt=F32):
            return ctx.enter_context(nc.sbuf_tensor(name, shape, dt))

        def pb(name, shape, dt=F32):
            return ctx.enter_context(nc.psum_tensor(name, shape, dt))

        def sem(name):
            return ctx.enter_context(nc.semaphore(name))

        ident, h, qn, sel = g["ident"], g["h"], g["qn"], g["sel"]
        NTS = SEQ // P
        QUADS = HEADS // QUAD
        wp = sb("a_wp", [P, KD, D])
        bp = sb("a_bp", [1, D])
        one = sb("a_one", [1, P])
        left = sb("a_left", [P, RING, HEADS, SEQ], BF16)
        right = sb("a_right", [P, RING, HEADS, SEQ], BF16)
        qs = sb("a_qs", [P, RING, NTS, HEADS, HW])
        nmax = sb("a_nmax", [P, NTS, HEADS])
        nrest = sb("a_nrest", [P, NTS, HEADS])
        npart = sb("a_npart", [P, NTS, P], BF16)
        nT = sb("a_nT", [P, RING, SEQ], BF16)
        ET = sb("a_ET", [P, 4, NTS, SEQ])
        OT = sb("a_OT", [P, 2, SEQ])
        rrec = sb("a_rrec", [P, QUADS, NTS, QUAD])
        y = sb("a_y", [P, NTS, D])
        yT = sb("a_yT", [P, KD, SEQ])
        pA = [pb(f"a_pA{i}", [P, NTS, SEQ]) for i in range(2)]
        pB = [pb(f"a_pB{i}", [P, NTS, SEQ]) for i in range(2)]
        pO = [pb(f"a_pO{i}", [P, SEQ]) for i in range(2)]
        pR = pb("a_pR", [P, NTS, P])
        pC = pb("a_pC", [P, KD, SEQ])
        pM = pC[:, 0, :].bitcast(BF16)[:, 0:SEQ]
        pH = pC[:, :, :].rearrange("p k t -> p (k t)").rearrange("p (n d) -> p n d", d=D)

        s_w = sem("a_weights_loaded")
        s_one = sem("a_constants_made")
        s_pk = [sem(f"a_packs{i}_loaded") for i in range(RING)]
        s_qs = sem("a_qs_ready")
        s_s = sem("a_scores_done")
        s_m = sem("a_max_ready")
        s_nr = sem("a_max_parts_ready")
        s_sp = sem("a_max_rest_ready")
        s_nt = sem("a_max_transposed")
        s_nte = sem("a_maxT_ready")
        s_b = sem("a_shifted_done")
        s_e = sem("a_exp_ready")
        s_o = sem("a_heads_done")
        s_ot = sem("a_quad_copied")
        s_r = sem("a_quad_transposed")
        s_rr = sem("a_sums_inverted")
        s_y = sem("a_y_ready")
        s_yt = sem("a_y_transposed")
        s_yte = sem("a_yT_ready")
        s_p = sem("a_projected")
        s_h = sem("a_h_added")

        block = ctx.enter_context(nc.Block())

        def sequences(eng, body):
            body(0, 0)
            with eng.Fori(0, (SEQS - 2) // RING) as l:
                for i in range(1, RING + 1):
                    body(i, l)
            body(SEQS - 1, 0)

        @block.sync
        def _(sp):
            sp.dma_start(wp[:, :, :], a["wp"].rearrange("(k p) n -> p k n", p=P)).then_inc(s_w, 16)
            sp.dma_start(bp[:, :], a["bp"].rearrange("(o n) -> o n", o=1)).then_inc(s_w, 16)
            for n in range(SEQS):
                if n >= RING:
                    sp.wait_ge(s_b, HEADS * (n - RING + 1))
                for side, parts in ((left, LEFT), (right, RIGHT)):
                    for b, part in enumerate(parts):
                        sp.dma_start(side[b * DH:(b + 1) * DH, n % RING, :, :],
                                     g["qparts"][part].rearrange("(h r) t -> r h t", r=DH)[:, :, n * SEQ:(n + 1) * SEQ])\
                            .then_inc(s_pk[n % RING], 16)

        @block.gpsimd
        def _(pool):
            pool.memset(one[:, :], 1.0).then_inc(s_one, 1)
            pool.memset(npart[:, :, :], 0.0).then_inc(s_one, 1)
            pool.memset(qs[:, :, :, :, DH:DH + 1], 1.0).then_inc(s_one, 1)
            pool.memset(qs[:, :, :, :, DH + 1:], 0.0).then_inc(s_one, 1)
            for n in range(SEQS):
                if n >= RING:
                    pool.wait_ge(s_o, HEADS * (n - RING + 1) + 4)
                for j in range(NTS):
                    last = pool.tensor_copy(qs[:, n % RING, j, :, 0:DH], qn[:, NTS * n + j, :, :])
                last.then_inc(s_qs, 1)

        @block.tensor
        def _(pe):
            pe.wait_ge(s_one, 4)
            pe.wait_ge(s_w, 32)

            def maxima(i, l, hd):
                slot, n = i % RING, HEADS * (RING * l + i) + hd
                if hd == 0:
                    pe.wait_ge(s_pk[slot], 16 * 16 * (l + i // RING + 1))
                if i or hd >= 2:
                    pe.wait_ge(s_m, n - 1)
                for nt in range(NTS):
                    last = pe.matmul(pA[hd % 2][:, nt, :], left[:, slot, hd, nt * P:(nt + 1) * P], right[:, slot, hd, :],
                                     start=True, stop=True)
                last.then_inc(s_s, 1)

            def maxima_transposed(i, l):
                pe.wait_ge(s_nr, 3 * (RING * l + i) + 3)
                if i >= 2:
                    pe.wait_ge(s_h, RING * l + i - 1)
                for nt in range(NTS):
                    last = pe.transpose(pM[:, nt * P:(nt + 1) * P], npart[:, nt, :], g["ident_b"][:, :])
                last.then_inc(s_nt, 1)

            def shifted(i, l, hd):
                slot, n = i % RING, HEADS * (RING * l + i) + hd
                if hd == 0:
                    pe.wait_ge(s_nte, RING * l + i + 1)
                pe.wait_ge(s_e, n + 1)
                for mt in range(NTS):
                    pe.matmul(pB[hd % 2][:, mt, :], left[:, slot, hd, mt * P:(mt + 1) * P], right[:, slot, hd, :],
                              start=True, stop=False)
                    last = pe.matmul(pB[hd % 2][:, mt, :], sel[:, hd, :], nT[:, slot, :], start=False, stop=True)
                last.then_inc(s_b, 1)

            def values(i, l, hd):
                n, slot, part = HEADS * (RING * l + i) + hd, i % RING, hd % QUAD
                if hd == 0:
                    pe.wait_ge(s_qs, RING * l + i + 1)
                if part == 0:
                    pe.wait_ge(s_ot, QUADS * (RING * l + i) + hd // QUAD + 1)
                pe.wait_ge(s_e, n + 3)
                for mt in range(NTS):
                    last = pe.matmul(pO[hd // QUAD % 2][part * HW:(part + 1) * HW, :], qs[:, slot, mt, hd, :],
                                     ET[:, hd % 4, mt, :], start=(mt == 0), stop=(mt == NTS - 1))
                last.then_inc(s_o, 1)

            def quad_transposed(i, l, k):
                n = QUADS * (RING * l + i) + k
                pe.wait_ge(s_ot, n + 3)
                pe.wait_ge(s_y, n + 1)
                for nt in range(NTS):
                    last = pe.transpose(pR[:, nt, :], OT[:, k % 2, nt * P:(nt + 1) * P], ident[:, :])
                last.then_inc(s_r, 1)

            def y_transposed(i, l):
                pe.wait_ge(s_y, QUADS * (RING * l + i + 1) + 1)
                pe.wait_ge(s_nte, min(i + 2, SEQS) if isinstance(l, int) else RING * l + i + 2)
                for nt in range(NTS):
                    for k in range(KD):
                        last = pe.transpose(pC[:, k, nt * P:(nt + 1) * P], y[:, nt, k * P:(k + 1) * P], ident[:, :])
                last.then_inc(s_yt, 1)

            def project(i, l):
                pe.wait_ge(s_yte, RING * l + i + 1)
                for nt in range(NTS):
                    for k in range(KD):
                        pe.matmul(pH[:, nt, :], yT[:, k, nt * P:(nt + 1) * P], wp[:, k, :], start=(k == 0), stop=False)
                    last = pe.matmul(pH[:, nt, :], one[:, :], bp[:, :], start=False, stop=True)
                last.then_inc(s_p, 1)

            def body(i, l):
                for hd in range(HEADS):
                    if i < SEQS - 1 and hd < HEADS - 1:
                        if hd == 0:
                            maxima(i + 1, l, 0)
                        maxima(i + 1, l, hd + 1)
                    shifted(i, l, hd)
                    if hd:
                        values(i, l, hd - 1)
                    elif i:
                        values(i - 1, l, HEADS - 1)
                    if hd in (6, 10, 14):
                        quad_transposed(i, l, hd // QUAD - 1)
                    if i and hd == 2:
                        quad_transposed(i - 1, l, QUADS - 1)
                    if i and hd == 5:
                        y_transposed(i - 1, l)
                    if i and hd == 8:
                        project(i - 1, l)
                if i < SEQS - 1:
                    maxima_transposed(i + 1, l)

            for hd in range(HEADS):
                maxima(0, 0, hd)
            maxima_transposed(0, 0)
            sequences(pe, body)
            values(SEQS - 1, 0, HEADS - 1)
            quad_transposed(SEQS - 1, 0, QUADS - 1)
            y_transposed(SEQS - 1, 0)
            project(SEQS - 1, 0)

        @block.scalar
        def _(act):
            for i in range(2):
                act.sem_inc(s_e, 1)
                act.sem_inc(s_ot, 1)

            def maxima_copied(i, l):
                act.wait_ge(s_nt, RING * l + i + 1)
                act.activation(nT[:, i % RING, :], pM, ACT.Copy).then_inc(s_nte, 1)

            def quad_copied(i, l, k):
                n = QUADS * (RING * l + i) + k
                act.wait_ge(s_o, QUAD * (n + 1) + 4)
                act.wait_ge(s_r, n + 1)
                act.activation(OT[:, k % 2, :], pO[k % 2][:, :], ACT.Copy).then_inc(s_ot, 1)

            def y_copied(i, l):
                act.wait_ge(s_yt, RING * l + i + 1)
                act.activation(yT[:, :, :], pC[:, :, :], ACT.Copy).then_inc(s_yte, 1)

            def body(i, l):
                for hd in range(HEADS):
                    n = HEADS * (RING * l + i) + hd
                    act.wait_ge(s_b, n + 1)
                    act.wait_ge(s_o, n + 1)
                    act.activation(ET[:, hd % 4, :, :], pB[hd % 2][:, :, :], ACT.Exp, scale=4.0).then_inc(s_e, 1)
                    if hd in (5, 9, 13):
                        quad_copied(i, l, hd // QUAD - 1)
                    if i and hd == 1:
                        quad_copied(i - 1, l, QUADS - 1)
                    if i and hd == 6:
                        y_copied(i - 1, l)
                if i < SEQS - 1:
                    maxima_copied(i + 1, l)

            maxima_copied(0, 0)
            sequences(act, body)
            quad_copied(SEQS - 1, 0, QUADS - 1)
            y_copied(SEQS - 1, 0)

        @block.vector
        def _(dve):
            def maximum(i, l, hd):
                dve.wait_ge(s_s, HEADS * (RING * l + i) + hd + 1)
                dve.tensor_reduce(nmax[:, :, hd], pA[hd % 2][:, :, :], AX.X, ALU.max, negate=True).then_inc(s_m, 1)

            def split(i, l):
                n = RING * l + i
                dve.wait_ge(s_m, HEADS * (n + 1))
                if i:
                    dve.wait_ge(s_nt, n)
                dve.tensor_copy(npart[:, :, 0:HEADS], nmax[:, :, :]).then_inc(s_nr, 1)
                dve.wait_ge(s_nr, 3 * n + 1)
                dve.tensor_tensor(nrest[:, :, :], nmax[:, :, :], npart[:, :, 0:HEADS], ALU.subtract).then_inc(s_sp, 1)
                dve.wait_ge(s_sp, n + 1)
                dve.tensor_copy(npart[:, :, HEADS:2 * HEADS], nrest[:, :, :]).then_inc(s_nr, 1)
                dve.wait_ge(s_nr, 3 * n + 2)
                dve.tensor_tensor(npart[:, :, 2 * HEADS:SPLIT * HEADS], nrest[:, :, :], npart[:, :, HEADS:2 * HEADS], ALU.subtract)\
                    .then_inc(s_nr, 1)

            def divide(i, l, k):
                n = QUADS * (RING * l + i) + k
                quad = pR[:, :, :].rearrange("p t (g c) -> p t g c", c=HW)
                dve.wait_ge(s_r, n + 3)
                dve.reciprocal(rrec[:, k, :, :], quad[:, :, :, DH]).then_inc(s_rr, 1)
                dve.wait_ge(s_rr, n + 1)
                if k == 0 and i:
                    dve.wait_ge(s_yt, RING * l + i)
                dve.tensor_tensor(y[:, :, k * QUAD * DH:(k + 1) * QUAD * DH].rearrange("p t (g d) -> p t g d", d=DH),
                                  quad[:, :, :, 0:DH], rrec[:, k, :, :].unsqueeze(3).to_broadcast([P, NTS, QUAD, DH]), ALU.mult)\
                    .then_inc(s_y, 1)

            def add(i, l):
                n = RING * l + i
                dve.wait_ge(s_p, n + 1)
                rows = h[:, NTS * i:NTS * (i + 1), :] if isinstance(l, int) else h[:, bass.ds(NTS * n, NTS), :]
                dve.tensor_tensor(rows, rows, pH[:, :, :], ALU.add).then_inc(s_h, 1)

            def body(i, l):
                for hd in range(HEADS):
                    if i < SEQS - 1 and hd < HEADS - 1:
                        if hd == 0:
                            maximum(i + 1, l, 0)
                        maximum(i + 1, l, hd + 1)
                        if hd == HEADS - 2:
                            split(i + 1, l)
                    if hd in (7, 11, 15):
                        divide(i, l, hd // QUAD - 1)
                    if i and hd == 3:
                        divide(i - 1, l, QUADS - 1)
                    if i and hd == 9:
                        add(i - 1, l)

            dve.wait_ge(s_one, 4)
            dve.sem_inc(s_y, 1)
            for i in range(2):
                dve.sem_inc(s_r, 1)
            for i in range(4):
                dve.sem_inc(s_o, 1)
            for hd in range(HEADS):
                maximum(0, 0, hd)
            split(0, 0)
            sequences(dve, body)
            divide(SEQS - 1, 0, QUADS - 1)
            add(SEQS - 1, 0)
            dve.wait_ge(s_h, SEQS)


NEXP = 64
TOPK = 8
CAP = 256
NG = 8
TG = 4
EPG = NEXP // NG
ROUTE_SCALE = 2.5
SLOTS = NEXP * CAP
ST = SLOTS // P
SPE = CAP // P
KS = 2
HID = 128


def router_phase(nc, ctx0, g, a):
    ctx = ExitStack()
    with ctx:
        def sb(name, shape, dt=F32):
            return ctx.enter_context(nc.sbuf_tensor(name, shape, dt))

        def pb(name, shape, dt=F32):
            return ctx.enter_context(nc.psum_tensor(name, shape, dt))

        def sem(name):
            return ctx.enter_context(nc.semaphore(name))

        ident, h, idx, wk = g["ident"], g["h"], g["idx"], g["wk"]
        gate = sb("m_gate", [P, KD, NEXP])
        sgate = sb("m_sgate", [P, KD, KS * P])
        sup = sb("m_sup", [P, KD, KS * P])
        sdown = sb("m_sdown", [P, KS, D])
        ebias = sb("m_ebias", [P, NEXP])
        hc = sb("m_hc", [P, TPC, D])
        stats = sb("m_stats", [P, TPC, 6])
        mv = sb("m_mv", [P, TPC, 2])
        veps = sb("m_veps", [P, TPC])
        rstd = sb("m_rstd", [P, TPC])
        mhalf = sb("m_mhalf", [P, TPC])
        xn = sb("m_xn", [P, TPC, D])
        xT = sb("m_xT", [P, KD, CH])
        ones_b = sb("m_ones_b", [P, P], BF16)
        before = sb("m_before", [P, P], BF16)
        lower = sb("m_lower", [P, NG, NG])
        first_i = sb("m_first_i", [P, NEXP], I32)
        first = sb("m_first", [P, NEXP])
        tok_i = sb("m_tok_i", [P, NT], I32)
        tok = sb("m_tok", [P, NT])
        zeros = sb("m_zeros", [P, ST])
        score = sb("m_score", [P, TPC, NEXP])
        sfc = sb("m_sfc", [P, TPC, NEXP])
        top2 = sb("m_top2", [P, TPC * NG, 8])
        gs = sb("m_gs", [P, TPC, NG])
        gt = sb("m_gt", [P, TPC, NG * NG])
        eq = sb("m_eq", [P, TPC, NG * NG])
        eql = sb("m_eql", [P, TPC, NG * NG])
        rank = sb("m_rank", [P, TPC * NG])
        keep = sb("m_keep", [P, TPC * NG])
        kept = sb("m_kept", [P, TPC, NEXP])
        cand = sb("m_cand", [P, TPC, NEXP])
        v8 = sb("m_v8", [P, TPC, 8])
        rest = sb("m_rest", [P, TPC, NEXP])
        M = sb("m_M", [P, TPC, NEXP])
        Mb = sb("m_Mb", [P, TPC, NEXP], BF16)
        w = sb("m_w", [P, TPC, NEXP])
        wsum = sb("m_wsum", [P, TPC])
        wsum2 = sb("m_wsum2", [P, TPC])
        wrec = sb("m_wrec", [P, TPC])
        wfull = sb("m_wfull", [P, TPC, NEXP])
        valid = sb("m_valid", [P, TPC, NEXP])
        slot = sb("m_slot", [P, TPC, NEXP])
        slot1 = sb("m_slot1", [P, TPC, NEXP])
        wv = sb("m_wv", [P, TPC, NEXP])
        s8 = sb("m_s8", [P, TPC, TOPK])
        wkc = sb("m_wkc", [P, TPC, TOPK])
        junk = sb("m_junk", [P, TPC * TOPK, NEXP])
        mch = sb("m_mch", [P, NEXP])
        cum = [sb("m_cum", [P, NEXP]), sb("m_cumb", [P, NEXP], BF16)]
        sg = sb("m_sg", [P, KS, CH])
        sgg = sb("m_sgg", [P, KS, CH])
        hid = sb("m_hid", [P, KS, CH])
        pR = [pb(f"m_pR{i}", [P, CH]) for i in range(KD)]
        pG = pb("m_pG", [P, TPC, NEXP])
        pP = pb("m_pP", [P, TPC, NEXP])
        pA = [pb(f"m_pA{i}", [P, CH]) for i in range(2 * KS)]

        s_w = sem("m_weights_loaded")
        s_z = sem("m_zeros_made")
        s_zd = sem("m_list_zeroed")
        s_c = sem("m_constants_made")
        s_cc = sem("m_constants_cast")
        s_dve = sem("m_dve_steps")
        s_ve = sem("m_veps_ready")
        s_rs = sem("m_rstd_ready")
        s_xn = sem("m_xn_ready")
        s_xd = sem("m_rows_stored")
        s_r = sem("m_xn_transposed")
        s_x = sem("m_xT_ready")
        s_l = sem("m_logits_done")
        s_sc = sem("m_scores_ready")
        s_m = sem("m_mask_ready")
        s_p = sem("m_ranks_done")
        s_ix = sem("m_slots_ready")
        s_sl = sem("m_list_written")
        s_a = sem("m_shared_done")
        s_sg = sem("m_sigmoid_ready")
        s_hd = sem("m_hidden_ready")
        s_d = sem("m_down_done")
        s_h = sem("m_h_added")

        block = ctx.enter_context(nc.Block())

        @block.sync
        def _(sp):
            sp.dma_start(gate[:, :, :], a["gate"].rearrange("(k p) n -> p k n", p=P)).then_inc(s_w, 16)
            sp.dma_start(sgate[:, :, :], a["sgate"].rearrange("(k p) n -> p k n", p=P)).then_inc(s_w, 16)
            sp.dma_start(sup[:, :, :], a["sup"].rearrange("(k p) n -> p k n", p=P)).then_inc(s_w, 16)
            sp.dma_start(sdown[:, :, :], a["sdown"].rearrange("(k p) n -> p k n", p=P)).then_inc(s_w, 16)
            sp.dma_start(ebias[:, :], a["ebias"].rearrange("(o n) -> o n", o=1).to_broadcast([P, NEXP])).then_inc(s_w, 16)
            sp.wait_ge(s_z, 1)
            sp.dma_start(g["slots"].rearrange("(s p) o -> s (p o)", p=P), zeros[:, :]).then_inc(s_zd, 16)
            sp.sem_inc(s_xd, 16)
            with sp.Fori(0, NC) as l:
                sp.wait_ge(s_xn, l + 1)
                sp.dma_start(g["xrows"][bass.ds(l * CH, CH), :].rearrange("(j p) d -> p j d", p=P), xn[:, :, :]).then_inc(s_xd, 16)
            sp.wait_ge(s_xd, 16 * NC + 16)
            sp.wait_ge(s_zd, 16)

        @block.gpsimd
        def _(pool):
            pool.memset(zeros[:, :], 0.0).then_inc(s_z, 1)
            pool.memset(mhalf[:, :], -0.5).then_inc(s_c, 1)
            pool.memset(ones_b[:, :], 1.0).then_inc(s_c, 1)
            pool.memset(before[:, :], 1.0).then_inc(s_c, 1)
            pool.memset(lower[:, :, :], 1.0).then_inc(s_c, 1)
            pool.wait_ge(s_c, 4)
            pool.affine_select(out=before[:, :], in_=before[:, :], compare_op=ALU.is_gt, fill=0.0, base=0,
                               pattern=[[1, P]], channel_multiplier=-1).then_inc(s_c, 1)
            pool.affine_select(out=lower[:, :, :], in_=lower[:, :, :], compare_op=ALU.is_gt, fill=0.0, base=0,
                               pattern=[[1, NG], [-1, NG]], channel_multiplier=0).then_inc(s_c, 1)
            pool.iota(first_i[:, :], [[CAP, NEXP]], base=1, channel_multiplier=0).then_inc(s_c, 1)
            pool.iota(tok_i[:, :], [[P, NT]], base=0, channel_multiplier=1).then_inc(s_c, 1)
            pool.wait_ge(s_zd, 16)
            pool.wait_ge(s_cc, 2)
            for c in range(NC):
                pool.wait_ge(s_ve, c + 1)
                pool.tensor_tensor(rstd[:, :], veps[:, :], mhalf[:, :], ALU.pow).then_inc(s_rs, 1)
                pool.wait_ge(s_ix, c + 1)
                for t in range(c * TPC, (c + 1) * TPC):
                    for k in range(TOPK):
                        pool.indirect_dma_start(
                            g["slots"][:, :], bass.IndirectOffsetOnAxis(ap=idx[:, t, k:k + 1].bitcast(U32), axis=0),
                            tok[:, t:t + 1], None, bounds_check=SLOTS - 1, oob_is_err=False).then_inc(s_sl, 16)
            pool.wait_ge(s_sl, 16 * NT * TOPK)

        @block.tensor
        def _(pe):
            pe.wait_ge(s_c, 8)
            pe.wait_ge(s_w, 80)
            with pe.Fori(0, NC) as l:
                pe.wait_ge(s_xn, l + 1)
                pe.wait_ge(s_h, l + 1)
                to_columns(pe, pR, xn, ident).then_inc(s_r, 1)
                pe.wait_ge(s_x, l + 1)
                for j in range(TPC):
                    for k in range(KD):
                        last = pe.matmul(pG[:, j, :], xT[:, k, j * P:(j + 1) * P], gate[:, k, :], start=(k == 0), stop=(k == KD - 1))
                last.then_inc(s_l, 1)
                for f in range(KS):
                    for i, wt in enumerate((sgate, sup)):
                        for k in range(KD):
                            last = pe.matmul(pA[2 * f + i][:, :], wt[:, k, f * P:(f + 1) * P], xT[:, k, :],
                                             start=(k == 0), stop=(k == KD - 1))
                    last.then_inc(s_a, 1)
                pe.wait_ge(s_m, l + 1)
                for j in range(TPC):
                    pe.matmul(pP[:, j, :], before[:, :], Mb[:, j, :], start=True, stop=False)
                    for i in range(j):
                        pe.matmul(pP[:, j, :], ones_b[:, :], Mb[:, i, :], start=False, stop=False)
                    last = pe.matmul(pP[:, j, :], ones_b[:, :], cum[1][:, :], start=False, stop=True)
                last.then_inc(s_p, 1)
                pe.wait_ge(s_hd, l + 1)
                for j in range(TPC):
                    for f in range(KS):
                        last = pe.matmul(pR[j // 2][:, j % 2 * D:(j % 2 + 1) * D], hid[:, f, j * P:(j + 1) * P], sdown[:, f, :],
                                         start=(f == 0), stop=(f == KS - 1))
                last.then_inc(s_d, 1)

        @block.scalar
        def _(act):
            with act.Fori(0, NC) as l:
                act.wait_ge(s_r, l + 1)
                for k in range(KD):
                    last = act.activation(xT[:, k, :], pR[k][:, :], ACT.Copy)
                last.then_inc(s_x, 1)
                act.wait_ge(s_l, l + 1)
                act.activation(score[:, :, :], pG[:, :, :], ACT.Sigmoid).then_inc(s_sc, 1)
                for f in range(KS):
                    act.wait_ge(s_a, KS * l + f + 1)
                    act.activation(sg[:, f, :], pA[2 * f][:, :], ACT.Sigmoid).then_inc(s_sg, 1)

        @block.vector
        def _(dve):
            dve.wait_ge(s_c, 8)
            dve.tensor_copy(first[:, :], first_i[:, :]).then_inc(s_cc, 1)
            dve.tensor_copy(tok[:, :], tok_i[:, :]).then_inc(s_cc, 1)
            dve.memset(cum[0][:, :], 0.0).then_inc(s_cc, 1)
            dve.memset(cum[1][:, :], 0.0).then_inc(s_cc, 1)
            dve.wait_ge(s_cc, 4)
            dve.wait_ge(s_w, 80)
            dve.sem_inc(s_h, 1)
            with dve.Fori(0, NC) as l:
                LINKS = 26
                chain = Chain(dve, s_dve, LINKS * l)
                link = chain.link
                link(dve.tensor_copy(hc[:, :, :], h[:, bass.ds(l * TPC, TPC), :]))
                dve.wait_ge(s_xd, 16 * l + 16)
                normalise(dve, chain, hc, stats, mv, veps, 1e-5, s_ve, s_rs, l + 1, rstd, xn, g["carrier"]).then_inc(s_xn, 1)
                dve.wait_ge(s_sc, l + 1)
                link(dve.tensor_tensor(sfc[:, :, :], score[:, :, :],
                                       ebias[:, :].unsqueeze(1).to_broadcast([P, TPC, NEXP]), ALU.add))
                by_group = sfc[:, :, :].rearrange("p t (g e) -> p (t g) e", g=NG)
                dve.memset(g["carrier"][:, :], 0.0)
                for i in range(TPC * NG):
                    last = dve.max(top2[:, i, :], by_group[:, i, :])
                link(last)
                link(dve.tensor_tensor(gs[:, :, :].rearrange("p t g -> p (t g)"), top2[:, :, 0], top2[:, :, 1], ALU.add))
                other = gs[:, :, :].unsqueeze(2).to_broadcast([P, TPC, NG, NG])
                own = gs[:, :, :].unsqueeze(3).to_broadcast([P, TPC, NG, NG])
                sq4 = "p t (g o) -> p t g o"
                dve.tensor_tensor(gt[:, :, :].rearrange(sq4, g=NG), other, own, ALU.is_gt)
                link(dve.tensor_tensor(eq[:, :, :].rearrange(sq4, g=NG), other, own, ALU.is_equal))
                low = lower[:, :, :].rearrange("p g o -> p (g o)").unsqueeze(1).to_broadcast([P, TPC, NG * NG])
                link(dve.tensor_tensor(eql[:, :, :], eq[:, :, :], low, ALU.mult))
                link(dve.tensor_tensor(gt[:, :, :], gt[:, :, :], eql[:, :, :], ALU.add))
                link(dve.tensor_reduce(rank[:, :], gt[:, :, :].rearrange("p t (g o) -> p (t g) o", o=NG), AX.X, ALU.add))
                link(dve.tensor_scalar(keep[:, :], rank[:, :], TG - 0.5, None, ALU.is_lt))
                link(dve.tensor_tensor(kept[:, :, :].rearrange("p t (g e) -> p (t g) e", g=NG), by_group,
                                       keep[:, :].unsqueeze(2).to_broadcast([P, TPC * NG, EPG]), ALU.mult))
                link(dve.tensor_scalar(cand[:, :, :], kept[:, :, :], 0.0, None, ALU.add))
                dve.memset(g["carrier"][:, :], 0.0)
                for j in range(TPC):
                    last = dve.max(v8[:, j, :], cand[:, j, :])
                link(last)
                dve.memset(g["carrier"][:, :], 0.0)
                for j in range(TPC):
                    last = dve.match_replace(rest[:, j, :], v8[:, j, :], cand[:, j, :], -3.0e38)
                link(last)
                link(dve.tensor_tensor(M[:, :, :], rest[:, :, :], cand[:, :, :], ALU.not_equal))
                dve.tensor_copy(Mb[:, :, :], M[:, :, :]).then_inc(s_m, 1)
                link(dve.tensor_tensor(w[:, :, :], score[:, :, :], M[:, :, :], ALU.mult))
                link(dve.tensor_reduce(wsum[:, :], w[:, :, :], AX.X, ALU.add))
                link(dve.tensor_scalar(wsum2[:, :], wsum[:, :], 1e-20, 1.0 / ROUTE_SCALE, ALU.add, ALU.mult))
                link(dve.reciprocal(wrec[:, :], wsum2[:, :]))
                link(dve.tensor_tensor(wfull[:, :, :], w[:, :, :], wrec[:, :].unsqueeze(2).to_broadcast([P, TPC, NEXP]), ALU.mult))
                dve.wait_ge(s_p, l + 1)
                dve.tensor_tensor(slot[:, :, :], pP[:, :, :], first[:, :].unsqueeze(1).to_broadcast([P, TPC, NEXP]), ALU.add)
                link(dve.scalar_tensor_tensor(valid[:, :, :], pP[:, :, :], float(CAP), M[:, :, :], ALU.is_lt, ALU.mult))
                dve.tensor_tensor(wv[:, :, :], wfull[:, :, :], valid[:, :, :], ALU.mult)
                dve.tensor_reduce(mch[:, :], M[:, :, :].rearrange("p t e -> p e t"), AX.X, ALU.add)
                link(dve.tensor_tensor(slot1[:, :, :], slot[:, :, :], valid[:, :, :], ALU.mult))
                dve.memset(g["carrier"][:, :], 0.0)
                for j in range(TPC):
                    last = dve.max(s8[:, j, :], slot1[:, j, :])
                link(last)
                dve.tensor_scalar(idx[:, bass.ds(l * TPC, TPC), :], s8[:, :, :], -1.0, None, ALU.add).then_inc(s_ix, 1)
                dve.tensor_tensor(cum[0][:, :], cum[0][:, :], mch[:, :], ALU.add)
                for j in range(TPC):
                    for k in range(TOPK):
                        last = dve.scalar_tensor_tensor(junk[:, TOPK * j + k, :], slot1[:, j, :], s8[:, j, k:k + 1], wv[:, j, :],
                                                        ALU.is_equal, ALU.mult, accum_out=wkc[:, j, k:k + 1])
                link(last)
                dve.tensor_copy(wk[:, bass.ds(l * TPC, TPC), :], wkc[:, :, :])
                dve.tensor_copy(cum[1][:, :], cum[0][:, :])
                for f in range(KS):
                    dve.wait_ge(s_sg, KS * l + f + 1)
                    last = dve.tensor_tensor(sgg[:, f, :], sg[:, f, :], pA[2 * f][:, :], ALU.mult)
                link(last)
                for f in range(KS):
                    last = dve.tensor_tensor(hid[:, f, :], sgg[:, f, :], pA[2 * f + 1][:, :], ALU.mult)
                last.then_inc(s_hd, 1)
                dve.wait_ge(s_d, l + 1)
                for i in range(2):
                    last = dve.tensor_tensor(h[:, bass.ds(l * TPC + 2 * i, 2), :], hc[:, 2 * i:2 * i + 2, :],
                                             pR[i][:, :].rearrange("p (a b) -> p a b", a=2), ALU.add)
                last.then_inc(s_h, 1)
                dve.wait_ge(s_h, l + 2)
                assert chain.n == LINKS, chain.n


RINGX = 4


def expert_steps(eng, body):
    for s in range(2):
        body(s, 0)
    with eng.Fori(0, (NEXP - 4) // RINGX) as l:
        for s in range(2, 2 + RINGX):
            body(s, l)
    for s in range(NEXP - 2, NEXP + 2):
        body(s, 0)


def experts_phase(nc, ctx0, g, a):
    ctx = ExitStack()
    with ctx:
        def sb(name, shape, dt=F32):
            return ctx.enter_context(nc.sbuf_tensor(name, shape, dt))

        def pb(name, shape, dt=F32):
            return ctx.enter_context(nc.psum_tensor(name, shape, dt))

        def sem(name):
            return ctx.enter_context(nc.semaphore(name))

        ident = g["ident"]
        WCOL = 2 * KD * HID + D
        wt = sb("x_wt", [P, RINGX, WCOL])
        lst = sb("x_lst", [P, P])
        lstT = sb("x_lstT", [P, P], I32)
        rows = sb("x_rows", [P, RINGX, SPE, D])
        rowsT = sb("x_rowsT", [P, RINGX, KD * CAP])
        sg = sb("x_sg", [P, RINGX, CAP])
        sgg = sb("x_sgg", [P, RINGX, CAP])
        hid = sb("x_hid", [P, RINGX, CAP])
        ye = sb("x_ye", [P, RINGX, SPE, D])
        pX = [pb(f"x_pX{i}", [P, KD * CAP]) for i in range(2)]
        pU = [pb(f"x_pU{i}", [P, 2, CAP]) for i in range(2)]
        pY = [pb(f"x_pY{i}", [P, SPE, D]) for i in range(2)]

        s_wt = [sem(f"x_weights{i}_loaded") for i in range(RINGX)]
        s_ls = sem("x_list_loaded")
        s_lt = sem("x_list_transposed")
        s_li = sem("x_list_ready")
        s_rw = [sem(f"x_rows{i}_gathered") for i in range(RINGX)]
        s_t = sem("x_rows_transposed")
        s_xt = sem("x_rowsT_ready")
        s_u = sem("x_gate_up_done")
        s_sg = sem("x_sigmoid_ready")
        s_g1 = sem("x_silu_ready")
        s_hd = sem("x_hidden_ready")
        s_y = sem("x_down_done")
        s_ye = sem("x_ye_ready")
        s_yd = [sem(f"x_ye{i}_stored") for i in range(RINGX)]

        block = ctx.enter_context(nc.Block())

        @block.sync
        def _(sp):
            sp.dma_start(lst[:, :], g["slots"].rearrange("(s p) o -> s (p o)", p=P)).then_inc(s_ls, 16)
            for i in range(RINGX):
                sp.dma_start(wt[:, i, :], a["wexp"][i]).then_inc(s_wt[i], 16)
            with sp.Fori(1, NEXP // RINGX) as r:
                for i in range(RINGX):
                    sp.wait_ge(s_y, RINGX * r + i - RINGX + 1)
                    sp.dma_start(wt[:, i, :], a["wexp"][bass.ds(RINGX * r + i, 1), :, :].rearrange("e p n -> p (e n)")).then_inc(s_wt[i], 16)

        @block.gpsimd
        def _(pool):
            pool.wait_ge(s_li, 1)
            for e in range(NEXP):
                if e >= RINGX:
                    pool.wait_ge(s_t, e - RINGX + 1)
                for i in range(SPE):
                    pool.indirect_dma_start(
                        rows[:, e % RINGX, i, :], None, g["xrows"][:, :],
                        bass.IndirectOffsetOnAxis(ap=lstT[:, SPE * e + i:SPE * e + i + 1].bitcast(U32), axis=0),
                        bounds_check=T - 1, oob_is_err=False).then_inc(s_rw[e % RINGX], 16)

        @block.tensor
        def _(pe):
            pe.wait_ge(s_ls, 16)
            pe.transpose(pX[0][:, 0:P], lst[:, :], ident[:, :]).then_inc(s_lt, 1)
            pe.wait_ge(s_li, 1)

            def body(s, l):
                i0 = RINGX * l
                if s < NEXP:
                    pe.wait_ge(s_rw[s % RINGX], 16 * SPE * (l + s // RINGX + 1))
                    for i in range(SPE):
                        for k in range(KD):
                            last = pe.transpose(pX[s % 2][:, k * CAP + i * P:k * CAP + (i + 1) * P],
                                                rows[:, s % RINGX, i, k * P:(k + 1) * P], ident[:, :])
                    last.then_inc(s_t, 1)
                if 1 <= s <= NEXP:
                    e = s - 1
                    pe.wait_ge(s_wt[e % RINGX], 16 * (l + e // RINGX + 1))
                    pe.wait_ge(s_xt, i0 + e + 1)
                    for u in range(2):
                        for k in range(KD):
                            o = (u * KD + k) * HID
                            last = pe.matmul(pU[e % 2][:, u, :], wt[:, e % RINGX, o:o + HID],
                                             rowsT[:, e % RINGX, k * CAP:(k + 1) * CAP], start=(k == 0), stop=(k == KD - 1))
                    last.then_inc(s_u, 1)
                if 2 <= s:
                    e = s - 2
                    pe.wait_ge(s_hd, i0 + e + 1)
                    pe.wait_ge(s_ye, i0 + e + 1)
                    for i in range(SPE):
                        last = pe.matmul(pY[e % 2][:, i, :], hid[:, e % RINGX, i * P:(i + 1) * P],
                                         wt[:, e % RINGX, 2 * KD * HID:], start=True, stop=True)
                    last.then_inc(s_y, 1)

            expert_steps(pe, body)

        @block.scalar
        def _(act):
            def body(s, l):
                i0 = RINGX * l
                if s < NEXP:
                    act.wait_ge(s_t, i0 + s + 1)
                    act.activation(rowsT[:, s % RINGX, :], pX[s % 2][:, :], ACT.Copy).then_inc(s_xt, 1)
                if 1 <= s <= NEXP:
                    e = s - 1
                    act.wait_ge(s_u, i0 + e + 1)
                    act.activation(sg[:, e % RINGX, :], pU[e % 2][:, 0, :], ACT.Sigmoid).then_inc(s_sg, 1)
                if 2 <= s:
                    e = s - 2
                    act.wait_ge(s_y, i0 + e + 1)
                    act.wait_ge(s_yd[e % RINGX], 16 * (l + e // RINGX + 1))
                    act.activation(ye[:, e % RINGX, :, :], pY[e % 2][:, :, :], ACT.Copy).then_inc(s_ye, 1)
                    act.wait_ge(s_ye, i0 + e + 3)
                    act.dma_start(g["yrows"][bass.ds((i0 + e) * CAP, CAP), :].rearrange("(i p) d -> p i d", p=P),
                                  ye[:, e % RINGX, :, :]).then_inc(s_yd[e % RINGX], 16)

            for i in range(RINGX):
                act.sem_inc(s_yd[i], 16)
            for i in range(2):
                act.sem_inc(s_ye, 1)
            expert_steps(act, body)
            for i in range(RINGX):
                act.wait_ge(s_yd[i], 16 * NEXP // RINGX + 16)

        @block.vector
        def _(dve):
            dve.wait_ge(s_lt, 1)
            dve.tensor_copy(lstT[:, :], pX[0][:, 0:P]).then_inc(s_li, 1)

            def body(s, l):
                if 1 <= s <= NEXP:
                    e = s - 1
                    n = RINGX * l + e + 1
                    dve.wait_ge(s_sg, n)
                    dve.tensor_tensor(sgg[:, e % RINGX, :], sg[:, e % RINGX, :], pU[e % 2][:, 0, :], ALU.mult).then_inc(s_g1, 1)
                    dve.wait_ge(s_g1, n)
                    dve.tensor_tensor(hid[:, e % RINGX, :], sgg[:, e % RINGX, :], pU[e % 2][:, 1, :], ALU.mult).then_inc(s_hd, 1)

            expert_steps(dve, body)


def combine_phase(nc, ctx0, g, a, out):
    ctx = ExitStack()
    with ctx:
        def sem(name):
            return ctx.enter_context(nc.semaphore(name))

        h, idx, wk = g["h"], g["idx"], g["wk"]
        yg = ctx.enter_context(nc.sbuf_tensor("c_yg", [P, 2, TOPK, D], F32))
        s_z = sem("c_zeroed")
        s_g = [sem(f"c_rows{i}_gathered") for i in range(2)]
        s_a = sem("c_rows_added")
        s_o = sem("c_out_stored")
        block = ctx.enter_context(nc.Block())

        @block.gpsimd
        def _(pool):
            pool.wait_ge(s_z, 1)
            for t in range(NT):
                if t >= 2:
                    pool.wait_ge(s_a, TOPK * (t - 1))
                for k in range(TOPK):
                    pool.indirect_dma_start(
                        yg[:, t % 2, k, :], None, g["yrows"][:, :],
                        bass.IndirectOffsetOnAxis(ap=idx[:, t, k:k + 1].bitcast(U32), axis=0),
                        bounds_check=SLOTS - 1, oob_is_err=False).then_inc(s_g[t % 2], 16)

        @block.vector
        def _(dve):
            dve.memset(yg[:, :, :, :], 0.0).then_inc(s_z, 1)
            for t in range(NT):
                dve.wait_ge(s_g[t % 2], 16 * TOPK * (t // 2 + 1))
                for k in range(TOPK):
                    dve.scalar_tensor_tensor(h[:, t, :], yg[:, t % 2, k, :], wk[:, t, k:k + 1], h[:, t, :],
                                             ALU.mult, ALU.add).then_inc(s_a, 1)
                    dve.wait_ge(s_a, TOPK * t + k + 1)

        @block.sync
        def _(sp):
            for t in range(NT):
                sp.wait_ge(s_a, TOPK * (t + 1))
                sp.dma_start(out[t * P:(t + 1) * P, :], h[:, t, :]).then_inc(s_o, 16)
            sp.wait_ge(s_o, 16 * NT)


def build(nc, a, out):
    ctx = ExitStack()
    with ctx:
        g = {}
        g["ident"] = ctx.enter_context(nc.sbuf_tensor("ident", [P, P], F32))
        g["ones"] = ctx.enter_context(nc.sbuf_tensor("ones", [P, P], F32))
        g["h"] = ctx.enter_context(nc.sbuf_tensor("h", [P, NT, D], F32))
        g["XT"] = ctx.enter_context(nc.sbuf_tensor("XT", [P, KD, T], F32))
        g["prob"] = ctx.enter_context(nc.sbuf_tensor("prob", [P, NT, EXPERTS0], F32))
        g["routed"] = ctx.enter_context(nc.sbuf_tensor("routed", [P, 1], I32))
        g["ident_b"] = ctx.enter_context(nc.sbuf_tensor("ident_b", [P, P], BF16))
        g["qn"] = ctx.enter_context(nc.sbuf_tensor("qn", [P, NT, HEADS, DH], F32))
        g["sel"] = ctx.enter_context(nc.sbuf_tensor("sel", [P, HEADS, P], BF16))
        g["qparts"] = nc.dram_tensor("qparts", (SPLIT, D, T), BF16, kind="Internal").ap()
        g["idx"] = ctx.enter_context(nc.sbuf_tensor("idx", [P, NT, TOPK], I32))
        g["wk"] = ctx.enter_context(nc.sbuf_tensor("wk", [P, NT, TOPK], F32))
        g["xrows"] = nc.dram_tensor("xrows", (T, D), F32, kind="Internal").ap()
        g["slots"] = nc.dram_tensor("slots", (SLOTS, 1), F32, kind="Internal").ap()
        g["yrows"] = nc.dram_tensor("yrows", (SLOTS, D), F32, kind="Internal").ap()
        g["carrier"] = ctx.enter_context(nc.sbuf_tensor("carrier", [P, 1], F32))
        g["junk"] = ctx.enter_context(nc.sbuf_tensor("junk", [P, 4, SEQ], F32))
        embed_phase(nc, ctx, g, a)
        blocks_phase(nc, ctx, g, a)
        shared0_phase(nc, ctx, g, a)
        routed0_phase(nc, ctx, g, a)
        queries_phase(nc, ctx, g, a)
        attention_phase(nc, ctx, g, a)
        router_phase(nc, ctx, g, a)
        experts_phase(nc, ctx, g, a)
        combine_phase(nc, ctx, g, a, out)



def kernel(**inputs):
    import concourse.bacc as bacc
    from concourse.bass_utils import run_bass_kernel_spmd

    i = {k: np.asarray(v) for k, v in inputs.items()}
    A = "L0_attn_"

    def cols(v):
        return v.reshape(BLOCKS, -1, P).transpose(0, 2, 1)

    w1, w3 = (i["L1_ffn_" + n].transpose(0, 2, 1).reshape(NEXP, KD, P, HID).transpose(0, 2, 1, 3).reshape(NEXP, P, KD * HID)
              for n in ("w1", "w3"))
    experts = np.concatenate([w1, w3, i["L1_ffn_w2"].transpose(0, 2, 1)], 2)

    arrays = {
        "x": i["x"].reshape(T),
        "head_rows": i["L0_tok_head_weight"].T[:CUTS[1]],
        "tail0_rows": i["L0_tok_tail_weight_0"].T,
        "tail1_rows": i["L0_tok_tail_weight_1"].T,
        "head_proj": i["L0_tok_head_weight_proj"].T,
        "tail0_proj": i["L0_tok_tail_weight_proj_0"].T,
        "tail1_proj": i["L0_tok_tail_weight_proj_1"].T,
        "wqkv": np.stack([i[A + "Wq"], i[A + "Wk"], i[A + "Wv"]], 1),
        "wo": i[A + "Wo"], "w1": i[A + "W1"], "w2": i[A + "W2"],
        "ws1": i["L0_ffn_Ws1"], "ws2": i["L0_ffn_Ws2"], "wr": i["L0_ffn_Wr"],
        "w1r": i["L0_ffn_W1"], "w2r": i["L0_ffn_W2"],
        "gate": i["L1_ffn_gate_weight"].T, "ebias": i["L1_ffn_e_bias"],
        "sgate": i["L1_ffn_shared_gate"].T, "sup": i["L1_ffn_shared_up"].T, "sdown": i["L1_ffn_shared_down"].T,
        "wexp": experts,
        "wq1": i["L1_attn_Wq"].transpose(0, 2, 1), "wp": i["L1_attn_Wp"].T, "bp": i["L1_attn_bp"],
        "vec": np.concatenate([cols(i[A + n]) for n in VEC], 2).transpose(1, 0, 2).reshape(P, BLOCKS * NVEC),
    }
    nc = bacc.Bacc("TRN2", target_bir_lowering=False, num_devices=1)
    arrays = {"in_" + k: np.ascontiguousarray(v) for k, v in arrays.items()}
    aps = {k[3:]: nc.dram_tensor(k, v.shape, mybir.dt.from_np(v.dtype), kind="ExternalInput").ap()
           for k, v in arrays.items()}
    out = nc.dram_tensor("out", (T, D), F32, kind="ExternalOutput").ap()
    build(nc, aps, out)
    r = run_bass_kernel_spmd(nc, [arrays], core_ids=[0])
    return r.results[0]["out"].reshape(8, 256, 256)
```

```python
import numpy as np
import concourse.bass as bass
from concourse import mybir
from contextlib import ExitStack

F32 = mybir.dt.float32
BF16 = mybir.dt.bfloat16
I32 = mybir.dt.int32
U32 = mybir.dt.uint32
ALU = mybir.AluOpType
ACT = mybir.ActivationFunctionType
AX = mybir.AxisListType

P = 128
T = 2048
D = 256
KD = D // P
NT = T // P
CH = 512
NC = T // CH
TPC = CH // P
SEQ = 256
CUTS = [0, 5000, 20000, 50000]
EMB = [256, 64, 16]
EOFF = [0, 256, 320]
EW = sum(EMB)
BLOCKS = 4
FF = 1024
KF = FF // P
VEC = {}
for _name, _n in (("bq", 2), ("bk", 2), ("bv", 2), ("bo", 2), ("b1", 8), ("b2", 2),
                  ("ln1_s", 2), ("ln1_b", 2), ("ln2_s", 2), ("ln2_b", 2)):
    VEC[_name] = sum(n for _, n in VEC.values()), _n
NVEC = sum(n for _, n in VEC.values())
SCALE_EMB = 16.0


class Chain:

    def __init__(self, eng, sem, base=0):
        self.eng, self.sem, self.base, self.n = eng, sem, base, 0

    def link(self, ins):
        self.n += 1
        ins.then_inc(self.sem, 1)
        self.eng.wait_ge(self.sem, self.base + self.n)


def make_identity(nc, ident, made, eng):
    eng.memset(ident[:, :], 0.0).then_inc(made, 1)
    eng.wait_ge(made, 1)
    eng.affine_select(out=ident[:, :], in_=ident[:, :], compare_op=ALU.not_equal, fill=1.0,
                      base=0, pattern=[[-1, P]], channel_multiplier=1).then_inc(made, 1)
    eng.wait_ge(made, 2)


def normalise(dve, chain, src, stats, mv, veps, eps, veps_ready, rstd_ready, rstd_count, rstd, dst, carrier):
    n = src.shape[1]
    for j in range(n):
        last = dve.bn_stats(stats[:, j, :], src[:, j, :])
    chain.link(last)
    dve.memset(carrier[:, :], 0.0)
    for j in range(n):
        last = dve.bn_aggr(mv[:, j, :], stats[:, j, :])
    chain.link(last)
    dve.tensor_scalar(veps[:, 0:n], mv[:, 0:n, 1], eps, None, ALU.add).then_inc(veps_ready, 1)
    dve.wait_ge(rstd_ready, rstd_count)
    for j in range(n):
        last = dve.tensor_scalar(dst[:, j, :], src[:, j, :], mv[:, j, 0:1], rstd[:, j:j + 1],
                                 ALU.subtract, ALU.mult)
    return last


def embed_phase(nc, ctx0, g, a):
    ctx = ExitStack()
    with nc.cleanup_on_exit(), ctx:
        def sb(name, shape, dt=F32):
            return ctx.enter_context(nc.sbuf_tensor(name, shape, dt))

        def pb(name, shape, dt=F32):
            return ctx.enter_context(nc.psum_tensor(name, shape, dt))

        def sem(name):
            return nc.alloc_semaphore(name)

        ids = sb("e_ids", [P, NT], I32)
        idx = sb("e_idx", [P, 3, NT], I32)
        rows = sb("e_rows", [P, NT, EW])
        proj = sb("e_proj", [P, 3, D])
        rowsT = sb("e_rowsT", [P, 2, 3, P])
        stats = sb("e_stats", [P, TPC, 6])
        mv = sb("e_mv", [P, TPC, 2])
        veps = sb("e_veps", [P, TPC])
        rstd = sb("e_rstd", [P, TPC])
        mhalf = sb("e_mhalf", [P, TPC])
        xn = sb("e_xn", [P, TPC, D])
        pT = [pb(f"e_pT{i}", [P, 512]) for i in range(2)]
        pY = [pb(f"e_pY{i}", [P, 512]) for i in range(2)]
        pX = [pb(f"e_pX{i}", [P, CH]) for i in range(KD)]

        s_ids = sem("e_ids_loaded")
        s_proj = sem("e_proj_loaded")
        s_zero = sem("e_rows_zeroed")
        s_idx = sem("e_idx_ready")
        s_id = sem("e_ident_made")
        s_g = [sem(f"e_gathered{c}") for c in range(NC)]
        s_t = sem("e_rows_transposed")
        s_tc = sem("e_rowsT_ready")
        s_y = sem("e_projected")
        s_h = sem("e_h_ready")
        s_ve = sem("e_veps_ready")
        s_rs = sem("e_rstd_ready")
        s_xn = sem("e_xn_ready")
        s_xt = sem("e_xn_transposed")
        s_xc = sem("e_xT_ready")
        s_dve = sem("e_dve_steps")
        s_mh = sem("e_mhalf_made")

        LATE = 2

        block = ctx.enter_context(nc.Block())
        ident, h, XT = g["ident"], g["h"], g["XT"]
        tables = [a["head_rows"], a["tail0_rows"], a["tail1_rows"]]

        @block.sync
        def _(sp):
            with nc.allow_non_contiguous_dma(reason="token ids, one per partition"):
                sp.dma_start(ids[:, :], a["x"].rearrange("(t p) -> p t", p=P)).then_inc(s_ids, 16)
            sp.dma_start(proj[:, 0:2, :], a["head_proj"].rearrange("(k p) n -> p k n", p=P)).then_inc(s_proj, 16)
            sp.dma_start(proj[0:EMB[1], 2, :], a["tail0_proj"]).then_inc(s_proj, 16)
            sp.dma_start(proj[EMB[1]:EMB[1] + EMB[2], 2, :], a["tail1_proj"]).then_inc(s_proj, 16)

        @block.gpsimd
        def _(pool):
            make_identity(nc, ident, s_id, pool)
            pool.memset(g["ones"][:, :], 1.0)
            pool.memset(mhalf[:, :], -0.5).then_inc(s_mh, 1)
            pool.wait_ge(s_idx, 1)
            pool.wait_ge(s_mh, 1)

            def norm(c):
                pool.wait_ge(s_ve, c + 1)
                pool.tensor_tensor(rstd[:, :], veps[:, :], mhalf[:, :], ALU.pow).then_inc(s_rs, 1)

            for c in range(NC):
                if c < 2:
                    pool.wait_ge(s_zero, c + 1)
                for t in range(c * TPC, (c + 1) * TPC):
                    for i in range(3):
                        pool.indirect_dma_start(
                            rows[:, t, EOFF[i]:EOFF[i] + EMB[i]], None, tables[i][:, :],
                            bass.IndirectOffsetOnAxis(ap=idx[:, i, t:t + 1].bitcast(U32), axis=0),
                            bounds_check=CUTS[i + 1] - CUTS[i] - 1, oob_is_err=False,
                        ).then_inc(s_g[c], 16)
                if c:
                    norm(c - 1)
            norm(NC - 1)

        @block.vector
        def _(dve):
            chain = Chain(dve, s_dve)
            dve.memset(rows[:, 0:TPC, :], 0.0).then_inc(s_zero, 1)
            dve.wait_ge(s_ids, 16)
            for i in range(3):
                last = dve.tensor_scalar(idx[:, i, :], ids[:, :], float(-CUTS[i]), None, ALU.add)
            last.then_inc(s_idx, 1)
            dve.memset(rows[:, TPC:, :], 0.0).then_inc(s_zero, 1)
            for c in range(NC):
                dve.wait_ge(s_h, TPC * (c + 1))
                if c:
                    dve.wait_ge(s_xt, c)
                hc = h[:, c * TPC:(c + 1) * TPC, :]
                normalise(dve, chain, hc, stats, mv, veps, 1e-5, s_ve, s_rs, c + 1, rstd, xn, g["carrier"]).then_inc(s_xn, 1)

        @block.tensor
        def _(pe):
            pe.wait_ge(s_id, 2)

            def rows_transposed(t):
                if t % TPC == 0:
                    pe.wait_ge(s_g[t // TPC], 16 * 3 * TPC)
                if t >= 2:
                    pe.wait_ge(s_tc, t - 1)
                for k in range(3):
                    w = P if k < 2 else EW - 2 * P
                    last = pe.transpose(pT[t % 2][0:w, k * P:(k + 1) * P], rows[:, t, k * P:k * P + w], ident[:, :])
                last.then_inc(s_t, 1)

            def xn_transposed(c):
                pe.wait_ge(s_xn, c + 1)
                if c:
                    pe.wait_ge(s_xc, c)
                to_columns(pe, pX, xn, ident).then_inc(s_xt, 1)

            rows_transposed(0)
            for t in range(NT):
                if t % TPC < TPC - 1:
                    rows_transposed(t + 1)
                if t == 0:
                    pe.wait_ge(s_proj, 48)
                pe.wait_ge(s_tc, t + 1)
                for k in range(3):
                    w = P if k < 2 else EW - 2 * P
                    last = pe.matmul(pY[t % 2][:, 0:D], rowsT[0:w, t % 2, k, :], proj[0:w, k, :],
                                     start=(k == 0), stop=(k == 2))
                last.then_inc(s_y, 1)
                if t % TPC == LATE and t > TPC:
                    xn_transposed(t // TPC - 1)
                if t % TPC == TPC - 1 and t + 1 < NT:
                    rows_transposed(t + 1)
            xn_transposed(NC - 1)

        @block.scalar
        def _(act):
            def xT_copied(c):
                act.wait_ge(s_xt, c + 1)
                for k in range(KD):
                    last = act.activation(XT[:, k, c * CH:(c + 1) * CH], pX[k][:, :], ACT.Copy)
                last.then_inc(s_xc, 1)

            def h_copied(t):
                act.wait_ge(s_y, t + 1)
                act.activation(h[:, t, :], pY[t % 2][:, 0:D], ACT.Copy, scale=SCALE_EMB).then_inc(s_h, 1)

            for t in range(NT):
                act.wait_ge(s_t, t + 1)
                if t >= 2:
                    act.wait_ge(s_y, t - 1)
                act.activation(rowsT[:, t % 2, 0:2, :], pT[t % 2][:, 0:2 * P].rearrange("p (k q) -> p k q", k=2), ACT.Copy)
                w = EW - 2 * P
                act.activation(rowsT[0:w, t % 2, 2, :], pT[t % 2][0:w, 2 * P:3 * P], ACT.Copy).then_inc(s_tc, 1)
                if t % TPC:
                    h_copied(t - 1)
                if t % TPC == TPC - 1:
                    if t > TPC:
                        xT_copied(t // TPC - 1)
                    h_copied(t)
            xT_copied(NC - 1)


def normaliser(dve, chain, last_stats, h, stats, mv, veps, eps, veps_ready, rstd_ready, rstd):
    chain.link(last_stats)
    for t in range(NT):
        last = dve.bn_aggr(mv[:, t, :], stats[:, t, :])
    chain.link(last)
    dve.tensor_scalar(veps[:, :], mv[:, :, 1], eps, None, ALU.add).then_inc(veps_ready, 1)
    dve.wait_ge(rstd_ready, 1)

    def rows_scaled(c, dst):
        for j in range(TPC):
            t = c * TPC + j
            last = dve.tensor_scalar(dst[:, j, :], h[:, t, :], mv[:, t, 0:1], rstd[:, t:t + 1], ALU.subtract, ALU.mult)
        return last

    return rows_scaled


ITEMS = BLOCKS * NC
RING = 4
PER_STEP = 3 * KD + KF + KD + KD
STEPS_BEFORE, LOOPS = 2, (ITEMS - 4) // NC


def products_before(s):
    return 0 if s == 0 else 4 * KD + PER_STEP * (s - 1)


def steps(eng, body):
    for s in range(STEPS_BEFORE):
        body(s, 0)
    with eng.Fori(0, LOOPS) as l:
        for s in range(STEPS_BEFORE, STEPS_BEFORE + NC):
            body(s, l)
    for s in range(STEPS_BEFORE + NC * LOOPS, ITEMS + 2):
        body(s, 0)


def blocks_phase(nc, ctx0, g, a):
    ctx = ExitStack()
    with nc.cleanup_on_exit(), ctx:
        def sb(name, shape, dt=F32):
            return ctx.enter_context(nc.sbuf_tensor(name, shape, dt))

        def pb(name, shape, dt=F32):
            return ctx.enter_context(nc.psum_tensor(name, shape, dt))

        def sem(name):
            return nc.alloc_semaphore(name)

        ident, XT = g["ident"], g["XT"]
        X1T = sb("b_X1T", [P, KD, T])
        wqkv = sb("b_wqkv", [P, 3, KD, D])
        wo = sb("b_wo", [P, KD, D])
        w1 = sb("b_w1", [P, KD, FF])
        w2 = sb("b_w2", [P, KF, D])
        vec = sb("b_vec", [P, BLOCKS * NVEC])
        cur = sb("b_cur", [P, NVEC])
        ncur = sb("b_ncur", [P, 2 * KD])
        nqk = sb("b_nqk", [P, 2, KD, CH])
        eqk = sb("b_eqk", [P, 2, KD, CH])
        em1 = sb("b_em1", [P, 2, KD, CH])
        rqk = sb("b_rqk", [P, 2, KD, CH])
        vv = sb("b_vv", [P, KD, CH])
        Q = sb("b_Q", [P, KD, CH])
        K = sb("b_K", [P, KD, CH])
        prod = sb("b_prod", [P, SEQ])
        ksum = sb("b_ksum", [P, 2 * KD])
        kv = sb("b_kv", [P, 2 * KD])
        den = sb("b_den", [P, KD, CH])
        rec = sb("b_rec", [P, KD, CH])
        mix = sb("b_mix", [P, KD, CH])
        a1 = sb("b_a1", [P, KD, CH])
        a2 = sb("b_a2", [P, KD, CH])
        H = sb("b_H", [P, KF, CH])
        ffo = sb("b_ffo", [P, KD, CH])
        s1 = sb("b_s1", [P, KD, CH])
        s2 = sb("b_s2", [P, KD, CH])
        xn = [sb(f"b_xn{i}", [P, TPC, D]) for i in range(2)]
        stats = sb("b_stats", [P, TPC, 6])
        mv = sb("b_mv", [P, TPC, 2])
        veps = sb("b_veps", [P, TPC])
        rstd = sb("b_rstd", [P, TPC])
        mhalf = sb("b_mhalf", [P, TPC])
        nil = sb("b_nil", [P, D])
        ring = [pb(f"b_ring{i}", [P, CH]) for i in range(RING)]
        pN = pb("b_pN", [P, TPC, D])
        pR = [pb(f"b_pR{i}", [P, CH]) for i in range(KD)]

        s_vec = sem("b_vec_loaded")
        s_wqkv = sem("b_wqkv_loaded")
        s_wo = sem("b_wo_loaded")
        s_w1 = sem("b_w1_loaded")
        s_w2 = sem("b_w2_loaded")
        s_full = sem("b_ring_full")
        s_free = sem("b_ring_free")
        s_qkv = sem("b_qkv_ready")
        s_mix = sem("b_mix_ready")
        s_a = sem("b_a_ready")
        s_a1 = sem("b_a1_ready")
        s_s1 = sem("b_s1_ready")
        s_s2 = sem("b_s2_ready")
        s_h = sem("b_h_ready")
        s_ff = sem("b_ffo_ready")
        s_n = sem("b_rows_natural")
        s_nf = sem("b_pN_free")
        s_ve = sem("b_veps_ready")
        s_rs = sem("b_rstd_ready")
        s_xn1 = sem("b_xn1_ready")
        s_xn2 = sem("b_xn2_ready")
        s_r1 = sem("b_ln1_returned")
        s_r2 = sem("b_ln2_returned")
        s_x1 = sem("b_x1_ready")
        s_x = sem("b_x_ready")
        s_dve = sem("b_dve_steps")
        s_mh = sem("b_mhalf_made")
        s_yz = sem("b_yrows_zeroed")
        s_cur = sem("b_columns_copied")

        block = ctx.enter_context(nc.Block())

        def ln1(s):
            return 1 <= s <= ITEMS

        def ln2(s):
            return 2 <= s <= ITEMS + 1

        def columns_by(s):
            return sum((x % NC == 0 and x < ITEMS) + (ln1(x) and x % NC == 1) + (ln2(x) and x % NC == 2)
                       for x in range(s + 1))

        def norms_before(s):
            return sum(ln1(x) + ln2(x) for x in range(s))

        @block.sync
        def _(sp):
            def load(b, wait):
                if wait:
                    sp.wait_ge(s_full, products_before(NC - 1) + 3 * KD + NC * PER_STEP * (b - 1))
                sp.dma_start(wqkv[:, :, :, :], a["wqkv"][bass.ds(b, 1), :, :, :].rearrange("b j (k p) n -> p (b j) k n", p=P)).then_inc(s_wqkv, 16)
                if wait:
                    sp.wait_ge(s_full, products_before(NC) + NC * PER_STEP * (b - 1))
                sp.dma_start(wo[:, :, :], a["wo"][bass.ds(b, 1), :, :].rearrange("b (k p) n -> p (b k) n", p=P)).then_inc(s_wo, 16)
                if wait:
                    sp.wait_ge(s_full, products_before(NC) + 3 * KD + KF + NC * PER_STEP * (b - 1))
                sp.dma_start(w1[:, :, :], a["w1"][bass.ds(b, 1), :, :].rearrange("b (k p) n -> p (b k) n", p=P)).then_inc(s_w1, 16)
                if wait:
                    sp.wait_ge(s_full, products_before(NC + 1) + NC * PER_STEP * (b - 1))
                sp.dma_start(w2[:, :, :], a["w2"][bass.ds(b, 1), :, :].rearrange("b (k p) n -> p (b k) n", p=P)).then_inc(s_w2, 16)

            sp.dma_start(vec[:, :], a["vec"]).then_inc(s_vec, 16)
            load(0, False)
            with sp.Fori(1, BLOCKS) as b:
                load(b, True)

        @block.tensor
        def _(pe):
            def body(s, l):
                r = [products_before(min(s, ITEMS))]
                if s > ITEMS:
                    r[0] += KF + KD
                at = NC * PER_STEP * l
                loaded = 16 * (l + s // NC + 1)
                loaded1 = 16 * (l + (s - 1) // NC + 1)

                def product(n_k, lhsT, rhs, ready=None):
                    bank = ring[r[0] % RING]
                    pe.wait_ge(s_free, at + r[0] + 1)
                    for k in range(n_k):
                        if ready:
                            ready(k)
                        last = pe.matmul(bank[:, :], lhsT(k), rhs(k), start=(k == 0), stop=(k == n_k - 1))
                    last.then_inc(s_full, 1)
                    r[0] += 1

                def qkv(j, tiles=range(KD)):
                    c = s % NC
                    for m in tiles:
                        product(KD, lambda k: wqkv[:, j, k, m * P:(m + 1) * P], lambda k: XT[:, k, c * CH:(c + 1) * CH])

                def to_rows(src, n):
                    if n:
                        pe.wait_ge(s_nf, 2 * NC * l + n)
                    for j in range(TPC):
                        for k in range(KD):
                            last = pe.transpose(pN[:, j, k * P:(k + 1) * P], src[:, k, j * P:(j + 1) * P], ident[:, :])
                    last.then_inc(s_n, 1)

                def to_columns(src, done):
                    for j in range(TPC):
                        for k in range(KD):
                            last = pe.transpose(pR[k][:, j * P:(j + 1) * P], src[:, j, k * P:(k + 1) * P], ident[:, :])
                    last.then_inc(done, 1)

                def w2_product(m, ready=None):
                    product(KF, lambda k: w2[:, k, m * P:(m + 1) * P], lambda k: H[:, k, :], ready)

                n = norms_before(s)
                if s < ITEMS:
                    if s % NC == 0:
                        pe.wait_ge(s_wqkv, loaded)
                    if s >= NC:
                        pe.wait_ge(s_x, NC * l + s - NC + 1)
                    qkv(0)
                if ln1(s):
                    pe.wait_ge(s_s1, NC * l + s)
                    to_rows(s1, n)
                    n += 1
                if s < ITEMS:
                    qkv(1)
                if s < ITEMS:
                    qkv(2, range(0, KD - 1))
                if ln1(s):
                    pe.wait_ge(s_xn1, NC * l + s)
                    if s >= 3:
                        pe.wait_ge(s_x, NC * l + s - 2)
                    to_columns(xn[0], s_r1)
                if s < ITEMS:
                    qkv(2, range(KD - 1, KD))
                if ln2(s):
                    pe.wait_ge(s_s2, NC * l + s - 1)
                    to_rows(s2, n)
                if ln1(s):
                    c = (s - 1) % NC
                    if c == 0:
                        pe.wait_ge(s_w1, loaded1)
                    pe.wait_ge(s_x1, NC * l + s)
                    for f in range(KF):
                        product(KD, lambda k: w1[:, k, f * P:(f + 1) * P], lambda k: X1T[:, k, c * CH:(c + 1) * CH])
                if ln2(s):
                    pe.wait_ge(s_xn2, NC * l + s - 1)
                    pe.wait_ge(s_x1, min(ITEMS, s) + NC * l)
                    to_columns(xn[1], s_r2)
                if ln1(s):
                    if (s - 1) % NC == 0:
                        pe.wait_ge(s_w2, loaded1)
                    w2_product(0, lambda k: pe.wait_ge(s_h, KF * (NC * l + s - 1) + k + 1))
                if s < ITEMS:
                    if s % NC == 0:
                        pe.wait_ge(s_wo, loaded)
                    pe.wait_ge(s_mix, NC * l + s + 1)
                    for m in range(KD):
                        product(KD, lambda k: wo[:, k, m * P:(m + 1) * P], lambda k: mix[:, k, :])
                if ln1(s):
                    w2_product(1)

            steps(pe, body)

        @block.scalar
        def _(act):
            act.wait_ge(s_vec, 16)
            for i in range(RING):
                act.sem_inc(s_free, 1)

            def body(s, l):
                r = [products_before(min(s, ITEMS))]
                if s > ITEMS:
                    r[0] += KF + KD
                at = NC * PER_STEP * l

                def col(name, m):
                    return cur[:, VEC[name][0] + m:VEC[name][0] + m + 1]

                def columns(i, first, last):
                    if i % NC == 0:
                        lo, n = VEC[first][0], VEC[last][0] + VEC[last][1] - VEC[first][0]
                        act.activation(cur[:, lo:lo + n], vec[:, bass.ds((l + i // NC) * NVEC + lo, n)], ACT.Copy)\
                           .then_inc(s_cur, 1)

                if s < ITEMS:
                    if s % NC == 0:
                        act.activation(ncur[:, :], vec[:, bass.ds((l + s // NC) * NVEC, 2 * KD)], ACT.Copy, scale=-1.0)
                    columns(s, "bq", "bo")
                if ln1(s):
                    columns(s - 1, "b1", "ln1_b")
                if ln2(s):
                    columns(s - 2, "ln2_s", "ln2_b")
                if s % NC < 3:
                    act.wait_ge(s_cur, columns_by(s) + 3 * l)

                def full():
                    act.wait_ge(s_full, at + r[0] + 1)
                    r[0] += 1
                    return ring[(r[0] - 1) % RING]

                def x1_copied():
                    act.wait_ge(s_r1, NC * l + s)
                    c = (s - 1) % NC
                    for m in range(KD):
                        last = act.activation(X1T[:, m, c * CH:(c + 1) * CH], pR[m][:, :], ACT.Identity,
                                              bias=col("ln1_b", m), scale=col("ln1_s", m))
                    last.then_inc(s_x1, 1)

                def f_made(m):
                    bank = full()
                    act.activation(ffo[:, m, :], bank[:, :], ACT.Gelu_apprx_tanh, bias=col("b2", m)).then_inc(s_ff, 1)
                    act.wait_ge(s_ff, KD * (NC * l + s - 1) + m + 1)
                    act.sem_inc(s_free, 1)

                if s < ITEMS:
                    for j, name in enumerate(("bq", "bk")):
                        for m in range(KD):
                            bank = full()
                            act.activation(nqk[:, j, m, :], bank[:, :], ACT.Relu, scale=-1.0,
                                           bias=ncur[:, KD * j + m:KD * j + m + 1])
                            act.activation(rqk[:, j, m, :], bank[:, :], ACT.Relu, bias=col(name, m)).then_inc(s_free, 1)
                    for m in range(KD):
                        if m == KD - 1 and ln1(s):
                            x1_copied()
                        bank = full()
                        act.activation(vv[:, m, :], bank[:, :], ACT.Identity, bias=col("bv", m)).then_inc(s_free, 1)
                    act.wait_ge(s_free, RING + at + r[0])
                    act.activation(eqk[:, :, :, :], nqk[:, :, :, :], ACT.Exp, scale=-1.0)
                    act.activation(prod[0:1, 0:1], vec[0:1, 0:1], ACT.Copy).then_inc(s_qkv, 1)
                if ln1(s):
                    if s == ITEMS:
                        x1_copied()
                    for f in range(KF):
                        bank = full()
                        act.activation(H[:, f, :], bank[:, :], ACT.Gelu_apprx_tanh, bias=col("b1", f)).then_inc(s_h, 1)
                        act.wait_ge(s_h, KF * (NC * l + s - 1) + f + 1)
                        act.sem_inc(s_free, 1)
                if ln2(s):
                    act.wait_ge(s_r2, NC * l + s - 1)
                    c = (s - 2) % NC
                    for m in range(KD):
                        last = act.activation(XT[:, m, c * CH:(c + 1) * CH], pR[m][:, :], ACT.Identity,
                                              bias=col("ln2_b", m), scale=col("ln2_s", m))
                    last.then_inc(s_x, 1)
                if ln1(s):
                    f_made(0)
                if s < ITEMS:
                    for m in range(KD):
                        bank = full()
                        act.activation(a1[:, m, :], bank[:, :], ACT.Gelu_apprx_tanh, bias=col("bo", m)).then_inc(s_free, 1)
                    act.wait_ge(s_free, RING + at + r[0])
                    act.activation(a2[:, :, :], a1[:, :, :], ACT.Gelu_apprx_tanh).then_inc(s_a, 1)
                if ln1(s):
                    f_made(1)

            steps(act, body)

        @block.gpsimd
        def _(pool):
            pool.memset(mhalf[:, :], -0.5).then_inc(s_mh, 1)
            pool.memset(nil[:, :], 0.0).then_inc(s_mh, 1)
            pool.wait_ge(s_mh, 2)
            ROWS = SLOTS // ITEMS
            with pool.Fori(0, ITEMS) as i:
                for j in range(2):
                    pool.wait_ge(s_ve, 2 * i + j + 1)
                    pool.tensor_tensor(rstd[:, :], veps[:, :], mhalf[:, :], ALU.pow).then_inc(s_rs, 1)
                pool.dma_start(g["yrows"][bass.ds(i * ROWS, ROWS), :].rearrange("(p r) d -> p r d", p=P),
                               nil[:, :].unsqueeze(1).to_broadcast([P, ROWS // P, D])).then_inc(s_yz, 16)
            pool.wait_ge(s_yz, 16 * ITEMS)

        @block.vector
        def _(dve):
            def chain_at(s, l):
                before = sum(2 * ln1(x) + 2 * ln2(x) + 5 * (x < ITEMS) for x in range(s))
                return before + 9 * NC * l

            def body(s, l):
                chain = Chain(dve, s_dve, chain_at(s, l))
                n = norms_before(s)
                if ln1(s):
                    dve.wait_ge(s_a, NC * l + s)
                    c = (s - 1) % NC
                    dve.tensor_tensor(s1[:, :, :], a2[:, :, :], XT[:, :, c * CH:(c + 1) * CH], ALU.add).then_inc(s_s1, 1)
                if ln2(s):
                    dve.wait_ge(s_ff, KD * (NC * l + s - 1))
                    c = (s - 2) % NC
                    dve.tensor_tensor(s2[:, :, :], ffo[:, :, :], X1T[:, :, c * CH:(c + 1) * CH], ALU.add).then_inc(s_s2, 1)
                if ln1(s):
                    n += 1
                    dve.wait_ge(s_n, 2 * NC * l + n)
                    last = normalise(dve, chain, pN, stats, mv, veps, 1e-6, s_ve, s_rs, 2 * NC * l + n, rstd, xn[0], g["carrier"])
                    last.then_inc(s_xn1, 1)
                    dve.wait_ge(s_xn1, NC * l + s)
                    dve.sem_inc(s_nf, 1)
                if ln2(s):
                    n += 1
                    dve.wait_ge(s_n, 2 * NC * l + n)
                    last = normalise(dve, chain, pN, stats, mv, veps, 1e-6, s_ve, s_rs, 2 * NC * l + n, rstd, xn[1], g["carrier"])
                    last.then_inc(s_xn2, 1)
                    dve.wait_ge(s_xn2, NC * l + s - 1)
                    dve.sem_inc(s_nf, 1)
                if s < ITEMS:
                    dve.wait_ge(s_qkv, NC * l + s + 1)
                    chain.link(dve.tensor_scalar(em1[:, :, :, :], eqk[:, :, :, :], -1.0, None, ALU.add))
                    for m in range(KD):
                        for b in range(2):
                            o = slice(b * SEQ, (b + 1) * SEQ)
                            last = dve.scalar_tensor_tensor(K[:, m, o], em1[:, 1, m, o], 1.0, rqk[:, 1, m, o],
                                                            ALU.add, ALU.add, accum_out=ksum[:, 2 * m + b:2 * m + b + 1])
                    last = dve.scalar_tensor_tensor(Q[:, :, :], em1[:, 0, :, :], 1.0, rqk[:, 0, :, :], ALU.add, ALU.add)
                    chain.link(last)
                    for m in range(KD):
                        for b in range(2):
                            o = slice(b * SEQ, (b + 1) * SEQ)
                            dve.scalar_tensor_tensor(g["junk"][:, 2 * m + b, :], K[:, m, o], 1.0, vv[:, m, o], ALU.mult, ALU.mult,
                                                     accum_out=kv[:, 2 * m + b:2 * m + b + 1])
                            last = dve.tensor_scalar(den[:, m, o], Q[:, m, o], ksum[:, 2 * m + b:2 * m + b + 1], 1e-6,
                                                     ALU.mult, ALU.add)
                    chain.link(last)
                    chain.link(dve.reciprocal(rec[:, :, :], den[:, :, :]))
                    for m in range(KD):
                        for b in range(2):
                            o = slice(b * SEQ, (b + 1) * SEQ)
                            last = dve.scalar_tensor_tensor(mix[:, m, o], Q[:, m, o], kv[:, 2 * m + b:2 * m + b + 1],
                                                            rec[:, m, o], ALU.mult, ALU.mult)
                    last.then_inc(s_mix, 1)
                    chain.n += 1
                    dve.sem_inc(s_dve, 1)
                want = 2 * ln1(s) + 2 * ln2(s) + 5 * (s < ITEMS)
                assert chain.n == want, (s, chain.n, want)

            steps(dve, body)


def to_rows(pe, out, src, col, ident):
    for j in range(TPC):
        for k in range(KD):
            last = pe.transpose(out[:, j, k * P:(k + 1) * P], src[:, k, col + j * P:col + (j + 1) * P], ident[:, :])
    return last


def to_columns(pe, out, src, ident):
    for j in range(TPC):
        for k in range(KD):
            last = pe.transpose(out[k][:, j * P:(j + 1) * P], src[:, j, k * P:(k + 1) * P], ident[:, :])
    return last


EXPERTS0 = 8


def shared0_phase(nc, ctx0, g, a):
    ctx = ExitStack()
    with ctx:
        def sb(name, shape, dt=F32):
            return ctx.enter_context(nc.sbuf_tensor(name, shape, dt))

        def pb(name, shape, dt=F32):
            return ctx.enter_context(nc.psum_tensor(name, shape, dt))

        def sem(name):
            return ctx.enter_context(nc.semaphore(name))

        ident, h, XT, prob = g["ident"], g["h"], g["XT"], g["prob"]
        ws1 = sb("f_ws1", [P, KD, P])
        ws2 = sb("f_ws2", [P, D])
        wr = sb("f_wr", [P, KD, EXPERTS0])
        stats = sb("f_stats", [P, NT, 6])
        mv = sb("f_mv", [P, NT, 2])
        veps = sb("f_veps", [P, NT])
        rstd = sb("f_rstd", [P, NT])
        mhalf = sb("f_mhalf", [P, NT])
        xn = sb("f_xn", [P, TPC, D])
        relu = sb("f_relu", [P, CH])
        act2 = sb("f_act2", [P, CH])
        top = sb("f_top", [P, TPC, 8])
        gap = sb("f_gap", [P, TPC])
        egap = sb("f_egap", [P, TPC])
        tot = sb("f_tot", [P, TPC])
        rw = sb("f_rw", [P, TPC])
        whole = sb("f_whole", [P, TPC])
        most = sb("f_most", [P, 1])
        pN = pb("f_pN", [P, TPC, D])
        pR = [pb(f"f_pR{i}", [P, CH]) for i in range(KD)]
        pL = pb("f_pL", [P, 512])
        pH = pb("f_pH", [P, CH])
        pD = pb("f_pD", [P, TPC, D])

        s_w = sem("f_weights_loaded")
        s_mh = sem("f_mhalf_made")
        s_n = sem("f_rows_natural")
        s_nr = sem("f_rows_added")
        s_ve = sem("f_veps_ready")
        s_rs = sem("f_rstd_ready")
        s_xn = sem("f_xn_ready")
        s_r = sem("f_xn_transposed")
        s_x = sem("f_xT_ready")
        s_h1 = sem("f_hidden_done")
        s_re = sem("f_relu_ready")
        s_sq = sem("f_square_ready")
        s_l = sem("f_logits_done")
        s_gap = sem("f_gap_ready")
        s_eg = sem("f_exp_gap_ready")
        s_lr = sem("f_logits_read")
        s_d = sem("f_down_done")
        s_ha = sem("f_h_added")
        s_dve = sem("f_dve_steps")
        s_mo = sem("f_most_ready")
        s_c = sem("f_count_done")

        block = ctx.enter_context(nc.Block())

        @block.sync
        def _(sp):
            sp.dma_start(ws1[:, :, :], a["ws1"].rearrange("(k p) n -> p k n", p=P)).then_inc(s_w, 16)
            sp.dma_start(ws2[:, :], a["ws2"]).then_inc(s_w, 16)
            sp.dma_start(wr[:, :, :], a["wr"].rearrange("(k p) n -> p k n", p=P)).then_inc(s_w, 16)

        @block.tensor
        def _(pe):
            for c in range(NC):
                if c >= 2:
                    pe.wait_ge(s_nr, c - 1)
                to_rows(pe, (pN, pD)[c % 2], XT, c * CH, ident).then_inc(s_n, 1)

            def xn_transposed(c):
                pe.wait_ge(s_xn, c + 1)
                if c:
                    pe.wait_ge(s_x, c)
                to_columns(pe, pR, xn, ident).then_inc(s_r, 1)

            xn_transposed(0)
            for c in range(NC):
                pe.wait_ge(s_x, c + 1)
                if c == 0:
                    pe.wait_ge(s_w, 48)
                if c:
                    pe.wait_ge(s_re, c)
                for k in range(KD):
                    last = pe.matmul(pH[:, :], ws1[:, k, :], XT[:, k, c * CH:(c + 1) * CH], start=(k == 0), stop=(k == KD - 1))
                last.then_inc(s_h1, 1)
                if c:
                    pe.wait_ge(s_lr, c)
                for j in range(TPC):
                    for k in range(KD):
                        last = pe.matmul(pL[:, j * EXPERTS0:(j + 1) * EXPERTS0], XT[:, k, c * CH + j * P:c * CH + (j + 1) * P],
                                         wr[:, k, :], start=(k == 0), stop=(k == KD - 1))
                last.then_inc(s_l, 1)
                if c + 1 < NC:
                    xn_transposed(c + 1)
                pe.wait_ge(s_sq, c + 1)
                if c:
                    pe.wait_ge(s_ha, c)
                for j in range(TPC):
                    last = pe.matmul(pD[:, j, :], act2[:, j * P:(j + 1) * P], ws2[:, :], start=True, stop=True)
                last.then_inc(s_d, 1)
            pe.wait_ge(s_mo, 1)
            pe.matmul(pL[:, 0:1], g["ones"][:, :], most[:, :], start=True, stop=True).then_inc(s_c, 1)

        @block.scalar
        def _(act):
            def x_copied(c):
                act.wait_ge(s_r, c + 1)
                for k in range(KD):
                    last = act.activation(XT[:, k, c * CH:(c + 1) * CH], pR[k][:, :], ACT.Copy)
                last.then_inc(s_x, 1)

            x_copied(0)
            for c in range(NC):
                act.wait_ge(s_h1, c + 1)
                if c:
                    act.wait_ge(s_sq, c)
                act.activation(relu[:, :], pH[:, :], ACT.Relu).then_inc(s_re, 1)
                if c + 1 < NC:
                    x_copied(c + 1)
                act.wait_ge(s_gap, c + 1)
                act.activation(egap[:, :], gap[:, :], ACT.Exp).then_inc(s_eg, 1)

        @block.gpsimd
        def _(pool):
            pool.memset(mhalf[:, :], -0.5).then_inc(s_mh, 1)
            pool.wait_ge(s_mh, 1)
            pool.wait_ge(s_ve, 1)
            pool.tensor_tensor(rstd[:, :], veps[:, :], mhalf[:, :], ALU.pow).then_inc(s_rs, 1)

        @block.vector
        def _(dve):
            chain = Chain(dve, s_dve)
            for c in range(NC):
                hc = h[:, c * TPC:(c + 1) * TPC, :]
                dve.wait_ge(s_n, c + 1)
                dve.tensor_tensor(hc, hc, (pN, pD)[c % 2][:, :, :], ALU.add).then_inc(s_nr, 1)
                dve.wait_ge(s_nr, c + 1)
                for t in range(c * TPC, (c + 1) * TPC):
                    last = dve.bn_stats(stats[:, t, :], h[:, t, :])
            rows_scaled = normaliser(dve, chain, last, h, stats, mv, veps, 1e-5, s_ve, s_rs, rstd)
            rows_scaled(0, xn).then_inc(s_xn, 1)
            for c in range(NC):
                hc = h[:, c * TPC:(c + 1) * TPC, :]
                if c + 1 < NC:
                    dve.wait_ge(s_r, c + 1)
                    rows_scaled(c + 1, xn).then_inc(s_xn, 1)
                dve.wait_ge(s_re, c + 1)
                dve.tensor_tensor(act2[:, :], relu[:, :], relu[:, :], ALU.mult).then_inc(s_sq, 1)
                dve.wait_ge(s_l, c + 1)
                for j in range(TPC):
                    last = dve.max(top[:, j, :], pL[:, j * EXPERTS0:(j + 1) * EXPERTS0])
                chain.link(last)
                dve.tensor_tensor(gap[:, :], top[:, :, 1], top[:, :, 0], ALU.subtract).then_inc(s_gap, 1)
                dve.wait_ge(s_eg, c + 1)
                chain.link(dve.tensor_scalar(tot[:, :], egap[:, :], 1.0, None, ALU.add))
                chain.link(dve.reciprocal(rw[:, :], tot[:, :]))
                chain.link(dve.tensor_scalar(whole[:, :], rw[:, :], 1.0, None, ALU.is_ge))
                for j in range(TPC):
                    last = dve.tensor_scalar(prob[:, c * TPC + j, :], pL[:, j * EXPERTS0:(j + 1) * EXPERTS0],
                                             top[:, j, 0:1], whole[:, j:j + 1], ALU.is_equal, ALU.mult)
                last.then_inc(s_lr, 1)
                dve.wait_ge(s_d, c + 1)
                dve.tensor_tensor(hc, hc, pD[:, :, :], ALU.add).then_inc(s_ha, 1)
            dve.wait_ge(s_lr, NC)
            dve.tensor_reduce(most[:, :], prob[:, :, :], AX.XY, ALU.max).then_inc(s_mo, 1)
            dve.wait_ge(s_c, 1)
            dve.tensor_copy(g["routed"][:, :], pL[:, 0:1]).then_inc(s_mo, 1)
            dve.wait_ge(s_mo, 2)
            dve.wait_ge(s_ha, NC)


def routed0_phase(nc, ctx0, g, a):
    ctx = ExitStack()
    with ctx:
        def sb(name, shape, dt=F32):
            return ctx.enter_context(nc.sbuf_tensor(name, shape, dt))

        def sem(name):
            return ctx.enter_context(nc.semaphore(name))

        h, XT, prob, flag = g["h"], g["XT"], g["prob"], g["routed"]
        w1 = sb("r_w1", [P, KD, P])
        w2 = sb("r_w2", [P, D])
        pe_col = sb("r_col", [P, NT])
        relu = sb("r_relu", [P, CH])
        act2 = sb("r_act2", [P, CH])
        pH = ctx.enter_context(nc.psum_tensor("r_pH", [P, CH], F32))
        pD = ctx.enter_context(nc.psum_tensor("r_pD", [P, TPC, D], F32))
        s_w = sem("r_weights_loaded")
        s_h1 = sem("r_hidden_done")
        s_re = sem("r_relu_ready")
        s_sq = sem("r_square_ready")
        s_d = sem("r_down_done")
        s_ha = sem("r_h_added")
        s_pr = sem("r_prob_ready")
        block = ctx.enter_context(nc.Block())

        @block.sync
        def _(sp):
            any_routed = sp.value_load(flag[0:1, 0:1], min_val=0, max_val=P)
            with sp.If(any_routed > 0):
                with sp.Fori(0, EXPERTS0) as e:
                    sp.wait_ge(s_d, NC * e + 1)
                    sp.dma_start(w1[:, :, :], a["w1r"][bass.ds(e, 1), :, :].rearrange("e (k p) n -> p (e k) n", p=P)).then_inc(s_w, 16)
                    sp.dma_start(w2[:, :], a["w2r"][bass.ds(e, 1), :, :].rearrange("e p n -> p (e n)")).then_inc(s_w, 16)
                sp.nop()

        @block.tensor
        def _(pe):
            any_routed = pe.value_load(flag[0:1, 0:1], min_val=0, max_val=P)
            with pe.If(any_routed > 0):
                pe.sem_inc(s_d, 1)
                with pe.Fori(0, EXPERTS0) as e:
                    pe.wait_ge(s_w, 32 * e + 32)
                    for c in range(NC):
                        for k in range(KD):
                            last = pe.matmul(pH[:, :], w1[:, k, :], XT[:, k, c * CH:(c + 1) * CH], start=(k == 0), stop=(k == KD - 1))
                        last.then_inc(s_h1, 1)
                        pe.wait_ge(s_sq, NC * e + c + 1)
                        pe.wait_ge(s_ha, NC * e + c + 1)
                        for j in range(TPC):
                            last = pe.matmul(pD[:, j, :], act2[:, j * P:(j + 1) * P], w2[:, :], start=True, stop=True)
                        last.then_inc(s_d, 1)
                pe.nop()

        @block.scalar
        def _(act):
            any_routed = act.value_load(flag[0:1, 0:1], min_val=0, max_val=P)
            with act.If(any_routed > 0):
                with act.Fori(0, EXPERTS0) as e:
                    for c in range(NC):
                        act.wait_ge(s_h1, NC * e + c + 1)
                        act.activation(relu[:, :], pH[:, :], ACT.Relu).then_inc(s_re, 1)
                act.nop()

        @block.vector
        def _(dve):
            any_routed = dve.value_load(flag[0:1, 0:1], min_val=0, max_val=P)
            with dve.If(any_routed > 0):
                dve.sem_inc(s_ha, 1)
                with dve.Fori(0, EXPERTS0) as e:
                    dve.tensor_copy(pe_col[:, :], prob[:, :, bass.ds(e, 1)]).then_inc(s_pr, 1)
                    dve.wait_ge(s_pr, e + 1)
                    for c in range(NC):
                        dve.wait_ge(s_re, NC * e + c + 1)
                        dve.tensor_tensor(act2[:, :], relu[:, :], relu[:, :], ALU.mult).then_inc(s_sq, 1)
                        dve.wait_ge(s_d, NC * e + c + 2)
                        for j in range(TPC):
                            t = c * TPC + j
                            last = dve.scalar_tensor_tensor(h[:, t, :], pD[:, j, :], pe_col[:, t:t + 1], h[:, t, :],
                                                            ALU.mult, ALU.add)
                        last.then_inc(s_ha, 1)
                        dve.wait_ge(s_ha, NC * e + c + 2)
                dve.nop()


HEADS = 16
DH = 16
SEQS = T // SEQ
SPLIT = 3
LEFT = (0, 0, 1, 1, 0, 2, 1, 2)
RIGHT = (0, 1, 0, 1, 2, 0, 2, 1)
QUAD = 4
HW = P // QUAD
PACKS = 3


def queries_phase(nc, ctx0, g, a):
    ctx = ExitStack()
    with ctx:
        def sb(name, shape, dt=F32):
            return ctx.enter_context(nc.sbuf_tensor(name, shape, dt))

        def pb(name, shape, dt=F32):
            return ctx.enter_context(nc.psum_tensor(name, shape, dt))

        def sem(name):
            return ctx.enter_context(nc.semaphore(name))

        ident, h, qn = g["ident"], g["h"], g["qn"]
        wq = sb("q_wq", [P, KD, P])
        stats = sb("q_stats", [P, NT, 6])
        mv = sb("q_mv", [P, NT, 2])
        veps = sb("q_veps", [P, NT])
        rstd = sb("q_rstd", [P, NT])
        mhalf = sb("q_mhalf", [P, NT])
        xn = sb("q_xn", [P, 2, TPC, D])
        xT = sb("q_xT", [P, 2, KD, CH])
        part = sb("q_part", [P, 2, SPLIT, KD, CH], BF16)
        rest = sb("q_rest", [P, KD, CH])
        pR = [pb(f"q_pR{i}", [P, CH]) for i in range(KD)]
        pQ = [pb(f"q_pQ{i}", [P, CH]) for i in range(KD)]
        pN = [pb(f"q_pN{i}", [P, 2, D]) for i in range(2)]

        s_z = sem("q_weights_zeroed")
        s_w = sem("q_weights_loaded")
        s_c = sem("q_constants_made")
        s_dve = sem("q_dve_steps")
        s_ve = sem("q_veps_ready")
        s_rs = sem("q_rstd_ready")
        s_xn = sem("q_xn_ready")
        s_r = sem("q_xn_transposed")
        s_x = sem("q_xT_ready")
        s_q = sem("q_projected")
        s_n = sem("q_rows_projected")
        s_p1 = sem("q_part1_ready")
        s_r1 = sem("q_rest_ready")
        s_p2 = sem("q_part2_ready")
        s_p3 = sem("q_part3_ready")
        s_ne = sem("q_rows_ready")
        s_st = [sem(f"q_parts{i}_stored") for i in range(2)]

        block = ctx.enter_context(nc.Block())

        @block.sync
        def _(sp):
            sp.wait_ge(s_z, 1)
            for hd in range(HEADS):
                p0 = hd % 8 * DH
                sp.dma_start(wq[p0:p0 + DH, hd // 8, p0:p0 + DH], a["wq1"][hd]).then_inc(s_w, 16)
            for c in range(NC):
                sp.wait_ge(s_p3, c + 1)
                for i in range(SPLIT):
                    sp.dma_start(g["qparts"][i].rearrange("(k p) t -> p k t", p=P)[:, :, c * CH:(c + 1) * CH],
                                 part[:, c % 2, i, :, :]).then_inc(s_st[c % 2], 16)
            for i in range(2):
                sp.wait_ge(s_st[i], 16 * SPLIT * NC // 2)

        @block.gpsimd
        def _(pool):
            pool.memset(wq[:, :, :], 0.0).then_inc(s_z, 1)
            pool.memset(mhalf[:, :], -0.5).then_inc(s_c, 1)
            pool.wait_ge(s_c, 1)
            pool.wait_ge(s_ve, 1)
            pool.tensor_tensor(rstd[:, :], veps[:, :], mhalf[:, :], ALU.pow).then_inc(s_rs, 1)
            sel = g["sel"]
            pool.memset(sel[:, :, :], 0.0).then_inc(s_c, 1)
            for i in range(SPLIT):
                pool.wait_ge(s_c, 2 + i)
                pool.affine_select(out=sel[:, :, :], in_=sel[:, :, :], compare_op=ALU.not_equal, fill=1.0,
                                   base=-HEADS * i, pattern=[[-1, HEADS], [0, P]], channel_multiplier=1).then_inc(s_c, 1)
            pool.wait_ge(s_c, 2 + SPLIT)

        @block.tensor
        def _(pe):
            pe.wait_ge(s_w, 16 * HEADS)
            def xn_transposed(c):
                pe.wait_ge(s_xn, c + 1)
                if c:
                    pe.wait_ge(s_x, c)
                to_columns(pe, pR, xn[:, c % 2, :, :], ident).then_inc(s_r, 1)

            xn_transposed(0)
            for c in range(NC):
                pe.wait_ge(s_x, c + 1)
                if c:
                    pe.wait_ge(s_r1, c)
                for k in range(KD):
                    last = pe.matmul(pQ[k][:, :], wq[:, k, :], xT[:, c % 2, k, :], start=True, stop=True)
                last.then_inc(s_q, 1)
                if c:
                    pe.wait_ge(s_ne, c)
                for j in range(TPC):
                    for k in range(KD):
                        last = pe.matmul(pN[j // 2][:, j % 2, k * P:(k + 1) * P], xT[:, c % 2, k, j * P:(j + 1) * P], wq[:, k, :],
                                         start=True, stop=True)
                last.then_inc(s_n, 1)
                if c + 1 < NC:
                    xn_transposed(c + 1)

        @block.scalar
        def _(act):
            def x_copied(c):
                act.wait_ge(s_r, c + 1)
                if c >= 2:
                    act.wait_ge(s_n, c - 1)
                for k in range(KD):
                    last = act.activation(xT[:, c % 2, k, :], pR[k][:, :], ACT.Copy)
                last.then_inc(s_x, 1)

            x_copied(0)
            for c in range(NC):
                act.wait_ge(s_q, c + 1)
                if c >= 2:
                    act.wait_ge(s_st[c % 2], 16 * SPLIT * (c // 2))
                for k in range(KD):
                    last = act.activation(part[:, c % 2, 0, k, :], pQ[k][:, :], ACT.Copy)
                last.then_inc(s_p1, 1)
                act.wait_ge(s_r1, c + 1)
                act.activation(part[:, c % 2, 1, :, :], rest[:, :, :], ACT.Copy).then_inc(s_p2, 1)
                if c + 1 < NC:
                    x_copied(c + 1)

        @block.vector
        def _(dve):
            chain = Chain(dve, s_dve)

            dve.tensor_copy(g["ident_b"][:, :], ident[:, :]).then_inc(s_dve, 1)
            chain.n += 1
            for t in range(NT):
                last = dve.bn_stats(stats[:, t, :], h[:, t, :])
            rows_scaled = normaliser(dve, chain, last, h, stats, mv, veps, 1e-5, s_ve, s_rs, rstd)
            rows_scaled(0, xn[:, 0, :, :]).then_inc(s_xn, 1)
            for c in range(NC):
                if c + 1 < NC:
                    if c >= 1:
                        dve.wait_ge(s_r, c)
                    rows_scaled(c + 1, xn[:, (c + 1) % 2, :, :]).then_inc(s_xn, 1)
                dve.wait_ge(s_p1, c + 1)
                if c:
                    dve.wait_ge(s_p3, c)
                for k in range(KD):
                    last = dve.tensor_tensor(rest[:, k, :], pQ[k][:, :], part[:, c % 2, 0, k, :], ALU.subtract)
                last.then_inc(s_r1, 1)
                dve.wait_ge(s_n, c + 1)
                for i in range(2):
                    last = dve.tensor_copy(qn[:, c * TPC + 2 * i:c * TPC + 2 * i + 2, :, :],
                                           pN[i][:, :, :].rearrange("p a (h d) -> p a h d", d=DH))
                last.then_inc(s_ne, 1)
                dve.wait_ge(s_p2, c + 1)
                dve.wait_ge(s_r1, c + 1)
                dve.tensor_tensor(part[:, c % 2, 2, :, :], rest[:, :, :], part[:, c % 2, 1, :, :], ALU.subtract).then_inc(s_p3, 1)
            dve.wait_ge(s_ne, NC)


def attention_phase(nc, ctx0, g, a):
    ctx = ExitStack()
    with ctx:
        def sb(name, shape, dt=F32):
            return ctx.enter_context(nc.sbuf_tensor(name, shape, dt))

        def pb(name, shape, dt=F32):
            return ctx.enter_context(nc.psum_tensor(name, shape, dt))

        def sem(name):
            return ctx.enter_context(nc.semaphore(name))

        ident, h, qn, sel = g["ident"], g["h"], g["qn"], g["sel"]
        NTS = SEQ // P
        QUADS = HEADS // QUAD
        wp = sb("a_wp", [P, KD, D])
        bp = sb("a_bp", [1, D])
        one = sb("a_one", [1, P])
        left = sb("a_left", [P, PACKS, HEADS, SEQ], BF16)
        right = sb("a_right", [P, PACKS, HEADS, SEQ], BF16)
        qs = sb("a_qs", [P, PACKS, NTS, HEADS, HW])
        nmax = sb("a_nmax", [P, NTS, HEADS])
        nrest = sb("a_nrest", [P, NTS, HEADS])
        npart = sb("a_npart", [P, NTS, P], BF16)
        nT = sb("a_nT", [P, PACKS, SEQ], BF16)
        ET = sb("a_ET", [P, 4, NTS, SEQ])
        OT = sb("a_OT", [P, 2, SEQ])
        rrec = sb("a_rrec", [P, QUADS, NTS, QUAD])
        y = sb("a_y", [P, NTS, D])
        yT = sb("a_yT", [P, KD, SEQ])
        pA = [pb(f"a_pA{i}", [P, NTS, SEQ]) for i in range(2)]
        pB = [pb(f"a_pB{i}", [P, NTS, SEQ]) for i in range(2)]
        pO = [pb(f"a_pO{i}", [P, SEQ]) for i in range(2)]
        pR = pb("a_pR", [P, NTS, P])
        pC = pb("a_pC", [P, KD, SEQ])
        pM = pC[:, 0, :].bitcast(BF16)[:, 0:SEQ]
        pH = pC[:, :, :].rearrange("p k t -> p (k t)").rearrange("p (n d) -> p n d", d=D)

        s_w = sem("a_weights_loaded")
        s_one = sem("a_constants_made")
        s_pk = [sem(f"a_packs{i}_loaded") for i in range(PACKS)]
        s_qs = sem("a_qs_ready")
        s_s = sem("a_scores_done")
        s_m = sem("a_max_ready")
        s_nr = sem("a_max_parts_ready")
        s_sp = sem("a_max_rest_ready")
        s_nt = sem("a_max_transposed")
        s_nte = sem("a_maxT_ready")
        s_b = sem("a_shifted_done")
        s_e = sem("a_exp_ready")
        s_o = sem("a_heads_done")
        s_ot = sem("a_quad_copied")
        s_r = sem("a_quad_transposed")
        s_rr = sem("a_sums_inverted")
        s_y = sem("a_y_ready")
        s_yt = sem("a_y_transposed")
        s_yte = sem("a_yT_ready")
        s_p = sem("a_projected")
        s_h = sem("a_h_added")

        block = ctx.enter_context(nc.Block())

        def sequences(eng, body):
            body(0, 0)
            with eng.Fori(0, (SEQS - 2) // PACKS) as l:
                for i in range(1, PACKS + 1):
                    body(i, l)
            body(SEQS - 1, 0)

        @block.sync
        def _(sp):
            sp.dma_start(wp[:, :, :], a["wp"].rearrange("(k p) n -> p k n", p=P)).then_inc(s_w, 16)
            sp.dma_start(bp[:, :], a["bp"].rearrange("(o n) -> o n", o=1)).then_inc(s_w, 16)
            for n in range(SEQS):
                if n >= PACKS:
                    sp.wait_ge(s_b, HEADS * (n - PACKS + 1))
                for side, parts in ((left, LEFT), (right, RIGHT)):
                    for b, part in enumerate(parts):
                        sp.dma_start(side[b * DH:(b + 1) * DH, n % PACKS, :, :],
                                     g["qparts"][part].rearrange("(h r) t -> r h t", r=DH)[:, :, n * SEQ:(n + 1) * SEQ])\
                            .then_inc(s_pk[n % PACKS], 16)

        @block.gpsimd
        def _(pool):
            pool.memset(one[:, :], 1.0).then_inc(s_one, 1)
            pool.memset(npart[:, :, :], 0.0).then_inc(s_one, 1)
            pool.memset(qs[:, :, :, :, DH:DH + 1], 1.0).then_inc(s_one, 1)
            pool.memset(qs[:, :, :, :, DH + 1:], 0.0).then_inc(s_one, 1)
            for n in range(SEQS):
                if n >= PACKS:
                    pool.wait_ge(s_o, HEADS * (n - PACKS + 1) + 4)
                for j in range(NTS):
                    last = pool.tensor_copy(qs[:, n % PACKS, j, :, 0:DH], qn[:, NTS * n + j, :, :])
                last.then_inc(s_qs, 1)

        @block.tensor
        def _(pe):
            pe.wait_ge(s_one, 4)
            pe.wait_ge(s_w, 32)

            def maxima(i, l, hd):
                slot, n = i % PACKS, HEADS * (PACKS * l + i) + hd
                if hd == 0:
                    pe.wait_ge(s_pk[slot], 16 * 16 * (l + i // PACKS + 1))
                if i or hd >= 2:
                    pe.wait_ge(s_m, n - 1)
                for nt in range(NTS):
                    last = pe.matmul(pA[hd % 2][:, nt, :], left[:, slot, hd, nt * P:(nt + 1) * P], right[:, slot, hd, :],
                                     start=True, stop=True)
                last.then_inc(s_s, 1)

            def maxima_transposed(i, l):
                pe.wait_ge(s_nr, 3 * (PACKS * l + i) + 3)
                if i >= 2:
                    pe.wait_ge(s_h, PACKS * l + i - 1)
                for nt in range(NTS):
                    last = pe.transpose(pM[:, nt * P:(nt + 1) * P], npart[:, nt, :], g["ident_b"][:, :])
                last.then_inc(s_nt, 1)

            def shifted(i, l, hd):
                slot, n = i % PACKS, HEADS * (PACKS * l + i) + hd
                if hd == 0:
                    pe.wait_ge(s_nte, PACKS * l + i + 1)
                pe.wait_ge(s_e, n + 1)
                for mt in range(NTS):
                    pe.matmul(pB[hd % 2][:, mt, :], left[:, slot, hd, mt * P:(mt + 1) * P], right[:, slot, hd, :],
                              start=True, stop=False)
                    last = pe.matmul(pB[hd % 2][:, mt, :], sel[:, hd, :], nT[:, slot, :], start=False, stop=True)
                last.then_inc(s_b, 1)

            def values(i, l, hd):
                n, slot, part = HEADS * (PACKS * l + i) + hd, i % PACKS, hd % QUAD
                if hd == 0:
                    pe.wait_ge(s_qs, PACKS * l + i + 1)
                if part == 0:
                    pe.wait_ge(s_ot, QUADS * (PACKS * l + i) + hd // QUAD + 1)
                pe.wait_ge(s_e, n + 3)
                for mt in range(NTS):
                    last = pe.matmul(pO[hd // QUAD % 2][part * HW:(part + 1) * HW, :], qs[:, slot, mt, hd, :],
                                     ET[:, hd % 4, mt, :], start=(mt == 0), stop=(mt == NTS - 1))
                last.then_inc(s_o, 1)

            def quad_transposed(i, l, k):
                n = QUADS * (PACKS * l + i) + k
                pe.wait_ge(s_ot, n + 3)
                pe.wait_ge(s_y, n + 1)
                for nt in range(NTS):
                    last = pe.transpose(pR[:, nt, :], OT[:, k % 2, nt * P:(nt + 1) * P], ident[:, :])
                last.then_inc(s_r, 1)

            def y_transposed(i, l):
                pe.wait_ge(s_y, QUADS * (PACKS * l + i + 1) + 1)
                pe.wait_ge(s_nte, min(i + 2, SEQS) if isinstance(l, int) else PACKS * l + i + 2)
                for nt in range(NTS):
                    for k in range(KD):
                        last = pe.transpose(pC[:, k, nt * P:(nt + 1) * P], y[:, nt, k * P:(k + 1) * P], ident[:, :])
                last.then_inc(s_yt, 1)

            def project(i, l):
                pe.wait_ge(s_yte, PACKS * l + i + 1)
                for nt in range(NTS):
                    for k in range(KD):
                        pe.matmul(pH[:, nt, :], yT[:, k, nt * P:(nt + 1) * P], wp[:, k, :], start=(k == 0), stop=False)
                    last = pe.matmul(pH[:, nt, :], one[:, :], bp[:, :], start=False, stop=True)
                last.then_inc(s_p, 1)

            def body(i, l):
                for hd in range(HEADS):
                    if i < SEQS - 1 and hd < HEADS - 1:
                        if hd == 0:
                            maxima(i + 1, l, 0)
                        maxima(i + 1, l, hd + 1)
                    shifted(i, l, hd)
                    if hd:
                        values(i, l, hd - 1)
                    elif i:
                        values(i - 1, l, HEADS - 1)
                    if hd in (6, 10, 14):
                        quad_transposed(i, l, hd // QUAD - 1)
                    if i and hd == 2:
                        quad_transposed(i - 1, l, QUADS - 1)
                    if i and hd == 5:
                        y_transposed(i - 1, l)
                    if i and hd == 8:
                        project(i - 1, l)
                if i < SEQS - 1:
                    maxima_transposed(i + 1, l)

            for hd in range(HEADS):
                maxima(0, 0, hd)
            maxima_transposed(0, 0)
            sequences(pe, body)
            values(SEQS - 1, 0, HEADS - 1)
            quad_transposed(SEQS - 1, 0, QUADS - 1)
            y_transposed(SEQS - 1, 0)
            project(SEQS - 1, 0)

        @block.scalar
        def _(act):
            for i in range(2):
                act.sem_inc(s_e, 1)
                act.sem_inc(s_ot, 1)

            def maxima_copied(i, l):
                act.wait_ge(s_nt, PACKS * l + i + 1)
                act.activation(nT[:, i % PACKS, :], pM, ACT.Copy).then_inc(s_nte, 1)

            def quad_copied(i, l, k):
                n = QUADS * (PACKS * l + i) + k
                act.wait_ge(s_o, QUAD * (n + 1) + 4)
                act.wait_ge(s_r, n + 1)
                act.activation(OT[:, k % 2, :], pO[k % 2][:, :], ACT.Copy).then_inc(s_ot, 1)

            def y_copied(i, l):
                act.wait_ge(s_yt, PACKS * l + i + 1)
                act.activation(yT[:, :, :], pC[:, :, :], ACT.Copy).then_inc(s_yte, 1)

            def body(i, l):
                for hd in range(HEADS):
                    n = HEADS * (PACKS * l + i) + hd
                    act.wait_ge(s_b, n + 1)
                    act.wait_ge(s_o, n + 1)
                    act.activation(ET[:, hd % 4, :, :], pB[hd % 2][:, :, :], ACT.Exp, scale=4.0).then_inc(s_e, 1)
                    if hd in (5, 9, 13):
                        quad_copied(i, l, hd // QUAD - 1)
                    if i and hd == 1:
                        quad_copied(i - 1, l, QUADS - 1)
                    if i and hd == 6:
                        y_copied(i - 1, l)
                if i < SEQS - 1:
                    maxima_copied(i + 1, l)

            maxima_copied(0, 0)
            sequences(act, body)
            quad_copied(SEQS - 1, 0, QUADS - 1)
            y_copied(SEQS - 1, 0)

        @block.vector
        def _(dve):
            def maximum(i, l, hd):
                dve.wait_ge(s_s, HEADS * (PACKS * l + i) + hd + 1)
                dve.tensor_reduce(nmax[:, :, hd], pA[hd % 2][:, :, :], AX.X, ALU.max, negate=True).then_inc(s_m, 1)

            def split(i, l):
                n = PACKS * l + i
                dve.wait_ge(s_m, HEADS * (n + 1))
                if i:
                    dve.wait_ge(s_nt, n)
                dve.tensor_copy(npart[:, :, 0:HEADS], nmax[:, :, :]).then_inc(s_nr, 1)
                dve.wait_ge(s_nr, 3 * n + 1)
                dve.tensor_tensor(nrest[:, :, :], nmax[:, :, :], npart[:, :, 0:HEADS], ALU.subtract).then_inc(s_sp, 1)
                dve.wait_ge(s_sp, n + 1)
                dve.tensor_copy(npart[:, :, HEADS:2 * HEADS], nrest[:, :, :]).then_inc(s_nr, 1)
                dve.wait_ge(s_nr, 3 * n + 2)
                dve.tensor_tensor(npart[:, :, 2 * HEADS:SPLIT * HEADS], nrest[:, :, :], npart[:, :, HEADS:2 * HEADS], ALU.subtract)\
                    .then_inc(s_nr, 1)

            def divide(i, l, k):
                n = QUADS * (PACKS * l + i) + k
                quad = pR[:, :, :].rearrange("p t (g c) -> p t g c", c=HW)
                dve.wait_ge(s_r, n + 3)
                dve.reciprocal(rrec[:, k, :, :], quad[:, :, :, DH]).then_inc(s_rr, 1)
                dve.wait_ge(s_rr, n + 1)
                if k == 0 and i:
                    dve.wait_ge(s_yt, PACKS * l + i)
                dve.tensor_tensor(y[:, :, k * QUAD * DH:(k + 1) * QUAD * DH].rearrange("p t (g d) -> p t g d", d=DH),
                                  quad[:, :, :, 0:DH], rrec[:, k, :, :].unsqueeze(3).to_broadcast([P, NTS, QUAD, DH]), ALU.mult)\
                    .then_inc(s_y, 1)

            def add(i, l):
                n = PACKS * l + i
                dve.wait_ge(s_p, n + 1)
                rows = h[:, NTS * i:NTS * (i + 1), :] if isinstance(l, int) else h[:, bass.ds(NTS * n, NTS), :]
                dve.tensor_tensor(rows, rows, pH[:, :, :], ALU.add).then_inc(s_h, 1)
                dve.wait_ge(s_h, n + 1)
                for j in range(NTS):
                    t = NTS * n + j
                    if isinstance(l, int):
                        dve.bn_stats(g["stats"][:, t, :], h[:, t, :])
                    else:
                        dve.bn_stats(g["stats"][:, bass.ds(t, 1), :], h[:, bass.ds(t, 1), :])

            def body(i, l):
                for hd in range(HEADS):
                    if i < SEQS - 1 and hd < HEADS - 1:
                        if hd == 0:
                            maximum(i + 1, l, 0)
                        maximum(i + 1, l, hd + 1)
                        if hd == HEADS - 2:
                            split(i + 1, l)
                    if hd in (7, 11, 15):
                        divide(i, l, hd // QUAD - 1)
                    if i and hd == 3:
                        divide(i - 1, l, QUADS - 1)
                    if i and hd == 9:
                        add(i - 1, l)

            dve.wait_ge(s_one, 4)
            dve.sem_inc(s_y, 1)
            for i in range(2):
                dve.sem_inc(s_r, 1)
            for i in range(4):
                dve.sem_inc(s_o, 1)
            for hd in range(HEADS):
                maximum(0, 0, hd)
            split(0, 0)
            sequences(dve, body)
            divide(SEQS - 1, 0, QUADS - 1)
            add(SEQS - 1, 0)
            dve.wait_ge(s_h, SEQS)


NEXP = 64
TOPK = 8
CAP = 256
NG = 8
TG = 4
EPG = NEXP // NG
ROUTE_SCALE = 2.5
SLOTS = NEXP * CAP
ST = SLOTS // P
SPE = CAP // P
KSTEP = 2
KSTEPS = TOPK // KSTEP
KS = 2
HID = 128


def router_phase(nc, ctx0, g, a):
    ctx = ExitStack()
    with ctx:
        def sb(name, shape, dt=F32):
            return ctx.enter_context(nc.sbuf_tensor(name, shape, dt))

        def pb(name, shape, dt=F32):
            return ctx.enter_context(nc.psum_tensor(name, shape, dt))

        def sem(name):
            return ctx.enter_context(nc.semaphore(name))

        ident, h, idx, ones_b, before = (g[n] for n in ("ident", "h", "idx", "ones_b", "before"))
        gate = sb("m_gate", [P, KD, NEXP])
        sgate = sb("m_sgate", [P, KD, KS * P])
        sup = sb("m_sup", [P, KD, KS * P])
        sdown = sb("m_sdown", [P, KS, D])
        ebias = sb("m_ebias", [P, NEXP])
        mv = sb("m_mv", [P, NT, 2])
        veps = sb("m_veps", [P, NT])
        rstd = sb("m_rstd", [P, NT])
        mhalf = sb("m_mhalf", [P, NT])
        mvc = sb("m_mvc", [P, TPC, 2])
        rstdc = sb("m_rstdc", [P, TPC])
        xn = sb("m_xn", [P, TPC, D])
        xT = sb("m_xT", [P, KD, CH])
        lower = sb("m_lower", [P, NG, NG])
        first_i = sb("m_first_i", [P, NEXP], I32)
        first = sb("m_first", [P, NEXP])
        tok_i = sb("m_tok_i", [P, NT], I32)
        tok = sb("m_tok", [P, NT])
        zeros = sb("m_zeros", [P, ST])
        score = sb("m_score", [P, TPC, NEXP])
        sfc = sb("m_sfc", [P, TPC, NEXP])
        top2 = sb("m_top2", [P, TPC * NG, 8])
        gs = sb("m_gs", [P, TPC, NG])
        gt = sb("m_gt", [P, TPC, NG * NG])
        eq = sb("m_eq", [P, TPC, NG * NG])
        eql = sb("m_eql", [P, TPC, NG * NG])
        rank = sb("m_rank", [P, TPC * NG])
        keep = sb("m_keep", [P, TPC * NG])
        kept = sb("m_kept", [P, TPC, NEXP])
        cand = sb("m_cand", [P, TPC, NEXP])
        v8 = sb("m_v8", [P, TPC, 8])
        rest = sb("m_rest", [P, TPC, NEXP])
        M = sb("m_M", [P, TPC, NEXP])
        Mb = sb("m_Mb", [P, TPC, NEXP], BF16)
        w = sb("m_w", [P, TPC, NEXP])
        wsum = sb("m_wsum", [P, TPC])
        wsum2 = sb("m_wsum2", [P, TPC])
        wrec = sb("m_wrec", [P, TPC])
        wfull = sb("m_wfull", [P, TPC, NEXP])
        valid = sb("m_valid", [P, TPC, NEXP])
        slot = sb("m_slot", [P, TPC, NEXP])
        slot1 = sb("m_slot1", [P, TPC, NEXP])
        wv = sb("m_wv", [P, TPC, NEXP])
        s8 = sb("m_s8", [P, TPC, TOPK])
        v8b = sb("m_v8b", [P, TPC * TOPK], BF16)
        kall = sb("m_kall", [1, NT + 1])
        kcnt = sb("m_kcnt", [1, TPC])
        some = sb("m_some", [1, TPC, TOPK])
        mch = sb("m_mch", [P, NEXP])
        cum = [sb("m_cum", [P, NEXP]), g["taken"][:, 0:NEXP]]
        sg = sb("m_sg", [P, KS, CH])
        sgg = sb("m_sgg", [P, KS, CH])
        hid = sb("m_hid", [P, KS, CH])
        pR = [pb(f"m_pR{i}", [P, CH]) for i in range(KD)]
        pGF = pb("m_pGF", [P, 2, TPC, NEXP])
        pG = pGF[:, 0, :, :]
        pF = pGF[:, 1, 0, 0:TPC * TOPK]
        pP = pb("m_pP", [P, TPC, NEXP])
        pA = [pb(f"m_pA{i}", [P, CH]) for i in range(2 * KS)]

        s_w = sem("m_weights_loaded")
        s_z = sem("m_zeros_made")
        s_zd = sem("m_list_zeroed")
        s_c = sem("m_constants_made")
        s_cc = sem("m_constants_cast")
        s_dve = sem("m_dve_steps")
        s_ve = sem("m_veps_ready")
        s_rs = sem("m_rstd_ready")
        s_xn = sem("m_xn_ready")
        s_xd = sem("m_rows_stored")
        s_r = sem("m_xn_transposed")
        s_x = sem("m_xT_ready")
        s_l = sem("m_logits_done")
        s_sc = sem("m_scores_ready")
        s_w8 = sem("m_scores_used")
        s_m = sem("m_mask_ready")
        s_p = sem("m_ranks_done")
        s_ix = sem("m_slots_ready")
        s_v8 = sem("m_taken_ready")
        s_f = sem("m_taken_counted")
        s_kw = sem("m_waits_ready")
        s_kc = sem("m_kcount_ready")
        s_sl = sem("m_list_written")
        s_a = sem("m_shared_done")
        s_sg = sem("m_sigmoid_ready")
        s_hd = sem("m_hidden_ready")
        s_d = sem("m_down_done")
        s_h = sem("m_h_added")

        block = ctx.enter_context(nc.Block())

        def chunks(eng, body):
            body(0, True, False)
            with eng.Fori(1, NC - 1) as l:
                body(l, False, False)
            body(NC - 1, False, True)

        @block.sync
        def _(sp):
            sp.dma_start(gate[:, :, :], a["gate"].rearrange("(k p) n -> p k n", p=P)).then_inc(s_w, 16)
            sp.dma_start(sgate[:, :, :], a["sgate"].rearrange("(k p) n -> p k n", p=P)).then_inc(s_w, 16)
            sp.dma_start(sup[:, :, :], a["sup"].rearrange("(k p) n -> p k n", p=P)).then_inc(s_w, 16)
            sp.dma_start(sdown[:, :, :], a["sdown"].rearrange("(k p) n -> p k n", p=P)).then_inc(s_w, 16)
            sp.dma_start(ebias[:, :], a["ebias"].rearrange("(o n) -> o n", o=1).to_broadcast([P, NEXP])).then_inc(s_w, 16)
            sp.wait_ge(s_z, 1)
            sp.dma_start(g["slots"].rearrange("(s p) o -> s (p o)", p=P), zeros[:, :]).then_inc(s_zd, 16)
            sp.sem_inc(s_xd, 16)
            with sp.Fori(0, NC) as l:
                sp.wait_ge(s_xn, l + 1)
                sp.dma_start(g["xrows"][bass.ds(l * CH, CH), :].rearrange("(j p) d -> p j d", p=P), xn[:, :, :]).then_inc(s_xd, 16)
            sp.wait_ge(s_xd, 16 * NC + 16)
            sp.wait_ge(s_zd, 16)

        @block.gpsimd
        def _(pool):
            pool.memset(zeros[:, :], 0.0).then_inc(s_z, 1)
            pool.memset(mhalf[:, :], -0.5).then_inc(s_c, 1)
            pool.memset(ones_b[:, :], 1.0).then_inc(s_c, 1)
            pool.memset(before[:, :], 1.0).then_inc(s_c, 1)
            pool.memset(lower[:, :, :], 1.0).then_inc(s_c, 1)
            pool.wait_ge(s_c, 4)
            pool.affine_select(out=before[:, :], in_=before[:, :], compare_op=ALU.is_gt, fill=0.0, base=0,
                               pattern=[[1, P]], channel_multiplier=-1).then_inc(s_c, 1)
            pool.affine_select(out=lower[:, :, :], in_=lower[:, :, :], compare_op=ALU.is_gt, fill=0.0, base=0,
                               pattern=[[1, NG], [-1, NG]], channel_multiplier=0).then_inc(s_c, 1)
            pool.iota(first_i[:, :], [[CAP, NEXP]], base=1, channel_multiplier=0).then_inc(s_c, 1)
            pool.iota(tok_i[:, :], [[P, NT]], base=0, channel_multiplier=1).then_inc(s_c, 1)
            pool.wait_ge(s_zd, 16)
            pool.wait_ge(s_cc, 2)
            pool.wait_ge(s_ve, 1)
            pool.tensor_tensor(rstd[:, :], veps[:, :], mhalf[:, :], ALU.pow).then_inc(s_rs, 1)
            for t in range(NT):
                if t % TPC == 0:
                    pool.wait_ge(s_ix, t // TPC + 1)
                    pool.wait_ge(s_kc, t // TPC + 1)

                def scatter(q):
                    for k in range(q * KSTEP, (q + 1) * KSTEP):
                        pool.indirect_dma_start(
                            g["slots"][:, :], bass.IndirectOffsetOnAxis(ap=idx[:, t, k:k + 1].bitcast(U32), axis=0),
                            tok[:, t:t + 1], None, bounds_check=SLOTS - 1, oob_is_err=False).then_inc(s_sl, 16)

                taken = pool.value_load(g["ksteps"][0:1, t:t + 1], min_val=1, max_val=KSTEPS)
                scatter(0)
                for q in range(1, KSTEPS):
                    with pool.If(taken > q):
                        scatter(q)
                        pool.nop()
            pool.wait_ge(s_kw, 1)
            total = pool.value_load(g["kwait"][0:1, NT:NT + 1], min_val=NT * 16 * KSTEP, max_val=NT * 16 * TOPK)
            pool.wait_ge(s_sl, total)

        @block.tensor
        def _(pe):
            pe.wait_ge(s_c, 8)
            pe.wait_ge(s_w, 80)

            def logits(l, opening):
                pe.wait_ge(s_xn, l + 1)
                if not opening:
                    pe.wait_ge(s_h, l - 1 + 1)
                to_columns(pe, pR, xn, ident).then_inc(s_r, 1)
                pe.wait_ge(s_x, l + 1)
                for j in range(TPC):
                    for k in range(KD):
                        last = pe.matmul(pG[:, j, :], xT[:, k, j * P:(j + 1) * P], gate[:, k, :], start=(k == 0), stop=(k == KD - 1))
                last.then_inc(s_l, 1)

            def body(l, opening, last_chunk):
                if not opening:
                    pe.wait_ge(s_hd, l)
                for f in range(KS):
                    for i, wt in enumerate((sgate, sup)):
                        for k in range(KD):
                            last = pe.matmul(pA[2 * f + i][:, :], wt[:, k, f * P:(f + 1) * P], xT[:, k, :],
                                             start=(k == 0), stop=(k == KD - 1))
                    last.then_inc(s_a, 1)
                pe.wait_ge(s_m, l + 1)
                for j in range(TPC):
                    pe.matmul(pP[:, j, :], before[:, :], Mb[:, j, :], start=True, stop=False)
                    for i in range(j):
                        pe.matmul(pP[:, j, :], ones_b[:, :], Mb[:, i, :], start=False, stop=False)
                    last = pe.matmul(pP[:, j, :], ones_b[:, :], cum[1], start=False, stop=True)
                last.then_inc(s_p, 1)
                if not last_chunk:
                    logits(l + 1, False)
                pe.wait_ge(s_v8, l + 1)
                if not last_chunk:
                    pe.wait_ge(s_sc, l + 2)
                pe.matmul(pF, ones_b[:, :], v8b[:, :], start=True, stop=True).then_inc(s_f, 1)
                pe.wait_ge(s_hd, l + 1)
                for j in range(TPC):
                    for f in range(KS):
                        last = pe.matmul(pR[j // 2][:, j % 2 * D:(j % 2 + 1) * D], hid[:, f, j * P:(j + 1) * P], sdown[:, f, :],
                                         start=(f == 0), stop=(f == KS - 1))
                last.then_inc(s_d, 1)

            logits(0, True)
            chunks(pe, body)

        @block.scalar
        def _(act):
            def scores(l, opening):
                act.wait_ge(s_r, l + 1)
                for k in range(KD):
                    last = act.activation(xT[:, k, :], pR[k][:, :], ACT.Copy)
                last.then_inc(s_x, 1)
                act.wait_ge(s_l, l + 1)
                if not opening:
                    act.wait_ge(s_w8, l)
                act.activation(score[:, :, :], pG[:, :, :], ACT.Sigmoid).then_inc(s_sc, 1)

            def body(l, opening, last_chunk):
                for f in range(KS):
                    act.wait_ge(s_a, KS * l + f + 1)
                    act.activation(sg[:, f, :], pA[2 * f][:, :], ACT.Sigmoid).then_inc(s_sg, 1)
                if not last_chunk:
                    scores(l + 1, False)

            scores(0, True)
            chunks(act, body)

        @block.vector
        def _(dve):
            dve.wait_ge(s_c, 8)
            dve.tensor_copy(first[:, :], first_i[:, :]).then_inc(s_cc, 1)
            dve.tensor_copy(tok[:, :], tok_i[:, :]).then_inc(s_cc, 1)
            dve.memset(cum[0][:, :], 0.0).then_inc(s_cc, 1)
            dve.memset(g["taken"][:, :], 0.0).then_inc(s_cc, 1)
            dve.wait_ge(s_cc, 4)
            dve.wait_ge(s_w, 80)
            dve.sem_inc(s_h, 1)
            PRE = 1
            chain = Chain(dve, s_dve)
            for t in range(NT):
                last = dve.bn_aggr(mv[:, t, :], g["stats"][:, t, :])
            chain.link(last)
            dve.tensor_scalar(veps[:, :], mv[:, :, 1], 1e-5, None, ALU.add).then_inc(s_ve, 1)
            dve.wait_ge(s_rs, 1)
            XLINKS, LINKS = 1, 25

            def rows_normalised(l, chain):
                dve.tensor_copy(mvc[:, :, :], mv[:, bass.ds(l * TPC, TPC), :])
                chain.link(dve.tensor_copy(rstdc[:, :], rstd[:, bass.ds(l * TPC, TPC)]))
                dve.wait_ge(s_xd, 16 * l + 16)
                for j in range(TPC):
                    last = dve.tensor_scalar(xn[:, j:j + 1, :], h[:, bass.ds(l * TPC + j, 1), :], mvc[:, j, 0:1], rstdc[:, j:j + 1],
                                             ALU.subtract, ALU.mult)
                last.then_inc(s_xn, 1)

            def shared_added(l):
                dve.wait_ge(s_d, l + 1)
                for i in range(2):
                    rows = h[:, bass.ds(l * TPC + 2 * i, 2), :]
                    last = dve.tensor_tensor(rows, rows, pR[i][:, :].rearrange("p (a b) -> p a b", a=2), ALU.add)
                last.then_inc(s_h, 1)

            def body(l, opening, last_chunk):
                chain = Chain(dve, s_dve, PRE + XLINKS + (XLINKS + LINKS) * l)
                link = chain.link
                dve.wait_ge(s_sc, l + 1)
                link(dve.tensor_tensor(sfc[:, :, :], score[:, :, :],
                                       ebias[:, :].unsqueeze(1).to_broadcast([P, TPC, NEXP]), ALU.add))
                by_group = sfc[:, :, :].rearrange("p t (g e) -> p (t g) e", g=NG)
                dve.memset(g["carrier"][:, :], 0.0)
                for i in range(TPC * NG):
                    last = dve.max(top2[:, i, :], by_group[:, i, :])
                link(last)
                link(dve.tensor_tensor(gs[:, :, :].rearrange("p t g -> p (t g)"), top2[:, :, 0], top2[:, :, 1], ALU.add))
                other = gs[:, :, :].unsqueeze(2).to_broadcast([P, TPC, NG, NG])
                own = gs[:, :, :].unsqueeze(3).to_broadcast([P, TPC, NG, NG])
                sq4 = "p t (g o) -> p t g o"
                dve.tensor_tensor(gt[:, :, :].rearrange(sq4, g=NG), other, own, ALU.is_gt)
                link(dve.tensor_tensor(eq[:, :, :].rearrange(sq4, g=NG), other, own, ALU.is_equal))
                low = lower[:, :, :].rearrange("p g o -> p (g o)").unsqueeze(1).to_broadcast([P, TPC, NG * NG])
                link(dve.tensor_tensor(eql[:, :, :], eq[:, :, :], low, ALU.mult))
                link(dve.tensor_tensor(gt[:, :, :], gt[:, :, :], eql[:, :, :], ALU.add))
                link(dve.tensor_reduce(rank[:, :], gt[:, :, :].rearrange("p t (g o) -> p (t g) o", o=NG), AX.X, ALU.add))
                link(dve.tensor_scalar(keep[:, :], rank[:, :], TG - 0.5, None, ALU.is_lt))
                link(dve.tensor_tensor(kept[:, :, :].rearrange("p t (g e) -> p (t g) e", g=NG), by_group,
                                       keep[:, :].unsqueeze(2).to_broadcast([P, TPC * NG, EPG]), ALU.mult))
                link(dve.tensor_scalar(cand[:, :, :], kept[:, :, :], 0.0, None, ALU.add))
                dve.memset(g["carrier"][:, :], 0.0)
                for j in range(TPC):
                    last = dve.max(v8[:, j, :], cand[:, j, :])
                link(last)
                dve.memset(g["carrier"][:, :], 0.0)
                for j in range(TPC):
                    last = dve.match_replace(rest[:, j, :], v8[:, j, :], cand[:, j, :], -3.0e38)
                link(last)
                link(dve.tensor_tensor(M[:, :, :], rest[:, :, :], cand[:, :, :], ALU.not_equal))
                dve.tensor_copy(Mb[:, :, :], M[:, :, :]).then_inc(s_m, 1)
                dve.tensor_tensor(w[:, :, :], score[:, :, :], M[:, :, :], ALU.mult).then_inc(s_w8, 1)
                if not opening:
                    shared_added(l - 1)
                if not last_chunk:
                    rows_normalised(l + 1, chain)
                dve.wait_ge(s_w8, l + 1)
                link(dve.tensor_reduce(wsum[:, :], w[:, :, :], AX.X, ALU.add))
                link(dve.tensor_scalar(wsum2[:, :], wsum[:, :], 1e-20, 1.0 / ROUTE_SCALE, ALU.add, ALU.mult))
                link(dve.reciprocal(wrec[:, :], wsum2[:, :]))
                link(dve.tensor_tensor(wfull[:, :, :], w[:, :, :], wrec[:, :].unsqueeze(2).to_broadcast([P, TPC, NEXP]), ALU.mult))
                dve.wait_ge(s_p, l + 1)
                dve.tensor_tensor(slot[:, :, :], pP[:, :, :], first[:, :].unsqueeze(1).to_broadcast([P, TPC, NEXP]), ALU.add)
                link(dve.scalar_tensor_tensor(valid[:, :, :], pP[:, :, :], float(CAP), M[:, :, :], ALU.is_lt, ALU.mult))
                dve.tensor_tensor(wv[:, :, :], wfull[:, :, :], valid[:, :, :], ALU.mult)
                dve.tensor_reduce(mch[:, :], M[:, :, :].rearrange("p t e -> p e t"), AX.X, ALU.add)
                link(dve.tensor_tensor(slot1[:, :, :], slot[:, :, :], valid[:, :, :], ALU.mult))
                dve.memset(g["carrier"][:, :], 0.0)
                for j in range(TPC):
                    last = dve.max(s8[:, j, :], slot1[:, j, :])
                link(last)
                dve.tensor_scalar(v8b[:, :], s8[:, :, :].rearrange("p t k -> p (t k)"), 0.5, None, ALU.is_gt).then_inc(s_v8, 1)
                dve.tensor_scalar(idx[:, bass.ds(l * TPC, TPC), :], s8[:, :, :], -1.0, None, ALU.add).then_inc(s_ix, 1)
                dve.tensor_tensor(cum[0][:, :], cum[0][:, :], mch[:, :], ALU.add)
                dve.wait_ge(s_f, l + 1)
                link(dve.tensor_scalar(some[:, :, :].rearrange("o t k -> o (t k)"), pF[0:1, :], 0.5, None, ALU.is_gt))
                link(dve.tensor_reduce(kcnt[:, :], some[:, :, :].rearrange("o t (q s) -> o t q s", s=KSTEP)[:, :, :, 0], AX.X, ALU.add))
                link(dve.tensor_scalar(kcnt[:, :], kcnt[:, :], 1.0, None, ALU.max))
                dve.tensor_scalar(kall[:, bass.ds(l * TPC, TPC)], kcnt[:, :], 16.0 * KSTEP, None, ALU.mult)
                dve.tensor_copy(g["ksteps"][0:1, bass.ds(l * TPC, TPC)], kcnt[:, :]).then_inc(s_kc, 1)
                dve.tensor_copy(g["s8"][:, bass.ds(l * TPC, TPC), :], s8[:, :, :])
                dve.tensor_copy(g["slot1"][:, bass.ds(l * TPC, TPC), :], slot1[:, :, :])
                dve.tensor_copy(g["wv"][:, bass.ds(l * TPC, TPC), :], wv[:, :, :])
                link(dve.tensor_copy(cum[1], cum[0][:, :]))
                for f in range(KS):
                    dve.wait_ge(s_sg, KS * l + f + 1)
                    last = dve.tensor_tensor(sgg[:, f, :], sg[:, f, :], pA[2 * f][:, :], ALU.mult)
                link(last)
                for f in range(KS):
                    last = dve.tensor_tensor(hid[:, f, :], sgg[:, f, :], pA[2 * f + 1][:, :], ALU.mult)
                last.then_inc(s_hd, 1)
                assert chain.n == LINKS + (not last_chunk) * XLINKS, chain.n

            chain = Chain(dve, s_dve, PRE)
            rows_normalised(0, chain)
            chunks(dve, body)
            shared_added(NC - 1)
            dve.wait_ge(s_h, NC + 1)
            chain = Chain(dve, s_dve, PRE + (XLINKS + LINKS) * NC)
            for t in range(RINGX, NT, RINGX):
                chain.link(dve.tensor_tensor(kall[:, t:t + RINGX], kall[:, t:t + RINGX], kall[:, t - RINGX:t], ALU.add))
            chain.link(dve.tensor_reduce(kall[:, NT:NT + 1], kall[:, NT - RINGX:NT], AX.X, ALU.add))
            dve.tensor_copy(g["kwait"][:, :], kall[:, :]).then_inc(s_kw, 1)


RINGX = 4


def expert_steps(eng, chosen, body):
    for s in range(2):
        body(s, 0)
    with eng.Fori(0, NEXP // RINGX) as l:
        with eng.If(chosen > RINGX * l):
            for s in range(2, 2 + RINGX // 2):
                body(s, l)
            with eng.If(chosen > RINGX * l + RINGX // 2):
                for s in range(2 + RINGX // 2, 2 + RINGX):
                    body(s, l)
                eng.nop()
            eng.nop()


def experts_phase(nc, ctx0, g, a):
    ctx = ExitStack()
    with ctx:
        def sb(name, shape, dt=F32):
            return ctx.enter_context(nc.sbuf_tensor(name, shape, dt))

        def pb(name, shape, dt=F32):
            return ctx.enter_context(nc.psum_tensor(name, shape, dt))

        def sem(name):
            return ctx.enter_context(nc.semaphore(name))

        ident, taken, ones_b, before = g["ident"], g["taken"], g["ones_b"], g["before"]
        WCOL = 2 * KD * HID + D
        wt = sb("x_wt", [P, RINGX, WCOL])
        lst = sb("x_lst", [P, CAP])
        lstT = sb("x_lstT", [P, SPE, P], I32)
        unit_i = sb("x_unit_i", [P, P], I32)
        unit = sb("x_unit", [P, P])
        expert_i = sb("x_expert_i", [P, P], I32)
        expert = sb("x_expert", [P, 2, P])
        spare_i = sb("x_spare_i", [1, P], I32)
        spare = sb("x_spare", [1, P])
        past = sb("x_past", [1, P])
        chosen = sb("x_chosen", [P, P])
        chosen_b = sb("x_chosen_b", [P, P], BF16)
        place = sb("x_place", [P, 1])
        sel = sb("x_sel", [P, P])
        count = sb("x_count", [1, 1])
        below = sb("x_below", [1, NEXP // RINGX, 2])
        groups = sb("x_groups", [1, 2])
        counts = sb("x_counts", [1, 4], I32)
        erow = sb("x_erow", [1, 2, P], I32)
        rows = sb("x_rows", [P, RINGX, SPE, D])
        rowsT = sb("x_rowsT", [P, RINGX, KD * CAP])
        sg = sb("x_sg", [P, RINGX, CAP])
        sgg = sb("x_sgg", [P, RINGX, CAP])
        hid = sb("x_hid", [P, RINGX, CAP])
        ye = sb("x_ye", [P, RINGX, SPE, D])
        pX = [pb(f"x_pX{i}", [P, KD * CAP]) for i in range(2)]
        pU = [pb(f"x_pU{i}", [P, 2, CAP]) for i in range(2)]
        pY = [pb(f"x_pY{i}", [P, SPE, D]) for i in range(2)]

        s_wt = [sem(f"x_weights{i}_loaded") for i in range(RINGX)]
        s_ls = sem("x_list_loaded")
        s_z = sem("x_list_zeroed")
        s_i = sem("x_numbers_made")
        s_dve = sem("x_dve_steps")
        s_c = sem("x_chosen_counted")
        s_cb = sem("x_chosen_ready")
        s_pl = sem("x_places_done")
        s_se = sem("x_sel_ready")
        s_lt = sem("x_lists_ordered")
        s_li = sem("x_list_ready")
        s_tb = sem("x_tables_ready")
        s_end = sem("x_transfers_over")
        s_rw = [sem(f"x_rows{i}_gathered") for i in range(RINGX)]
        s_t = sem("x_rows_transposed")
        s_xt = sem("x_rowsT_ready")
        s_u = sem("x_gate_up_done")
        s_sg = sem("x_sigmoid_ready")
        s_g1 = sem("x_silu_ready")
        s_hd = sem("x_hidden_ready")
        s_y = sem("x_down_done")
        s_ye = sem("x_ye_ready")
        s_yd = [sem(f"x_ye{i}_stored") for i in range(RINGX)]

        block = ctx.enter_context(nc.Block())

        def load_chosen(eng):
            eng.wait_ge(s_tb, 1)
            return eng.value_load(counts[0:1, 0:1], min_val=1, max_val=NEXP)

        @block.sync
        def _(sp):
            sp.wait_ge(s_z, 1)
            sp.dma_start(lst[0:NEXP, :], g["slots"].rearrange("(e s) o -> e (s o)", s=CAP)).then_inc(s_ls, 16)
            chosen = load_chosen(sp)

            def load(i, u, used=None):
                e = sp.value_load(erow[0:1, 0, u], min_val=0, max_val=NEXP - 1)
                if used is not None:
                    sp.wait_ge(s_y, used)
                sp.dma_start(wt[:, i, :], a["wexp"][bass.ds(e, 1), :, :].rearrange("e p n -> p (e n)")).then_inc(s_wt[i], 16)

            for i in range(RINGX):
                load(i, slice(i, i + 1))
            with sp.Fori(0, NEXP // RINGX) as l:
                with sp.If(chosen > RINGX * l + RINGX // 2):
                    for i in range(RINGX // 2):
                        load(i, bass.ds(RINGX * (l + 1) + i, 1), RINGX * l + i + 1)
                    with sp.If(chosen > RINGX * (l + 1)):
                        for i in range(RINGX // 2, RINGX):
                            load(i, bass.ds(RINGX * (l + 1) + i, 1), RINGX * l + i + 1)
                        sp.nop()
                    sp.nop()
            loaded = [sp.value_load(counts[0:1, 2 + half:3 + half], min_val=32, max_val=16 * (NEXP // RINGX + 1))
                      for half in range(2)]
            for i in range(RINGX):
                sp.wait_ge(s_wt[i], loaded[i // (RINGX // 2)])
            sp.sem_inc(s_end, 1)

        @block.gpsimd
        def _(pool):
            pool.memset(lst[:, :], 0.0).then_inc(s_z, 1)
            pool.iota(unit_i[:, :], [[1, P]], base=0, channel_multiplier=0).then_inc(s_i, 1)
            pool.iota(spare_i[:, :], [[0, P // RINGX], [1, RINGX]], base=0, channel_multiplier=0).then_inc(s_i, 1)
            pool.iota(expert_i[:, :], [[0, P]], base=0, channel_multiplier=1).then_inc(s_i, 1)
            pool.wait_ge(s_li, 1)
            chosen = load_chosen(pool)

            def gather(u):
                if u >= RINGX:
                    pool.wait_ge(s_t, u - RINGX + 1)
                for i in range(SPE):
                    pool.indirect_dma_start(
                        rows[:, u % RINGX, i, :], None, g["xrows"][:, :],
                        bass.IndirectOffsetOnAxis(ap=lstT[:, i, u:u + 1].bitcast(U32), axis=0),
                        bounds_check=T - 1, oob_is_err=False).then_inc(s_rw[u % RINGX], 16)

            for u in range(2):
                gather(u)
            for l in range(NEXP // RINGX):
                with pool.If(chosen > RINGX * l):
                    for u in range(RINGX * l + 2, RINGX * l + 2 + RINGX // 2):
                        gather(u)
                    with pool.If(chosen > RINGX * l + RINGX // 2):
                        for u in range(RINGX * l + 2 + RINGX // 2, RINGX * l + 2 + RINGX):
                            gather(u)
                        pool.nop()
                    pool.nop()

        @block.tensor
        def _(pe):
            pe.matmul(pX[0][:, 0:P], taken[:, :], ones_b[:, :], start=True, stop=True).then_inc(s_c, 1)
            pe.wait_ge(s_cb, 1)
            pe.matmul(pX[1][:, 0:P], before[:, :], chosen_b[:, :], start=True, stop=True)
            pe.matmul(pX[1][:, P:2 * P], ones_b[:, :], chosen_b[:, :], start=True, stop=True).then_inc(s_pl, 1)
            pe.wait_ge(s_se, 1)
            pe.wait_ge(s_ls, 16)
            for i in range(SPE):
                pe.matmul(pU[0][:, 0, i * P:(i + 1) * P], lst[:, i * P:(i + 1) * P], sel[:, :], start=True, stop=True)
            for i in range(2):
                last = pe.matmul(pU[0][:, 1, i * P:(i + 1) * P], expert[:, i, :], sel[:, :], start=True, stop=True)
            last.then_inc(s_lt, 1)
            pe.wait_ge(s_li, 1)
            chosen = load_chosen(pe)

            def body(s, l):
                i0 = RINGX * l
                pe.wait_ge(s_rw[s % RINGX], 16 * SPE * (l + s // RINGX + 1))
                for i in range(SPE):
                    for k in range(KD):
                        last = pe.transpose(pX[s % 2][:, k * CAP + i * P:k * CAP + (i + 1) * P],
                                            rows[:, s % RINGX, i, k * P:(k + 1) * P], ident[:, :])
                last.then_inc(s_t, 1)
                if 1 <= s:
                    e = s - 1
                    pe.wait_ge(s_wt[e % RINGX], 16 * (l + e // RINGX + 1))
                    pe.wait_ge(s_xt, i0 + e + 1)
                    for u in range(2):
                        for k in range(KD):
                            o = (u * KD + k) * HID
                            last = pe.matmul(pU[e % 2][:, u, :], wt[:, e % RINGX, o:o + HID],
                                             rowsT[:, e % RINGX, k * CAP:(k + 1) * CAP], start=(k == 0), stop=(k == KD - 1))
                    last.then_inc(s_u, 1)
                if 2 <= s:
                    e = s - 2
                    pe.wait_ge(s_hd, i0 + e + 1)
                    pe.wait_ge(s_ye, i0 + e + 1)
                    for i in range(SPE):
                        last = pe.matmul(pY[e % 2][:, i, :], hid[:, e % RINGX, i * P:(i + 1) * P],
                                         wt[:, e % RINGX, 2 * KD * HID:], start=True, stop=True)
                    last.then_inc(s_y, 1)

            expert_steps(pe, chosen, body)

        @block.scalar
        def _(act):
            def body(s, l):
                i0 = RINGX * l
                act.wait_ge(s_t, i0 + s + 1)
                act.activation(rowsT[:, s % RINGX, :], pX[s % 2][:, :], ACT.Copy).then_inc(s_xt, 1)
                if 1 <= s:
                    e = s - 1
                    act.wait_ge(s_u, i0 + e + 1)
                    act.activation(sg[:, e % RINGX, :], pU[e % 2][:, 0, :], ACT.Sigmoid).then_inc(s_sg, 1)
                if 2 <= s:
                    e = s - 2
                    home = act.value_load(erow[0:1, 1, bass.ds(i0 + e, 1)], min_val=0, max_val=NEXP + RINGX - 1)
                    act.wait_ge(s_y, i0 + e + 1)
                    act.wait_ge(s_yd[e % RINGX], 16 * (l + e // RINGX + 1))
                    act.activation(ye[:, e % RINGX, :, :], pY[e % 2][:, :, :], ACT.Copy).then_inc(s_ye, 1)
                    act.wait_ge(s_ye, i0 + e + 3)
                    act.dma_start(g["yrows"][bass.ds(home * CAP, CAP), :].rearrange("(i p) d -> p i d", p=P),
                                  ye[:, e % RINGX, :, :]).then_inc(s_yd[e % RINGX], 16)

            for i in range(RINGX):
                act.sem_inc(s_yd[i], 16)
            for i in range(2):
                act.sem_inc(s_ye, 1)
            chosen = load_chosen(act)
            expert_steps(act, chosen, body)
            stored = [act.value_load(counts[0:1, 1 + half:2 + half], min_val=32, max_val=16 * (NEXP // RINGX + 1))
                      for half in range(2)]
            for i in range(RINGX):
                act.wait_ge(s_yd[i], stored[i // (RINGX // 2)])
            act.sem_inc(s_end, 1)

        @block.vector
        def _(dve):
            link = Chain(dve, s_dve).link
            dve.wait_ge(s_i, 3)
            dve.tensor_copy(spare[:, :], spare_i[:, :])
            dve.tensor_copy(unit[:, :], unit_i[:, :])
            for i in range(2):
                dve.tensor_scalar(expert[:, i, :], expert_i[:, :], float(-NEXP * i), None, ALU.add)
            dve.wait_ge(s_c, 1)
            dve.tensor_scalar(chosen_b[:, :], pX[0][:, 0:P], 0.5, None, ALU.is_gt).then_inc(s_cb, 1)
            dve.tensor_scalar(chosen[:, :], pX[0][:, 0:P], 0.5, None, ALU.is_gt)
            dve.wait_ge(s_pl, 1)
            dve.tensor_copy(count[:, :], pX[1][0:1, P:P + 1])
            link(dve.tensor_copy(place[:, :], pX[1][:, 0:1]))
            dve.scalar_tensor_tensor(sel[:, :], unit[:, :], place[:, :], chosen[:, :], ALU.is_equal, ALU.mult).then_inc(s_se, 1)
            link(dve.tensor_scalar(below[:, :, :].rearrange("o g h -> o (g h)"), unit[0:1, 0:NEXP:RINGX // 2], count[:, :], None,
                                   ALU.is_lt))
            link(dve.tensor_reduce(groups[:, :], below[:, :, :].rearrange("o g h -> o h g"), AX.X, ALU.add))
            dve.tensor_copy(counts[:, 0:1], count[:, :])
            dve.tensor_scalar(counts[:, 1:3], groups[:, :], 1.0, 16.0, ALU.add, ALU.mult)
            dve.tensor_scalar(counts[:, 3:4], groups[:, 0:1], 16.0, None, ALU.mult)
            dve.wait_ge(s_lt, 1)
            dve.tensor_copy(lstT[:, :, :], pU[0][:, 0, :].rearrange("p (i u) -> p i u", i=SPE)).then_inc(s_li, 1)
            dve.tensor_copy(erow[:, 0, :], pU[0][0:1, 1, 0:P])
            link(dve.scalar_tensor_tensor(past[:, :], pU[0][0:1, 1, P:2 * P], 0.0, spare[:, :], ALU.is_equal, ALU.mult))
            link(dve.scalar_tensor_tensor(erow[:, 1, :], pU[0][0:1, 1, P:2 * P], float(NEXP), past[:, :], ALU.add, ALU.add))
            dve.sem_inc(s_tb, 1)
            n_chosen = load_chosen(dve)

            def body(s, l):
                if 1 <= s:
                    e = s - 1
                    n = RINGX * l + e + 1
                    dve.wait_ge(s_sg, n)
                    dve.tensor_tensor(sgg[:, e % RINGX, :], sg[:, e % RINGX, :], pU[e % 2][:, 0, :], ALU.mult).then_inc(s_g1, 1)
                    dve.wait_ge(s_g1, n)
                    dve.tensor_tensor(hid[:, e % RINGX, :], sgg[:, e % RINGX, :], pU[e % 2][:, 1, :], ALU.mult).then_inc(s_hd, 1)

            expert_steps(dve, n_chosen, body)


def combine_phase(nc, ctx0, g, a, out):
    ctx = ExitStack()
    with ctx:
        def sem(name):
            return ctx.enter_context(nc.semaphore(name))

        h, idx, s8, slot1, wv = (g[n] for n in ("h", "idx", "s8", "slot1", "wv"))
        wk = ctx.enter_context(nc.sbuf_tensor("c_wk", [P, NT, TOPK], F32))
        match = ctx.enter_context(nc.sbuf_tensor("c_match", [P, NT * TOPK, NEXP], F32))
        yg = ctx.enter_context(nc.sbuf_tensor("c_yg", [P, RINGX, TOPK, D], F32))
        total = ctx.enter_context(nc.sbuf_tensor("c_total", [P, 2, D], F32))
        s_z = sem("c_zeroed")
        s_g = [sem(f"c_rows{i}_gathered") for i in range(RINGX)]
        s_wk = sem("c_weights_ready")
        s_sc = sem("c_rows_scaled")
        s_t = sem("c_rows_summed")
        s_a = sem("c_rows_added")
        s_o = sem("c_out_stored")
        block = ctx.enter_context(nc.Block())

        @block.gpsimd
        def _(pool):
            for t in range(NT):
                if t < RINGX:
                    pool.wait_ge(s_z, t + 1)
                if t >= RINGX:
                    pool.wait_ge(s_a, t - RINGX + 1)

                def gather(q):
                    for k in range(q * KSTEP, (q + 1) * KSTEP):
                        pool.indirect_dma_start(
                            yg[:, t % RINGX, k, :], None, g["yrows"][0:SLOTS, :],
                            bass.IndirectOffsetOnAxis(ap=idx[:, t, k:k + 1].bitcast(U32), axis=0),
                            bounds_check=SLOTS - 1, oob_is_err=False).then_inc(s_g[t % RINGX], 16)

                taken = pool.value_load(g["ksteps"][0:1, t:t + 1], min_val=1, max_val=KSTEPS)
                gather(0)
                for q in range(1, KSTEPS):
                    with pool.If(taken > q):
                        gather(q)
                        pool.nop()

        @block.vector
        def _(dve):
            for i in range(RINGX):
                dve.memset(yg[:, i, :, :], 0.0).then_inc(s_z, 1)

            def weights(t):
                for k in range(TOPK):
                    last = dve.scalar_tensor_tensor(match[:, t * TOPK + k, :], slot1[:, t, :], s8[:, t, k:k + 1], wv[:, t, :],
                                                    ALU.is_equal, ALU.mult, accum_out=wk[:, t, k:k + 1])
                last.then_inc(s_wk, 1)

            weights(0)
            weights(1)
            for t in range(NT):
                dve.wait_ge(s_sc, t + 1)
                dve.tensor_reduce(total[:, t % 2, :], yg[:, t % RINGX, :, :].rearrange("p k d -> p d k"), AX.X, ALU.add).then_inc(s_t, 1)
                dve.wait_ge(s_t, t + 1)
                dve.tensor_tensor(h[:, t, :], h[:, t, :], total[:, t % 2, :], ALU.add).then_inc(s_a, 1)
                if t + 2 < NT:
                    weights(t + 2)

        @block.scalar
        def _(act):
            for t in range(NT):
                gathered = act.value_load(g["kwait"][0:1, t:t + 1], min_val=16 * KSTEP, max_val=NT // RINGX * 16 * TOPK)
                act.wait_ge(s_g[t % RINGX], gathered)
                act.wait_ge(s_wk, t + 1)
                for k in range(TOPK):
                    last = act.activation(yg[:, t % RINGX, k, :], yg[:, t % RINGX, k, :], ACT.Copy, scale=wk[:, t, k:k + 1])
                last.then_inc(s_sc, 1)

        @block.sync
        def _(sp):
            for t in range(NT):
                sp.wait_ge(s_a, t + 1)
                sp.dma_start(out[t * P:(t + 1) * P, :], h[:, t, :]).then_inc(s_o, 16)
            sp.wait_ge(s_o, 16 * NT)


def second_layer_tensors(nc, ctx, g):
    g["ident_b"] = ctx.enter_context(nc.sbuf_tensor("ident_b", [P, P], BF16))
    g["qn"] = ctx.enter_context(nc.sbuf_tensor("qn", [P, NT, HEADS, DH], F32))
    g["sel"] = ctx.enter_context(nc.sbuf_tensor("sel", [P, HEADS, P], BF16))
    g["idx"] = ctx.enter_context(nc.sbuf_tensor("idx", [P, NT, TOPK], I32))
    g["s8"] = ctx.enter_context(nc.sbuf_tensor("s8", [P, NT, TOPK], F32))
    g["stats"] = ctx.enter_context(nc.sbuf_tensor("stats", [P, NT, 6], F32))
    g["slot1"] = ctx.enter_context(nc.sbuf_tensor("slot1", [P, NT, NEXP], F32))
    g["wv"] = ctx.enter_context(nc.sbuf_tensor("wv", [P, NT, NEXP], F32))
    g["ksteps"] = ctx.enter_context(nc.sbuf_tensor("ksteps", [1, NT], I32))
    g["kwait"] = ctx.enter_context(nc.sbuf_tensor("kwait", [1, NT + 1], I32))
    g["taken"] = ctx.enter_context(nc.sbuf_tensor("taken", [P, P], BF16))
    g["ones_b"] = ctx.enter_context(nc.sbuf_tensor("ones_b", [P, P], BF16))
    g["before"] = ctx.enter_context(nc.sbuf_tensor("before", [P, P], BF16))


def build(nc, a, out):
    ctx = ExitStack()
    with ctx:
        g = {}
        g["ident"] = ctx.enter_context(nc.sbuf_tensor("ident", [P, P], F32))
        g["ones"] = ctx.enter_context(nc.sbuf_tensor("ones", [P, P], F32))
        g["h"] = ctx.enter_context(nc.sbuf_tensor("h", [P, NT, D], F32))
        g["XT"] = ctx.enter_context(nc.sbuf_tensor("XT", [P, KD, T], F32))
        g["prob"] = ctx.enter_context(nc.sbuf_tensor("prob", [P, NT, EXPERTS0], F32))
        g["routed"] = ctx.enter_context(nc.sbuf_tensor("routed", [P, 1], I32))
        g["qparts"] = nc.dram_tensor("qparts", (SPLIT, D, T), BF16, kind="Internal").ap()
        g["xrows"] = nc.dram_tensor("xrows", (T, D), F32, kind="Internal").ap()
        g["slots"] = nc.dram_tensor("slots", (SLOTS, 1), F32, kind="Internal").ap()
        g["yrows"] = nc.dram_tensor("yrows", (SLOTS + RINGX * CAP, D), F32, kind="Internal").ap()
        g["carrier"] = ctx.enter_context(nc.sbuf_tensor("carrier", [P, 1], F32))
        g["junk"] = ctx.enter_context(nc.sbuf_tensor("junk", [P, 4, SEQ], F32))
        embed_phase(nc, ctx, g, a)
        blocks_phase(nc, ctx, g, a)
        second_layer_tensors(nc, ctx, g)
        shared0_phase(nc, ctx, g, a)
        routed0_phase(nc, ctx, g, a)
        queries_phase(nc, ctx, g, a)
        attention_phase(nc, ctx, g, a)
        router_phase(nc, ctx, g, a)
        experts_phase(nc, ctx, g, a)
        combine_phase(nc, ctx, g, a, out)



def kernel(**inputs):
    import concourse.bacc as bacc
    from concourse.bass_utils import run_bass_kernel_spmd

    i = {k: np.asarray(v) for k, v in inputs.items()}
    A = "L0_attn_"

    def cols(v):
        return v.reshape(BLOCKS, -1, P).transpose(0, 2, 1)

    w1, w3 = (i["L1_ffn_" + n].transpose(0, 2, 1).reshape(NEXP, KD, P, HID).transpose(0, 2, 1, 3).reshape(NEXP, P, KD * HID)
              for n in ("w1", "w3"))
    experts = np.concatenate([w1, w3, i["L1_ffn_w2"].transpose(0, 2, 1)], 2)

    arrays = {
        "x": i["x"].reshape(T),
        "head_rows": i["L0_tok_head_weight"].T[:CUTS[1]],
        "tail0_rows": i["L0_tok_tail_weight_0"].T,
        "tail1_rows": i["L0_tok_tail_weight_1"].T,
        "head_proj": i["L0_tok_head_weight_proj"].T,
        "tail0_proj": i["L0_tok_tail_weight_proj_0"].T,
        "tail1_proj": i["L0_tok_tail_weight_proj_1"].T,
        "wqkv": np.stack([i[A + "Wq"], i[A + "Wk"], i[A + "Wv"]], 1),
        "wo": i[A + "Wo"], "w1": i[A + "W1"], "w2": i[A + "W2"],
        "ws1": i["L0_ffn_Ws1"], "ws2": i["L0_ffn_Ws2"], "wr": i["L0_ffn_Wr"],
        "w1r": i["L0_ffn_W1"], "w2r": i["L0_ffn_W2"],
        "gate": i["L1_ffn_gate_weight"].T, "ebias": i["L1_ffn_e_bias"],
        "sgate": i["L1_ffn_shared_gate"].T, "sup": i["L1_ffn_shared_up"].T, "sdown": i["L1_ffn_shared_down"].T,
        "wexp": experts,
        "wq1": i["L1_attn_Wq"].transpose(0, 2, 1), "wp": i["L1_attn_Wp"].T, "bp": i["L1_attn_bp"],
        "vec": np.concatenate([cols(i[A + n]) for n in VEC], 2).transpose(1, 0, 2).reshape(P, BLOCKS * NVEC),
    }
    nc = bacc.Bacc("TRN2", target_bir_lowering=False, num_devices=1)
    arrays = {"in_" + k: np.ascontiguousarray(v) for k, v in arrays.items()}
    aps = {k[3:]: nc.dram_tensor(k, v.shape, mybir.dt.from_np(v.dtype), kind="ExternalInput").ap()
           for k, v in arrays.items()}
    out = nc.dram_tensor("out", (T, D), F32, kind="ExternalOutput").ap()
    build(nc, aps, out)
    r = run_bass_kernel_spmd(nc, [arrays], core_ids=[0])
    return r.results[0]["out"].reshape(8, 256, 256)
```
